# Optimizing a Trainium2 kernel written in Bass

```python
import numpy as np
import jax
import jax.numpy as jnp

def _softmax(x, axis=-1):
    return jax.nn.softmax(x, axis=axis)

def _gelu(x):
    return jax.nn.gelu(x, approximate=True)

def _silu(x):
    return jax.nn.silu(x)

def _sigmoid(x):
    return jax.nn.sigmoid(x)

def _layernorm(x, axis=-1, eps=1e-05):
    m = jnp.mean(x, axis=axis, keepdims=True)
    v = jnp.var(x, axis=axis, keepdims=True)
    return (x - m) / jnp.sqrt(v + eps)

def _scatter_add(tgt, idx, src, axis=0):
    return tgt.at[idx].add(src)

def _segment_sum(src, seg, n):
    return jax.ops.segment_sum(src, seg, n)
kernel_name = 'mk_gnn_preln_d2_gnn_r16_19786e'

def setup_inputs(seed: int=0):
    np.random.seed(seed)
    _w = jnp.asarray

    def _rec_inputs():
        import jax
        import jax.numpy as jnp
        _gk = jax.random.key(seed)
        x = -0.0001978 + 0.9998 * jax.random.normal(jax.random.fold_in(_gk, 1), (6250, 128), jnp.float32)
        _s = jax.random.randint(jax.random.fold_in(_gk, 2), (100000,), 0, 6250, jnp.int32)
        _d = jax.random.randint(jax.random.fold_in(_gk, 3), (100000,), 0, 6250, jnp.int32)
        _loop = jnp.arange(6250, dtype=jnp.int32)
        src = jnp.concatenate([_s, _d, _loop])
        dst = jnp.concatenate([_d, _s, _loop])
        _o = jnp.argsort(dst, stable=True)
        src = src[_o]
        dst = dst[_o]
        return (x, src, dst)
    x, src, dst = _rec_inputs()

    def _L0_gnn_setup():
        import jax, jax.numpy as jnp
        import numpy as np
        N_NODES = 3125
        N_EDGES = 50000
        D_MODEL = 128
        N_HEAD = 8
        key = jax.random.key(seed)
        k_e, k_x, k_q, k_k, k_v = jax.random.split(key, 5)
        bound = float(np.sqrt(6.0 / (D_MODEL + D_MODEL)))
        return {'edge_index': jax.random.randint(k_e, (2, N_EDGES), 0, N_NODES, dtype=jnp.int64), 'embeds': jax.random.normal(k_x, (N_NODES, D_MODEL), dtype=jnp.float32), 'Wq': jax.random.uniform(k_q, (D_MODEL, D_MODEL), jnp.float32, -bound, bound), 'Wk': jax.random.uniform(k_k, (D_MODEL, D_MODEL), jnp.float32, -bound, bound), 'Wv': jax.random.uniform(k_v, (D_MODEL, D_MODEL), jnp.float32, -bound, bound), 'gamma': jnp.ones((D_MODEL,), jnp.float32), 'beta': jnp.zeros((D_MODEL,), jnp.float32), 'n_head': N_HEAD}
    _L0_gnn_all = _L0_gnn_setup()
    _L0_gnn_in = {k: v for k, v in _L0_gnn_all.items() if k in ('Wq', 'Wk', 'Wv', 'gamma', 'beta')}
    del _L0_gnn_all

    def _L1_gnn_setup():
        import jax, jax.numpy as jnp
        import numpy as np
        N_NODES = 2500
        N_EDGES = 40000
        D_FEAT = 128
        key = jax.random.key(seed)
        k1, k2, k3, k4 = jax.random.split(key, 4)
        x = jax.random.normal(k1, (N_NODES, D_FEAT), dtype=jnp.float32)
        beta = jax.random.uniform(k2, (1,), dtype=jnp.float32)
        row = jax.random.randint(k3, (N_EDGES,), 0, N_NODES)
        col = (row + 1 + jax.random.randint(k4, (N_EDGES,), 0, N_NODES - 1)) % N_NODES
        edge_index = jnp.stack([row, col]).astype(jnp.int64)
        return {'x': x, 'beta': beta, 'edge_index': edge_index}
    _L1_gnn_all = _L1_gnn_setup()
    _L1_gnn_in = {k: v for k, v in _L1_gnn_all.items() if k in ('beta',)}
    del _L1_gnn_all
    return {'x': x, 'src': src, 'dst': dst, 'L0_gnn_Wq': _L0_gnn_in['Wq'], 'L0_gnn_Wk': _L0_gnn_in['Wk'], 'L0_gnn_Wv': _L0_gnn_in['Wv'], 'L0_gnn_gamma': _L0_gnn_in['gamma'], 'L0_gnn_beta': _L0_gnn_in['beta'], 'L1_gnn_beta': _L1_gnn_in['beta']}

def reference(x, src, dst, L0_gnn_Wq, L0_gnn_Wk, L0_gnn_Wv, L0_gnn_gamma, L0_gnn_beta, L1_gnn_beta):
    import jax
    import jax.numpy as jnp

    def _L0_gnn_ref(edge_index, embeds, Wq, Wk, Wv, gamma, beta, n_head):
        import jax, jax.numpy as jnp
        import numpy as np
        N_NODES = 3125
        N_EDGES = 50000
        D_MODEL = 128
        N_HEAD = 8
        rows, cols = (edge_index[0], edge_index[1])
        nvar, d_model = embeds.shape
        evar = rows.shape[0]
        hd = d_model // n_head
        rowE = embeds[rows]
        colE = embeds[cols]
        qE = (rowE @ Wq).reshape(evar, n_head, hd)
        kE = (colE @ Wk).reshape(evar, n_head, hd)
        vE = (colE @ Wv).reshape(evar, n_head, hd)
        att = jnp.einsum('ehd,ehd->eh', qE, kE)
        att = jnp.clip(att, -10.0, 10.0)
        expAtt = jnp.exp(att)
        attNorm = jax.ops.segment_sum(expAtt, rows, num_segments=nvar)[rows]
        att = expAtt / (attNorm + 1e-08)
        resE = (att[..., None] * vE).reshape(evar, d_model)
        res = jax.ops.segment_sum(resE, rows, num_segments=nvar)
        res = res + embeds
        mean = jnp.mean(res, axis=-1, keepdims=True)
        var = jnp.mean(jnp.square(res - mean), axis=-1, keepdims=True)
        res = (res - mean) * jax.lax.rsqrt(var + 1e-06) * gamma + beta
        return res

    def _L1_gnn_ref(x, beta, edge_index):
        import jax, jax.numpy as jnp
        import numpy as np
        N_NODES = 2500
        N_EDGES = 40000
        D_FEAT = 128
        num_nodes = x.shape[0]
        row, col = (edge_index[0], edge_index[1])
        loop = jnp.arange(num_nodes, dtype=row.dtype)
        row = jnp.concatenate([row, loop])
        col = jnp.concatenate([col, loop])
        norm = jnp.linalg.norm(x, axis=1)
        alpha = jnp.sum(x[row] * x[col], axis=1) / (norm[row] * norm[col])
        alpha = alpha * beta[0]
        amax = jax.ops.segment_max(alpha, row, num_segments=num_nodes)
        alpha = jnp.exp(alpha - amax[row])
        denom = jax.ops.segment_sum(alpha, row, num_segments=num_nodes)
        alpha = alpha / denom[row]
        out = jax.ops.segment_sum(alpha[:, None] * x[col], row, num_segments=num_nodes)
        return out
    edge_index = jnp.stack([src, dst])
    h = jnp.maximum(_layernorm(x, axis=-1), 0.0)
    x = x + _L0_gnn_ref(edge_index, h, L0_gnn_Wq, L0_gnn_Wk, L0_gnn_Wv, L0_gnn_gamma, L0_gnn_beta, 8)
    h = jnp.maximum(_layernorm(x, axis=-1), 0.0)
    x = x + _L1_gnn_ref(h, L1_gnn_beta, edge_index)
    return x

_drawn_inputs = setup_inputs


def setup_inputs(seed=0):
    import zlib

    import numpy as np

    out = dict(_drawn_inputs(seed))
    spreads = {'L0_gnn_gamma': (1.0, 0.2), 'L0_gnn_beta': (0.0, 0.1)}
    factors = {}
    for name, (base, spread) in spreads.items():
        noise = np.random.default_rng([zlib.crc32(name.encode()), seed]).standard_normal(out[name].shape)
        drawn = base * np.exp(spread * noise) if base else spread * noise
        out[name] = jnp.asarray(drawn.astype(out[name].dtype))
    for name, factor in factors.items():
        out[name] = (out[name] * factor).astype(out[name].dtype)
    return out
```

```python
import concourse.bass as bass
from concourse import mybir
from contextlib import ExitStack

P = 128
N = 6250
D = 128
HEADS = 8
HD = D // HEADS
E = 206250
NBLK = (N + P - 1) // P
NPAD = NBLK * P
NBUK = NBLK + 1
TAIL = N - (NBLK - 1) * P
LASTB = NBLK - 1

STEP = 10
CHUNK = 90
SPC = CHUNK // STEP
NCHUNK = 18
COLS = NCHUNK * CHUNK
NSTEP = COLS // STEP
LASTROW = E - (P - 1) * COLS
PAD_EDGES = P * COLS - E
PAD_SRC = P * NBLK

GT = 4
GE = GT * P
GROUPS = (E + NBLK * (GE - 1)) // GE + 1
NT = GT * (GROUPS + (PAD_EDGES + GE - 1) // GE)
PACK = 256
EMPTY = PACK - 1

RING = 6
RANKS = 2 * SPC
AW0 = D + HEADS
AW1 = D + 1
TW = D + 2
QKV_TILES = 4

f32 = mybir.dt.float32
bf16 = mybir.dt.bfloat16
i32 = mybir.dt.int32
ALU = mybir.AluOpType
ACT = mybir.ActivationFunctionType
AX_X = mybir.AxisListType.X
ds = bass.ds


def need(eng, semaphore, value):
    if isinstance(value, int) and value <= 0:
        return
    eng.wait_ge(semaphore, value)


class Chain:

    def __init__(self, eng, semaphore):
        self.eng, self.semaphore, self.count = eng, semaphore, 0

    def __call__(self, instruction):
        self.count += 1
        instruction.then_inc(self.semaphore, 1)
        self.eng.wait_ge(self.semaphore, self.count)


def over(ap, n):
    return ap.unsqueeze(2).broadcast_to((ap.shape[0], ap.shape[1], n))


def under(ap, n):
    return ap.unsqueeze(1).broadcast_to((ap.shape[0], n, ap.shape[1]))


def sort_and_project(nc, mem, dram, ins):
    src, dst, x, wq, wk, wv, gamma, beta, cos_beta = ins
    with ExitStack() as ctx:
        def sb(name, shape, dt=f32):
            return ctx.enter_context(nc.sbuf_tensor(name, shape, dt))

        def sem(name):
            return ctx.enter_context(nc.semaphore(name))

        iota, ident, x_sb, q_sb = mem["iota"], mem["ident"], mem["x"], mem["q"]
        h_sb = mem["h"][:, 0:NBLK * D].rearrange("p (t f) -> p t f", f=D)
        slots, loc_f, blkid, gb_sb, cb_sb = mem["slots"], mem["loc"], mem["blkid"], mem["gb"], mem["cb"]
        PS = mem["psum"]

        src_i = sb("src_i", [P, COLS], i32)
        dst_i = sb("dst_i", [P, COLS], i32)
        blk_f = sb("blk_f", [P, COLS])
        pk_i = sb("pk_i", [P, COLS], i32)
        tri = sb("tri", [P, P])
        tri_b = sb("tri_b", [P, P], bf16)
        ones_b = sb("ones_b", [P, 1], bf16)
        ones_r = sb("ones_r", [1, P])
        iota_g = sb("iota_g", [P, GROUPS])
        cnt = sb("cnt", [P, COLS])
        off = sb("off", [P, COLS])
        offc = sb("offc", [P, NCHUNK * NBUK])
        offrow = mem["acc"][0:1, 0:2 * CHUNK * NBUK].rearrange("p (r c) -> p r c", r=2)
        hot = sb("hot", [P, 3, STEP * NBUK], bf16)
        ranked = sb("ranked", [P, STEP * NBUK])
        pos_f = sb("pos_f", [P, STEP])
        pos = sb("pos", [P, STEP], i32)
        pos_p = sb("pos_p", [P, STEP], i32)
        pos_t = sb("pos_t", [P, STEP], i32)
        addr = sb("addr", [P, RANKS, STEP], i32)
        pk_ring = sb("pk_ring", [P, RANKS, STEP], i32)
        bk = sb("bk", [P, 8])
        bk_i = sb("bk_i", [P, 2], i32)
        ge = sb("ge", [P, GROUPS], bf16)
        gid = sb("gid", [1, GROUPS])
        w_sb = sb("w_sb", [P, 3 * D])
        stat = sb("stat", [P, 4, NBLK])
        hT = sb("hT", [P, QKV_TILES * P])
        kv = sb("kv", [P, QKV_TILES, 2 * D])

        cnt_ps = PS[0:NBUK, 0:COLS]
        rank_ps = [PS[:, 2048 + 512 * k:2048 + 512 * k + STEP * NBUK] for k in range(2)]
        base_ps = PS[0:NBUK, 3072:3073]
        gid_ps = PS[0:1, 3584:3584 + GROUPS]
        offT_ps = [PS[0:CHUNK, 512 * k:512 * k + 512] for k in range(2)]
        hT_ps = PS[:, 3072:3584]
        qkv_ps = [PS[:, 512 * k:512 * k + 3 * D] for k in range(QKV_TILES)]

        s_const = sem("s_const")
        s_pool = sem("s_pool")
        s_pads = sem("s_pads")
        s_src, s_dst, s_x, s_w, s_gb = (sem(n) for n in ("s_src", "s_dst", "s_x", "s_w", "s_gb"))
        s_filled = sem("s_filled")
        s_v = sem("s_v")
        s_prep = sem("s_prep")
        s_hot = sem("s_hot")
        s_hotread = sem("s_hotread")
        s_gcount = sem("s_gcount")
        s_base = sem("s_base")
        s_ge = sem("s_ge")
        s_gid = sem("s_gid")
        s_off = sem("s_off")
        s_offT = sem("s_offT")
        s_offc = sem("s_offc")
        s_offd = sem("s_offd")
        s_row = [sem("s_row0"), sem("s_row1")]
        s_rank = sem("s_rank")
        s_ranked = sem("s_ranked")
        s_pos = sem("s_pos")
        s_posi = sem("s_posi")
        s_posb = sem("s_posb")
        s_addr = sem("s_addr")
        s_scat = [sem(f"s_scat{k}") for k in range(RANKS)]
        s_go = sem("s_go")
        s_sorted = sem("s_sorted")
        s_back = sem("s_back")
        s_xc = sem("s_xc")
        s_sq = sem("s_sq")
        s_var = sem("s_var")
        s_std = sem("s_std")
        s_h = sem("s_h")
        s_hT = sem("s_hT")
        s_hTc = sem("s_hTc")
        s_qkv = sem("s_qkv")
        s_q = sem("s_q")
        s_kv = sem("s_kv")
        s_kvd = sem("s_kvd")

        block = ctx.enter_context(nc.Block())

        @block.sync
        def _(sp):
            sp.wait_ge(s_pads, 3)
            for tile, edges, done in ((src_i, src, s_src), (dst_i, dst, s_dst)):
                sp.dma_start(tile[0:P - 1, :], edges[0:(P - 1) * COLS].rearrange("(p c) -> p c", c=COLS)).then_inc(done, 16)
                sp.dma_start(tile[P - 1:P, 0:LASTROW],
                             edges[(P - 1) * COLS:E].rearrange("(p c) -> p c", p=1)).then_inc(done, 16)
            sp.wait_ge(s_pads, 4)
            sp.dma_start(dram["sorted"].rearrange("(p t) o -> p (t o)", p=P), slots[:, :]).then_inc(s_filled, 16)
            sp.dma_start(x_sb[:, 0:LASTB, :], x[0:LASTB * P, :].rearrange("(t p) f -> p t f", p=P)).then_inc(s_x, 16)
            sp.dma_start(x_sb[0:TAIL, LASTB, :], x[LASTB * P:N, :]).then_inc(s_x, 16)
            for k, w in enumerate((wq, wk, wv)):
                sp.dma_start(w_sb[:, k * D:(k + 1) * D], w).then_inc(s_w, 16)
            for k, w in enumerate((gamma, beta)):
                sp.dma_start(gb_sb[:, k, :], w.rearrange("(o f) -> o f", o=1).broadcast_to((P, D))).then_inc(s_gb, 16)
            sp.dma_start(cb_sb[:, 0:1], cos_beta.rearrange("(o f) -> o f", o=1).broadcast_to((P, 1))).then_inc(s_gb, 16)
            sp.wait_ge(s_offc, 1)
            sp.dma_start(dram["offs"].rearrange("(k c) b -> c k b", c=CHUNK),
                         offc[0:CHUNK, :].rearrange("c (k b) -> c k b", b=NBUK)).then_inc(s_offd, 16)
            sp.wait_ge(s_offd, 16)
            rows = dram["offs"].rearrange("(k c) b -> k (c b)", c=CHUNK)
            for r in range(2):
                sp.dma_start(offrow[:, r, :], rows[r:r + 1, :]).then_inc(s_row[r], 16)
            with sp.Fori(1, NCHUNK // 2) as t:
                for r in range(2):
                    sp.wait_ge(s_rank, RANKS * t - SPC * (1 - r))
                    sp.dma_start(offrow[:, r, :], rows[ds(2 * t + r, 1), :]).then_inc(s_row[r], 16)
            for b in range(0, NBLK, QKV_TILES):
                n = min(QKV_TILES, NBLK - b)
                sp.wait_ge(s_kv, b + n)
                sp.dma_start(dram["kv"][b * P:(b + n) * P, :].rearrange("(t p) f -> p t f", p=P),
                             kv[:, 0:n, :]).then_inc(s_kvd, 16)
            sp.wait_ge(s_sorted, 1)
            sp.dma_start(slots[:, :], dram["sorted"].rearrange("(p t) o -> p (t o)", p=P)).then_inc(s_back, 16)
            sp.wait_ge(s_kvd, 16 * ((NBLK + QKV_TILES - 1) // QKV_TILES))
            sp.wait_ge(s_gb, 48)
            sp.wait_ge(s_filled, 16)

        @block.gpsimd
        def _(pool):
            nc.gpsimd.iota(iota[:, :], [[1, P]], base=0, channel_multiplier=0,
                           allow_small_or_imprecise_dtypes=True).then_inc(s_const, 1)
            nc.gpsimd.iota(iota_g[:, :], [[1, GROUPS]], base=0, channel_multiplier=0,
                           allow_small_or_imprecise_dtypes=True).then_inc(s_const, 1)
            nc.gpsimd.memset(ident[:, :], 0.0).then_inc(s_pool, 1)
            nc.gpsimd.memset(tri[:, :], 1.0).then_inc(s_pool, 1)
            nc.gpsimd.memset(ones_r[:, :], 1.0).then_inc(s_const, 1)
            pool.wait_ge(s_pool, 2)
            nc.gpsimd.affine_select(out=ident[:, :], in_=ident[:, :], compare_op=ALU.not_equal, fill=1.0,
                                    base=0, pattern=[[-1, P]], channel_multiplier=1).then_inc(s_const, 1)
            nc.gpsimd.affine_select(out=tri[:, :], in_=tri[:, :], compare_op=ALU.is_gt, fill=0.0,
                                    base=0, pattern=[[1, P]], channel_multiplier=-1).then_inc(s_const, 1)
            pool.wait_ge(s_filled, 16)
            with pool.Fori(0, NSTEP // RANKS) as t:
                for k in range(RANKS):
                    pool.wait_ge(s_addr, 2 * (RANKS * t + k + 1))
                    pool.sem_inc(s_go, 1)
                    for c in range(STEP):
                        pool.indirect_dma_start(
                            out=dram["sorted"], out_offset=bass.IndirectOffsetOnAxis(ap=addr[:, k, c:c + 1], axis=0),
                            in_=pk_ring[:, k, c:c + 1], in_offset=None).then_inc(s_scat[k], 16)
            for k in range(RANKS):
                pool.wait_ge(s_scat[k], 16 * STEP * (NSTEP // RANKS))
            pool.sem_inc(s_sorted, 1)

        @block.tensor
        def _(pe):
            pe.wait_ge(s_const, 5)
            pe.wait_ge(s_prep, 2)
            with pe.Fori(0, NSTEP // 3) as t:
                for k in range(3):
                    pe.wait_ge(s_hot, 3 * t + k + 1)
                    for c in range(STEP):
                        last = nc.tensor.matmul(cnt_ps[:, ds(3 * STEP * t + STEP * k + c, 1)],
                                                hot[:, k, c * NBUK:(c + 1) * NBUK], ones_b[:, :],
                                                start=True, stop=True)
                    last.then_inc(s_hotread, 1)
            pe.wait_ge(s_gcount, 1)
            nc.tensor.matmul(base_ps, tri[0:NBUK, 0:NBUK], bk[0:NBUK, 1:2], start=True, stop=True).then_inc(s_base, 1)
            pe.wait_ge(s_ge, 1)
            nc.tensor.matmul(gid_ps, ones_b[0:NBLK, :], ge[0:NBLK, :], start=True, stop=True).then_inc(s_gid, 1)
            pe.wait_ge(s_off, 1)
            for k in range(NCHUNK):
                last = nc.tensor.transpose(offT_ps[k // SPC][:, (k % SPC) * NBUK:(k % SPC + 1) * NBUK],
                                           off[0:NBUK, k * CHUNK:(k + 1) * CHUNK], ident[0:NBUK, 0:NBUK])
            last.then_inc(s_offT, 1)

            def rank(t):
                for k in range(RANKS):
                    q = RANKS * t + k
                    pe.wait_ge(s_hot, NSTEP + q + 1)
                    need(pe, s_ranked, q - 1)
                    nc.tensor.matmul(rank_ps[k % 2], tri_b[:, :], hot[:, k % 3, :],
                                     start=True, stop=False).then_inc(s_hotread, 1)
                    if k % SPC == 0:
                        pe.wait_ge(s_row[k // SPC], 16 * t + 16)
                    m = (k % SPC) * STEP * NBUK
                    nc.tensor.matmul(rank_ps[k % 2], ones_r[:, :], offrow[:, k // SPC, m:m + STEP * NBUK],
                                     start=False, stop=True).then_inc(s_rank, 1)
            rank(0)
            with pe.Fori(1, NSTEP // RANKS) as t:
                rank(t)
            pe.wait_ge(s_w, 48)
            pe.wait_ge(s_h, 1)
            for i, b in enumerate(range(0, NBLK, QKV_TILES)):
                n = min(QKV_TILES, NBLK - b)
                need(pe, s_hTc, i)
                for k in range(n):
                    last = nc.tensor.transpose(hT_ps[:, k * P:(k + 1) * P], h_sb[:, b + k, :], ident[:, :])
                last.then_inc(s_hT, 1)
                pe.wait_ge(s_hTc, i + 1)
                for k in range(n):
                    need(pe, s_q, b + k + 1 - QKV_TILES)
                    need(pe, s_kv, b + k + 1 - QKV_TILES)
                    nc.tensor.matmul(qkv_ps[k], hT[:, k * P:(k + 1) * P], w_sb[:, :],
                                     start=True, stop=True).then_inc(s_qkv, 1)

        @block.scalar
        def _(act):
            act.wait_ge(s_xc, 1)
            nc.scalar.activation(q_sb[:, :, :], h_sb[:, :, :], ACT.Square).then_inc(s_sq, 1)
            act.wait_ge(s_var, 1)
            nc.scalar.activation(stat[:, 2, :], stat[:, 1, :], ACT.Sqrt).then_inc(s_std, 1)
            for i, b in enumerate(range(0, NBLK, QKV_TILES)):
                n = min(QKV_TILES, NBLK - b)
                act.wait_ge(s_hT, i + 1)
                need(act, s_qkv, b)
                nc.scalar.activation(hT[:, 0:n * P], hT_ps[:, 0:n * P], ACT.Copy).then_inc(s_hTc, 1)
                need(act, s_kvd, 16 * i)
                for k in range(n):
                    act.wait_ge(s_q, b + k + 1)
                    nc.scalar.activation(kv[:, k, :], qkv_ps[k][:, D:3 * D], ACT.Copy).then_inc(s_kv, 1)

        @block.vector
        def _(dve):
            nc.vector.memset(src_i[96:P, LASTROW:COLS], PAD_SRC).then_inc(s_pads, 1)
            nc.vector.memset(dst_i[96:P, LASTROW:COLS], 0).then_inc(s_pads, 1)
            nc.vector.memset(x_sb[:, LASTB, :], 0.0).then_inc(s_pads, 1)
            nc.vector.memset(slots[:, :], EMPTY).then_inc(s_pads, 1)
            nc.vector.memset(ones_b[:, :], 1.0).then_inc(s_prep, 1)
            dve.wait_ge(s_const, 5)
            nc.vector.tensor_copy(tri_b[:, :], tri[:, :]).then_inc(s_prep, 1)
            link = Chain(dve, s_v)
            dve.wait_ge(s_src, 32)
            link(nc.vector.tensor_scalar(cnt[:, :].bitcast(i32), src_i[:, :], 7, None, ALU.logical_shift_right))
            link(nc.vector.tensor_copy(blk_f[:, :], cnt[:, :].bitcast(i32)))
            link(nc.vector.tensor_scalar(off[:, :].bitcast(i32), src_i[:, :], P - 1, None, ALU.bitwise_and))
            dve.wait_ge(s_dst, 32)
            link(nc.vector.scalar_tensor_tensor(pk_i[:, :], dst_i[:, :], float(PACK), off[:, :].bitcast(i32),
                                                ALU.mult, ALU.add))
            link(nc.vector.tensor_scalar(off[:, :], blk_f[:, :], float(NBLK), float(EMPTY), ALU.is_ge, ALU.mult))
            link(nc.vector.tensor_tensor(pk_i[:, :], pk_i[:, :], off[:, :], ALU.add))

            def one_hot(slot, col):
                return nc.vector.tensor_tensor(hot[:, slot, :].rearrange("p (c b) -> p c b", b=NBUK),
                                               over(blk_f[:, ds(col, STEP)], NBUK), under(iota[:, 0:NBUK], STEP),
                                               ALU.is_equal)

            def count(t):
                for k in range(3):
                    need(dve, s_hotread, 3 * t + k - 2)
                    one_hot(k, 3 * STEP * t + STEP * k).then_inc(s_hot, 1)
            count(0)
            with dve.Fori(1, NSTEP // 3) as t:
                count(t)
            dve.wait_ge(s_hotread, NSTEP)
            link(nc.vector.tensor_copy(cnt[0:NBUK, :], cnt_ps))
            link(nc.vector.reduce_sum(bk[0:NBUK, 0:1], cnt[0:NBUK, :], AX_X))
            link(nc.vector.tensor_scalar(bk_i[0:NBUK, 0:1], bk[0:NBUK, 0:1], float(GE - 1), None, ALU.add))
            link(nc.vector.tensor_scalar(bk_i[0:NBUK, 1:2], bk_i[0:NBUK, 0:1], GE.bit_length() - 1, None,
                                         ALU.logical_shift_right))
            nc.vector.tensor_copy(bk[0:NBUK, 1:2], bk_i[0:NBUK, 1:2]).then_inc(s_gcount, 1)
            link(nc.vector.memset(off[0:NBUK, :], 0.0))
            link(nc.vector.tensor_tensor_scan(off[0:NBUK, :], cnt[0:NBUK, :], off[0:NBUK, :], 0.0, ALU.add, ALU.add))
            link(nc.vector.tensor_tensor(off[0:NBUK, :], off[0:NBUK, :], cnt[0:NBUK, :], ALU.subtract))
            dve.wait_ge(s_base, 1)
            link(nc.vector.tensor_copy(bk[0:NBUK, 2:3], base_ps))
            link(nc.vector.tensor_scalar(bk[0:NBUK, 3:4], bk[0:NBUK, 2:3], float(GE), None, ALU.mult))
            nc.vector.tensor_scalar(off[0:NBUK, :], off[0:NBUK, :], bk[0:NBUK, 3:4], None, ALU.add).then_inc(s_off, 1)
            nc.vector.tensor_scalar(ge[0:NBLK, :], iota_g[0:NBLK, :], bk[0:NBLK, 2:3], None,
                                    ALU.is_ge).then_inc(s_ge, 1)
            dve.wait_ge(s_offT, 1)
            for k in range(2):
                last = nc.vector.tensor_copy(offc[0:CHUNK, k * SPC * NBUK:(k + 1) * SPC * NBUK],
                                             offT_ps[k][:, 0:SPC * NBUK])
            last.then_inc(s_offc, 1)
            dve.wait_ge(s_gid, 1)
            link(nc.vector.tensor_scalar(gid[:, :], gid_ps, -1.0, None, ALU.add))
            link(nc.vector.tensor_copy(blkid[:, :], gid[:, :]))

            def rank(t):
                for k in range(RANKS):
                    q = RANKS * t + k
                    dve.wait_ge(s_hotread, NSTEP + q - 2)
                    one_hot(k % 3, STEP * RANKS * t + STEP * k).then_inc(s_hot, 1)
                    dve.wait_ge(s_hot, NSTEP + q + 1)
                    dve.wait_ge(s_rank, q + 1)
                    need(dve, s_pos, q)
                    nc.vector.tensor_tensor(ranked[:, :], rank_ps[k % 2], hot[:, k % 3, :],
                                            ALU.mult).then_inc(s_ranked, 1)
                    dve.wait_ge(s_ranked, q + 1)
                    nc.vector.reduce_sum(pos_f[:, :], ranked[:, :].rearrange("p (c b) -> p c b", b=NBUK),
                                         AX_X).then_inc(s_pos, 1)
                    dve.wait_ge(s_pos, q + 1)
                    nc.vector.tensor_copy(pos[:, :], pos_f[:, :]).then_inc(s_posi, 1)
                    dve.wait_ge(s_posi, q + 1)
                    nc.vector.tensor_scalar(pos_p[:, :], pos[:, :], P - 1, None, ALU.bitwise_and).then_inc(s_posb, 1)
                    nc.vector.tensor_scalar(pos_t[:, :], pos[:, :], 7, None,
                                            ALU.logical_shift_right).then_inc(s_posb, 1)
                    dve.wait_ge(s_posb, 2 * q + 2)
                    need(dve, s_scat[k], 16 * STEP * t)
                    nc.vector.scalar_tensor_tensor(addr[:, k, :], pos_p[:, :], float(NT), pos_t[:, :],
                                                   ALU.mult, ALU.add).then_inc(s_addr, 1)
                    nc.vector.tensor_copy(pk_ring[:, k, :],
                                          pk_i[:, ds(STEP * RANKS * t + STEP * k, STEP)]).then_inc(s_addr, 1)
            rank(0)
            with dve.Fori(1, NSTEP // RANKS) as t:
                rank(t)

            dve.wait_ge(s_x, 32)
            link(nc.vector.reduce_sum(stat[:, 0, :], x_sb[:, :, :], AX_X))
            link(nc.vector.tensor_scalar(stat[:, 0, :], stat[:, 0, :], 1.0 / D, None, ALU.mult))
            nc.vector.tensor_tensor(h_sb[:, :, :], x_sb[:, :, :], over(stat[:, 0, :], D), ALU.subtract).then_inc(s_xc, 1)
            dve.wait_ge(s_sq, 1)
            link(nc.vector.reduce_sum(stat[:, 1, :], q_sb[:, :, :], AX_X))
            nc.vector.tensor_scalar(stat[:, 1, :], stat[:, 1, :], 1.0 / D, 1e-5, ALU.mult, ALU.add).then_inc(s_var, 1)
            dve.wait_ge(s_std, 1)
            link(nc.vector.reciprocal(stat[:, 3, :], stat[:, 2, :]))
            link(nc.vector.tensor_tensor(h_sb[:, :, :], h_sb[:, :, :], over(stat[:, 3, :], D), ALU.mult))
            nc.vector.tensor_scalar(h_sb[:, :, :], h_sb[:, :, :], 0.0, None, ALU.max).then_inc(s_h, 1)
            for b in range(NBLK):
                dve.wait_ge(s_qkv, b + 1)
                nc.vector.tensor_copy(q_sb[:, b, :], qkv_ps[b % QKV_TILES][:, 0:D]).then_inc(s_q, 1)

            dve.wait_ge(s_back, 16)
            link(nc.vector.tensor_scalar(loc_f[:, :].bitcast(i32), slots[:, :], PACK - 1, None, ALU.bitwise_and))
            link(nc.vector.tensor_copy(loc_f[:, :], loc_f[:, :].bitcast(i32)))
            link(nc.vector.tensor_scalar(slots[:, :], slots[:, :], PACK.bit_length() - 1, None,
                                         ALU.logical_shift_right))
            dve.wait_ge(s_q, NBLK)


def walk(eng, step, first=-2, ahead=RING, drain=4):
    whole = (GROUPS - ahead) // RING
    for i in range(first, RING):
        step(i, i % RING, i // RING)
    with eng.Fori(1, whole) as t:
        for u in range(RING):
            step(RING * t + u, u, t)
    for i in range(RING * whole, GROUPS + drain):
        step(i, i % RING, i // RING)


def inside(g):
    return not isinstance(g, int) or 0 <= g < GROUPS


def block_of(eng, blkid, g):
    return eng.value_load(blkid[0:1, ds(g, 1)], min_val=0, max_val=LASTB)


def gather_groups(pool, table, G, idx, s_idx, s_read, s_gat, s_go):
    def step(i, u, t):
        if not inside(i):
            return
        pool.wait_ge(s_idx, i + 1)
        need(pool, s_read, i - RING + 1)
        pool.sem_inc(s_go, 1)
        for j in range(GT):
            pool.indirect_dma_start(out=G[:, u, j, :], out_offset=None, in_=table,
                                    in_offset=bass.IndirectOffsetOnAxis(ap=idx[:, u, j:j + 1], axis=0)
                                    ).then_inc(s_gat[u], 16)
    walk(pool, step, first=0, drain=0)


def layer0_edges(nc, mem, dram):
    with ExitStack() as ctx:
        def sb(name, shape, dt=f32):
            return ctx.enter_context(nc.sbuf_tensor(name, shape, dt))

        def sem(name):
            return ctx.enter_context(nc.semaphore(name))

        iota, ident, q_sb = mem["iota"], mem["ident"], mem["q"]
        slots, loc_f, blkid, acc = mem["slots"], mem["loc"], mem["blkid"], mem["acc"]
        acc = acc[:, 0:NBLK * AW0]
        PS = mem["psum"]
        G = sb("kv_rows", [P, RING, GT, 2 * D])
        idx = sb("idx_ring", [P, RING, GT], i32)
        hot = sb("hot0", [P, RING, GE])
        hotT = sb("hotT0", [P, 2, GE])
        prod = sb("prod0", [P, GE])
        att = sb("att0", [P, 2, GT * HEADS])
        clip = sb("clip0", [P, 2, GT * HEADS])
        vx = sb("vx0", [P, 2, GT, AW0])
        T_ps = [PS[:, 512 * k:512 * k + GE] for k in (0, 1)]
        Q_ps = [PS[:, 512 * k:512 * k + GE] for k in (2, 3)]
        S_ps = [PS[:, 512 * k:512 * k + AW0] for k in (4, 5)]

        s_zero = sem("s_zero0")
        s_idx = sem("s_idx0")
        s_gat = [sem(f"s_gat0_{k}") for k in range(RING)]
        s_go = sem("s_go0")
        s_hot = sem("s_hot0")
        s_T = sem("s_T0")
        s_hotT = sem("s_hotT0")
        s_q = sem("s_q0")
        s_prod = sem("s_prod0")
        s_red = sem("s_red0")
        s_clip = sem("s_clip0")
        s_ex = sem("s_ex0")
        s_vx = sem("s_vx0")
        s_sum = sem("s_sum0")
        s_acc = sem("s_acc0")
        block = ctx.enter_context(nc.Block())

        @block.gpsimd
        def _(pool):
            gather_groups(pool, dram["kv"], G, idx, s_idx, s_vx, s_gat, s_go)

        @block.scalar
        def _(act):
            def indices(g, u):
                if inside(g):
                    nc.scalar.copy(idx[:, u, :], slots[:, ds(GT * g, GT)]).then_inc(s_idx, 1)

            for g in range(RING):
                indices(g, g)

            def step(i, u, t):
                if inside(i + 2):
                    act.wait_ge(s_T, i + 3)
                    need(act, s_q, i + 1)
                    nc.scalar.activation(hotT[:, u % 2, :], T_ps[u % 2], ACT.Copy).then_inc(s_hotT, 1)
                if inside(i):
                    act.wait_ge(s_clip, i + 1)
                    need(act, s_sum, i - 1)
                    nc.scalar.activation(vx[:, u % 2, :, D:AW0],
                                         clip[:, u % 2, :].rearrange("p (j h) -> p j h", h=HEADS),
                                         ACT.Exp).then_inc(s_ex, 1)
                    indices(i + RING, u)
            walk(act, step, drain=0)

        @block.tensor
        def _(pe):
            def step(i, u, t):
                if inside(i + 1):
                    blk = block_of(pe, blkid, i + 1)
                    pe.wait_ge(s_hotT, i + 2)
                    need(pe, s_prod, i)
                    for j in range(GT):
                        last = nc.tensor.matmul(Q_ps[(u + 1) % 2][:, j * P:(j + 1) * P],
                                                hotT[:, (u + 1) % 2, j * P:(j + 1) * P],
                                                q_sb[:, ds(blk, 1), :].rearrange("p o f -> p (o f)"),
                                                start=True, stop=True)
                    last.then_inc(s_q, 1)
                if inside(i + 2):
                    pe.wait_ge(s_hot, i + 3)
                    need(pe, s_hotT, i + 1)
                    for j in range(GT):
                        last = nc.tensor.transpose(T_ps[u % 2][:, j * P:(j + 1) * P],
                                                   hot[:, (u + 2) % RING, j * P:(j + 1) * P], ident[:, :])
                    last.then_inc(s_T, 1)
                if inside(i - 1):
                    pe.wait_ge(s_vx, i)
                    need(pe, s_acc, i - 2)
                    for j in range(GT):
                        last = nc.tensor.matmul(S_ps[(u + 1) % 2], hot[:, (u - 1) % RING, j * P:(j + 1) * P],
                                                vx[:, (u + 1) % 2, j, :], start=(j == 0), stop=(j == GT - 1))
                    last.then_inc(s_sum, 1)
            walk(pe, step, drain=1)

        @block.vector
        def _(dve):
            nc.vector.memset(acc[:, :], 0.0).then_inc(s_zero, 1)
            dve.wait_ge(s_zero, 1)

            def step(i, u, t):
                if inside(i + 2):
                    need(dve, s_sum, i + 3 - RING)
                    for j in range(GT):
                        last = nc.vector.tensor_scalar(hot[:, (u + 2) % RING, j * P:(j + 1) * P], iota[:, :],
                                                       loc_f[:, ds(GT * (i + 2) + j, 1)], None, ALU.is_equal)
                    last.then_inc(s_hot, 1)
                if inside(i):
                    dve.wait_ge(s_gat[u], 16 * GT * (t + 1))
                    dve.wait_ge(s_q, i + 1)
                    need(dve, s_red, i)
                    nc.vector.tensor_tensor(prod[:, :].rearrange("p (j f) -> p j f", f=D),
                                            Q_ps[u % 2].rearrange("p (j f) -> p j f", f=D),
                                            G[:, u, :, 0:D], ALU.mult).then_inc(s_prod, 1)
                if inside(i - 2):
                    blk = block_of(dve, blkid, i - 2)
                    dve.wait_ge(s_sum, i - 1)
                    need(dve, s_acc, i - 2)
                    rows = acc[:, ds(blk * AW0, AW0)]
                    nc.vector.tensor_tensor(rows, rows, S_ps[u % 2], ALU.add).then_inc(s_acc, 1)
                if inside(i):
                    dve.wait_ge(s_prod, i + 1)
                    nc.vector.reduce_sum(att[:, u % 2, :],
                                         prod[:, :].rearrange("p (a d) -> p a d", d=HD), AX_X).then_inc(s_red, 1)
                if inside(i - 1):
                    dve.wait_ge(s_ex, i)
                    need(dve, s_sum, i - 2)
                    v = vx[:, (u + 1) % 2, :, :]
                    nc.vector.tensor_tensor(v[:, :, 0:D].rearrange("p j (h d) -> p j h d", d=HD),
                                            G[:, (u - 1) % RING, :, D:2 * D].rearrange("p j (h d) -> p j h d", d=HD),
                                            v[:, :, D:AW0].unsqueeze(3).broadcast_to((P, GT, HEADS, HD)),
                                            ALU.mult).then_inc(s_vx, 1)
                if inside(i):
                    dve.wait_ge(s_red, i + 1)
                    need(dve, s_ex, i - 1)
                    nc.vector.tensor_scalar(clip[:, u % 2, :], att[:, u % 2, :], -10.0, 10.0,
                                            ALU.max, ALU.min).then_inc(s_clip, 1)
            walk(dve, step, drain=2)


def between_layers(nc, mem, dram):
    with ExitStack() as ctx:
        def sb(name, shape, dt=f32):
            return ctx.enter_context(nc.sbuf_tensor(name, shape, dt))

        def sem(name):
            return ctx.enter_context(nc.semaphore(name))

        x_sb, q_sb, gb, cb = mem["x"], mem["q"], mem["gb"], mem["cb"]
        h_sb = mem["h"][:, 0:NBLK * D].rearrange("p (t f) -> p t f", f=D)
        acc = mem["acc"][:, 0:NBLK * AW0].rearrange("p (t f) -> p t f", f=AW0)
        table = mem["acc"][:, 0:NBLK * TW].rearrange("p (t f) -> p t f", f=TW)
        sums = mem["h"][:, :].rearrange("p (t f) -> p t f", f=AW1)
        rden = sb("rden", [P, NBLK, HEADS])
        mean = sb("mean", [P, NBLK])
        var = sb("var", [P, NBLK])
        std = sb("std", [P, NBLK])
        rstd = sb("rstd", [P, NBLK])

        s_v = sem("s_v1")
        s_centred = sem("s_centred")
        s_sq = sem("s_sq1")
        s_var = sem("s_var1")
        s_std = sem("s_std1")
        s_tab = sem("s_tab")
        s_h1 = sem("s_h1")
        block = ctx.enter_context(nc.Block())

        @block.sync
        def _(sp):
            sp.wait_ge(s_tab, 1)
            sp.dma_start(dram["h1"].rearrange("(t p) f -> p t f", p=P), table[:, :, :]).then_inc(s_h1, 16)
            sp.wait_ge(s_h1, 16)

        @block.scalar
        def _(act):
            for n, (centred, square) in enumerate(((q_sb, h_sb), (h_sb, q_sb), (table[:, :, 0:D], q_sb))):
                act.wait_ge(s_centred, n + 1)
                nc.scalar.activation(square[:, :, :], centred[:, :, :], ACT.Square).then_inc(s_sq, 1)
                act.wait_ge(s_var, n + 1)
                nc.scalar.activation(std[:, :], var[:, :], ACT.Sqrt).then_inc(s_std, 1)

        @block.vector
        def _(dve):
            link = Chain(dve, s_v)
            tt, ts = nc.vector.tensor_tensor, nc.vector.tensor_scalar

            def normalise(src, centred, squares, n, eps):
                link(nc.vector.reduce_sum(mean[:, :], src, AX_X))
                link(ts(mean[:, :], mean[:, :], 1.0 / D, None, ALU.mult))
                tt(centred[:, :, :], src, over(mean[:, :], D), ALU.subtract).then_inc(s_centred, 1)
                dve.wait_ge(s_sq, n)
                link(nc.vector.reduce_sum(var[:, :], squares[:, :, :], AX_X))
                ts(var[:, :], var[:, :], 1.0 / D, eps, ALU.mult, ALU.add).then_inc(s_var, 1)
                dve.wait_ge(s_std, n)
                link(nc.vector.reciprocal(rstd[:, :], std[:, :]))

            link(ts(rden[:, :, :], acc[:, :, D:AW0], 1e-8, None, ALU.add))
            link(nc.vector.reciprocal(rden[:, :, :], rden[:, :, :]))
            heads = "p t (h d) -> p t h d"
            link(tt(q_sb[:, :, :].rearrange(heads, d=HD), acc[:, :, 0:D].rearrange(heads, d=HD),
                    rden[:, :, :].unsqueeze(3).broadcast_to((P, NBLK, HEADS, HD)), ALU.mult))
            link(tt(q_sb[:, :, :], q_sb[:, :, :], h_sb[:, :, :], ALU.add))
            normalise(q_sb[:, :, :], q_sb, h_sb, 1, 1e-6)
            link(tt(q_sb[:, :, :], q_sb[:, :, :], over(rstd[:, :], D), ALU.mult))
            link(tt(q_sb[:, :, :], q_sb[:, :, :], under(gb[:, 0, :], NBLK), ALU.mult))
            link(tt(q_sb[:, :, :], q_sb[:, :, :], under(gb[:, 1, :], NBLK), ALU.add))
            link(tt(x_sb[:, :, :], x_sb[:, :, :], q_sb[:, :, :], ALU.add))
            normalise(x_sb[:, :, :], h_sb, q_sb, 2, 1e-5)
            link(tt(h_sb[:, :, :], h_sb[:, :, :], over(rstd[:, :], D), ALU.mult))
            nc.vector.memset(table[:, :, D:D + 1], 1.0)
            ts(table[:, :, 0:D], h_sb[:, :, :], 0.0, None, ALU.max).then_inc(s_centred, 1)
            dve.wait_ge(s_sq, 3)
            nc.vector.reduce_sum(var[:, :], q_sb[:, :, :], AX_X).then_inc(s_var, 1)
            dve.wait_ge(s_std, 3)
            link(ts(std[:, :], std[:, :], 1e-30, None, ALU.max))
            link(nc.vector.reciprocal(rstd[:, :], std[:, :]))
            nc.vector.tensor_copy(table[:, :, D + 1:TW], rstd[:, :].unsqueeze(2)).then_inc(s_tab, 1)
            link(ts(mean[:, :], rstd[:, :], cb[:, 0:1], None, ALU.mult))
            link(tt(q_sb[:, :, :], table[:, :, 0:D], over(mean[:, :], D), ALU.mult))
            link(ts(cb[:, 1:2], cb[:, 0:1], -1.0, None, ALU.mult))
            link(tt(cb[:, 2:3], cb[:, 0:1], cb[:, 1:2], ALU.max))
            link(ts(cb[:, 1:2], cb[:, 2:3], 1.01, 1e-3, ALU.mult, ALU.add))
            link(nc.vector.tensor_copy(sums[:, :, :], table[:, :, 0:AW1]))
            link(tt(var[:, :], var[:, :], rstd[:, :], ALU.mult))
            link(tt(var[:, :], var[:, :], mean[:, :], ALU.mult))
            link(ts(mem["top"][:, :], var[:, :], cb[:, 1:2], None, ALU.add))


def layer1_edges(nc, mem, dram):
    with ExitStack() as ctx:
        def sb(name, shape, dt=f32):
            return ctx.enter_context(nc.sbuf_tensor(name, shape, dt))

        def sem(name):
            return ctx.enter_context(nc.semaphore(name))

        iota, ident, q_sb = mem["iota"], mem["ident"], mem["q"]
        slots, loc_f, blkid, cb = mem["slots"], mem["loc"], mem["blkid"], mem["cb"]
        acc = mem["h"]
        PS = mem["psum"]
        G = sb("h_rows", [P, RING, GT, TW])
        idx = sb("idx_ring1", [P, RING, GT], i32)
        hot = sb("hot1", [P, RING, GE])
        hotT = sb("hotT1", [P, RING, GE])
        prod = sb("prod1", [P, GE])
        dots = sb("dots", [P, GT])
        cosb = sb("cosb", [P, GT])
        logit = sb("logit", [P, RING, GT])
        hotl = sb("hotl", [P, 2, GE])
        hotw = sb("hotw", [P, 2, GE])
        gmax = sb("gmax", [P, 1])
        top = mem["top"]
        newtop = sb("newtop", [P, RING])
        fall = sb("fall", [P, 2])
        corr = sb("corr", [P, RING])
        below = sb("below", [P, 2, GT])
        wgt = sb("wgt", [P, 2, GT])
        T_ps = [PS[:, 512 * k:512 * k + GE] for k in (0, 1)]
        Q_ps = [PS[:, 512 * k:512 * k + GE] for k in (2, 3)]
        S_ps = [PS[:, 512 * k:512 * k + AW1] for k in (4, 5)]
        L_ps = PS[:, 512 * 6:512 * 6 + GE]
        E_ps = PS[:, 512 * 7:512 * 7 + GT]

        s_idx = sem("s_idx1")
        s_gat = [sem(f"s_gat1_{k}") for k in range(RING)]
        s_go = sem("s_go1")
        s_hot = sem("s_hot1")
        s_T = sem("s_T1")
        s_hotT = sem("s_hotT1")
        s_q = sem("s_q1")
        s_prod = sem("s_prod1")
        s_dots = sem("s_dots")
        s_cosb = sem("s_cosb")
        s_logit = sem("s_logit")
        s_hotl = sem("s_hotl")
        s_L = sem("s_L")
        s_gmax = sem("s_gmax")
        s_newtop = sem("s_newtop")
        s_fall = sem("s_fall")
        s_top = sem("s_top")
        s_corr = sem("s_corr")
        s_E = sem("s_E")
        s_below = sem("s_below")
        s_wgt = sem("s_wgt")
        s_hotw = sem("s_hotw")
        s_sum = sem("s_sum1")
        s_acc = sem("s_acc1")
        block = ctx.enter_context(nc.Block())

        @block.gpsimd
        def _(pool):
            gather_groups(pool, dram["h1"], G, idx, s_idx, s_sum, s_gat, s_go)

        @block.scalar
        def _(act):
            def indices(g, u):
                if inside(g):
                    nc.scalar.copy(idx[:, u, :], slots[:, ds(GT * g, GT)]).then_inc(s_idx, 1)

            for g in range(RING):
                indices(g, g)

            def step(i, u, t):
                if inside(i + 2):
                    act.wait_ge(s_T, i + 3)
                    need(act, s_E, i + 3 - RING)
                    nc.scalar.activation(hotT[:, (u + 2) % RING, :], T_ps[u % 2], ACT.Copy).then_inc(s_hotT, 1)
                if inside(i - 1):
                    p = (u + 1) % 2
                    act.wait_ge(s_fall, i)
                    need(act, s_acc, i - RING)
                    nc.scalar.activation(corr[:, (u - 1) % RING:(u - 1) % RING + 1], fall[:, p:p + 1],
                                         ACT.Exp).then_inc(s_corr, 1)
                    act.wait_ge(s_below, i)
                    nc.scalar.activation(wgt[:, p, :], below[:, p, :], ACT.Exp).then_inc(s_wgt, 1)
                    act.wait_ge(s_wgt, i)
                    need(act, s_sum, i - 2)
                    for j in range(GT):
                        last = nc.scalar.activation(hotw[:, p, j * P:(j + 1) * P],
                                                    hot[:, (u - 1) % RING, j * P:(j + 1) * P],
                                                    ACT.Copy, scale=wgt[:, p, j:j + 1])
                    last.then_inc(s_hotw, 1)
                if inside(i):
                    act.wait_ge(s_prod, i + 1)
                    indices(i + RING, u)
            walk(act, step, drain=1)

        @block.tensor
        def _(pe):
            def step(i, u, t):
                if inside(i + 1):
                    blk = block_of(pe, blkid, i + 1)
                    pe.wait_ge(s_hotT, i + 2)
                    need(pe, s_prod, i)
                    for j in range(GT):
                        last = nc.tensor.matmul(Q_ps[(u + 1) % 2][:, j * P:(j + 1) * P],
                                                hotT[:, (u + 1) % RING, j * P:(j + 1) * P],
                                                q_sb[:, ds(blk, 1), :].rearrange("p o f -> p (o f)"),
                                                start=True, stop=True)
                    last.then_inc(s_q, 1)
                if inside(i + 2):
                    pe.wait_ge(s_hot, i + 3)
                    need(pe, s_hotT, i + 1)
                    for j in range(GT):
                        last = nc.tensor.transpose(T_ps[u % 2][:, j * P:(j + 1) * P],
                                                   hot[:, (u + 2) % RING, j * P:(j + 1) * P], ident[:, :])
                    last.then_inc(s_T, 1)
                if inside(i - 1):
                    pe.wait_ge(s_newtop, i)
                    need(pe, s_below, i - 1)
                    for j in range(GT):
                        last = nc.tensor.matmul(E_ps[:, j:j + 1], hotT[:, (u - 1) % RING, j * P:(j + 1) * P],
                                                newtop[:, (u - 1) % RING:(u - 1) % RING + 1],
                                                start=True, stop=True)
                    last.then_inc(s_E, 1)
                if inside(i - 2):
                    pe.wait_ge(s_hotw, i - 1)
                    need(pe, s_acc, i - 3)
                    for j in range(GT):
                        last = nc.tensor.matmul(S_ps[u % 2], hotw[:, u % 2, j * P:(j + 1) * P],
                                                G[:, (u - 2) % RING, j, 0:AW1],
                                                start=(j == 0), stop=(j == GT - 1))
                    last.then_inc(s_sum, 1)
                if inside(i):
                    pe.wait_ge(s_hotl, i + 1)
                    need(pe, s_gmax, i)
                    for j in range(GT):
                        last = nc.tensor.transpose(L_ps[:, j * P:(j + 1) * P],
                                                   hotl[:, u % 2, j * P:(j + 1) * P], ident[:, :])
                    last.then_inc(s_L, 1)
            walk(pe, step, drain=2)

        @block.vector
        def _(dve):
            def step(i, u, t):
                if inside(i + 2):
                    need(dve, s_hotw, i + 3 - RING)
                    need(dve, s_T, i + 3 - RING)
                    for j in range(GT):
                        last = nc.vector.tensor_scalar(hot[:, (u + 2) % RING, j * P:(j + 1) * P], iota[:, :],
                                                       loc_f[:, ds(GT * (i + 2) + j, 1)], None, ALU.is_equal)
                    last.then_inc(s_hot, 1)
                if inside(i):
                    dve.wait_ge(s_gat[u], 16 * GT * (t + 1))
                    dve.wait_ge(s_q, i + 1)
                    need(dve, s_dots, i)
                    nc.vector.tensor_tensor(prod[:, :].rearrange("p (j f) -> p j f", f=D),
                                            Q_ps[u % 2].rearrange("p (j f) -> p j f", f=D),
                                            G[:, u, :, 0:D], ALU.mult).then_inc(s_prod, 1)
                if inside(i - 1):
                    blk = block_of(dve, blkid, i - 1)
                    w = (u - 1) % RING
                    v = (u + 1) % 2
                    old, new = top[:, ds(blk, 1)], newtop[:, w:w + 1]
                    dve.wait_ge(s_L, i)
                    need(dve, s_newtop, i - 1)
                    nc.vector.reduce_max(gmax[:, :], L_ps, AX_X).then_inc(s_gmax, 1)
                    dve.wait_ge(s_gmax, i)
                    need(dve, s_top, i - 1)
                    need(dve, s_E, i - RING)
                    nc.vector.tensor_tensor(new, old, gmax[:, :], ALU.max).then_inc(s_newtop, 1)
                if inside(i):
                    dve.wait_ge(s_prod, i + 1)
                    need(dve, s_cosb, i)
                    nc.vector.reduce_sum(dots[:, :], prod[:, :].rearrange("p (j f) -> p j f", f=D),
                                         AX_X).then_inc(s_dots, 1)
                if inside(i - 1):
                    dve.wait_ge(s_newtop, i)
                    need(dve, s_corr, i - 2)
                    nc.vector.tensor_tensor(fall[:, v:v + 1], old, new, ALU.subtract).then_inc(s_fall, 1)
                    dve.wait_ge(s_fall, i)
                    nc.vector.tensor_tensor(old, old, new, ALU.max).then_inc(s_top, 1)
                if inside(i):
                    dve.wait_ge(s_dots, i + 1)
                    need(dve, s_logit, i)
                    nc.vector.tensor_tensor(cosb[:, :].unsqueeze(2), dots[:, :].unsqueeze(2), G[:, u, :, D + 1:TW],
                                            ALU.mult).then_inc(s_cosb, 1)
                if inside(i - 3):
                    blk3 = block_of(dve, blkid, i - 3)
                    dve.wait_ge(s_sum, i - 2)
                    dve.wait_ge(s_corr, i - 2)
                    need(dve, s_acc, i - 3)
                    rows = acc[:, ds(blk3 * AW1, AW1)]
                    w3 = (u - 3) % RING
                    nc.vector.scalar_tensor_tensor(rows, rows, corr[:, w3:w3 + 1], S_ps[(u - 3) % 2],
                                                   ALU.mult, ALU.add).then_inc(s_acc, 1)
                if inside(i):
                    dve.wait_ge(s_cosb, i + 1)
                    nc.vector.tensor_scalar(logit[:, u, :], cosb[:, :], cb[:, 1:2], None,
                                            ALU.add).then_inc(s_logit, 1)
                if inside(i - 1):
                    dve.wait_ge(s_E, i)
                    need(dve, s_wgt, i - 2)
                    nc.vector.tensor_tensor(below[:, v, :], logit[:, w, :], E_ps, ALU.subtract).then_inc(s_below, 1)
                if inside(i):
                    dve.wait_ge(s_logit, i + 1)
                    need(dve, s_L, i - 1)
                    for j in range(GT):
                        last = nc.vector.tensor_scalar(hotl[:, u % 2, j * P:(j + 1) * P], iota[:, :],
                                                       loc_f[:, ds(GT * i + j, 1)], logit[:, u, j:j + 1],
                                                       ALU.is_equal, ALU.mult)
                    last.then_inc(s_hotl, 1)
            walk(dve, step, drain=3)


def finish(nc, mem, out):
    with ExitStack() as ctx:
        den = ctx.enter_context(nc.sbuf_tensor("den", [P, NBLK], f32))
        s_v = ctx.enter_context(nc.semaphore("s_v2"))
        s_res = ctx.enter_context(nc.semaphore("s_res"))
        s_out = ctx.enter_context(nc.semaphore("s_out"))
        x_sb, q_sb = mem["x"], mem["q"]
        acc = mem["h"][:, :].rearrange("p (t f) -> p t f", f=AW1)
        half = LASTB // 2
        block = ctx.enter_context(nc.Block())

        @block.vector
        def _(dve):
            link = Chain(dve, s_v)
            sums = acc[:, :, D:AW1].rearrange("p t o -> p (t o)")
            link(nc.vector.reciprocal(den[:, :], sums))
            for a, b in ((0, half), (half, NBLK)):
                link(nc.vector.tensor_tensor(q_sb[:, a:b, :], acc[:, a:b, 0:D], over(den[:, a:b], D), ALU.mult))
                nc.vector.tensor_tensor(q_sb[:, a:b, :], q_sb[:, a:b, :], x_sb[:, a:b, :], ALU.add).then_inc(s_res, 1)

        @block.sync
        def _(sp):
            sp.wait_ge(s_res, 1)
            sp.dma_start(out[0:half * P, :].rearrange("(t p) f -> p t f", p=P), q_sb[:, 0:half, :]).then_inc(s_out, 16)
            sp.wait_ge(s_res, 2)
            sp.dma_start(out[half * P:LASTB * P, :].rearrange("(t p) f -> p t f", p=P),
                         q_sb[:, half:LASTB, :]).then_inc(s_out, 16)
            sp.dma_start(out[LASTB * P:N, :], q_sb[0:TAIL, LASTB, :]).then_inc(s_out, 16)
            sp.wait_ge(s_out, 48)


_INS = ["x", "src", "dst", "L0_gnn_Wq", "L0_gnn_Wk", "L0_gnn_Wv", "L0_gnn_gamma", "L0_gnn_beta", "L1_gnn_beta"]


def program(nc, x, src, dst, wq, wk, wv, gamma, beta, cos_beta, out):
    dram = {
        "sorted": nc.dram_tensor("sorted_edges", (P * NT, 1), i32).ap(),
        "offs": nc.dram_tensor("column_offsets", (COLS, NBUK), f32).ap(),
        "kv": nc.dram_tensor("kv_table", (NPAD, 2 * D), f32).ap(),
        "h1": nc.dram_tensor("h1_table", (NPAD, TW), f32).ap(),
    }
    with ExitStack() as ctx:
        def sb(name, shape, dt=f32):
            return ctx.enter_context(nc.sbuf_tensor(name, shape, dt))
        mem = {
            "iota": sb("iota", [P, P]),
            "ident": sb("ident", [P, P]),
            "x": sb("x_sb", [P, NBLK, D]),
            "h": sb("h_sb", [P, NBLK * AW1]),
            "q": sb("q_sb", [P, NBLK, D]),
            "slots": sb("slots", [P, NT], i32),
            "loc": sb("loc_f", [P, NT]),
            "blkid": sb("blkid", [1, GROUPS], i32),
            "acc": sb("acc", [P, max(NBLK * AW0, 2 * CHUNK * NBUK)]),
            "gb": sb("gb_sb", [P, 2, D]),
            "cb": sb("cb_sb", [P, 3]),
            "top": sb("top", [P, NBLK]),
            "psum": ctx.enter_context(nc.psum_tensor("psum", [P, 4096], f32)),
        }
        sort_and_project(nc, mem, dram, (src, dst, x, wq, wk, wv, gamma, beta, cos_beta))
        layer0_edges(nc, mem, dram)
        between_layers(nc, mem, dram)
        layer1_edges(nc, mem, dram)
        finish(nc, mem, out)


def kernel(**inputs):
    import numpy as np
    import concourse.bacc as bacc
    from concourse.bass_utils import run_bass_kernel_spmd

    nc = bacc.Bacc("TRN2", target_bir_lowering=False, num_devices=1)
    arrays, args = {}, []
    for name in _INS:
        a = np.ascontiguousarray(inputs[name])
        arrays[f"in_{name}"] = a
        args.append(nc.dram_tensor(f"in_{name}", a.shape, mybir.dt.from_np(a.dtype), kind="ExternalInput").ap())
    args.append(nc.dram_tensor("out_0", (N, D), f32, kind="ExternalOutput").ap())
    program(nc, *args)
    return run_bass_kernel_spmd(nc, [arrays], core_ids=[0]).results[0]["out_0"]
```

```python
import concourse.bass as bass
from concourse import mybir
from contextlib import ExitStack

P = 128
N = 6250
D = 128
HEADS = 8
HD = D // HEADS
E = 206250
NBLK = (N + P - 1) // P
NPAD = NBLK * P
NBUK = NBLK + 1
TAIL = N - (NBLK - 1) * P
LASTB = NBLK - 1

STEP = 10
CHUNK = 90
SPC = CHUNK // STEP
CROW = CHUNK * NBUK // 9
NCHUNK = 18
COLS = NCHUNK * CHUNK
LASTROW = E - (P - 1) * COLS
PAD_SRC = P * NBLK
BATCH = 5
BRING = 3

GT = 4
GE = GT * P
ROW = GT
CG = (P * CHUNK + NBUK * (ROW - 1) + ROW * P - 1) // (ROW * P)
ALL_ROWS = (E + NCHUNK * NBLK * (ROW - 1)) // ROW
GROUPS = (ALL_ROWS + NBLK * (P - 1)) // P
ROOM = GROUPS + NCHUNK * CG
NT = GT * GROUPS
PACK = 256

RING0 = 6
RING1 = 8
AW0 = D + HEADS
AW1 = D + 1
TW = D + 2
QKV_TILES = 4

f32 = mybir.dt.float32
bf16 = mybir.dt.bfloat16
i32 = mybir.dt.int32
ALU = mybir.AluOpType
ACT = mybir.ActivationFunctionType
AX_X = mybir.AxisListType.X
ds = bass.ds


def need(eng, semaphore, value):
    if isinstance(value, int) and value <= 0:
        return
    eng.wait_ge(semaphore, value)


class Chain:

    def __init__(self, eng, semaphore):
        self.eng, self.semaphore, self.count = eng, semaphore, 0

    def __call__(self, instruction):
        self.count += 1
        instruction.then_inc(self.semaphore, 1)
        self.eng.wait_ge(self.semaphore, self.count)


def over(ap, n):
    return ap.unsqueeze(2).broadcast_to((ap.shape[0], ap.shape[1], n))


def under(ap, n):
    return ap.unsqueeze(1).broadcast_to((ap.shape[0], n, ap.shape[1]))


def sort_and_project(nc, mem, dram, ins):
    src, dst, x, wq, wk, wv, gamma, beta, cos_beta = ins
    with ExitStack() as ctx:
        def sb(name, shape, dt=f32):
            return ctx.enter_context(nc.sbuf_tensor(name, shape, dt))

        def sem(name):
            return ctx.enter_context(nc.semaphore(name))

        iota, ident, x_sb, q_sb = mem["iota"], mem["ident"], mem["x"], mem["q"]
        h_sb = mem["h"][:, 0:NBLK * D].rearrange("p (t f) -> p t f", f=D)
        slots, loc_f, blkid, gb_sb, cb_sb = mem["slots"], mem["loc"], mem["blkid"], mem["gb"], mem["cb"]
        PS = mem["psum"]

        src_i = sb("src_i", [P, COLS], i32)
        dst_i = sb("dst_i", [P, COLS], i32)
        blk_b = sb("blk_b", [P, COLS], bf16)
        pk_f = sb("pk_f", [P, COLS])
        tri = sb("tri", [P, P])
        tri_b = sb("tri_b", [P, P], bf16)
        bidiag = sb("bidiag", [P, P])
        ones_b = sb("ones_b", [P, 1], bf16)
        ones_2 = sb("ones_2", [2, P], bf16)
        zeros_b = sb("zeros_b", [1, P], bf16)
        iota_g = sb("iota_g", [P, GROUPS])
        rho = sb("rho", [P, CG])
        keep = sb("keep", [P, 1])
        room = sb("room", [P, NCHUNK])
        by_bucket = sb("by_bucket", [P, 2 * COLS])
        cnt = by_bucket[:, 0:COLS]
        off = by_bucket[:, COLS:2 * COLS]
        start = by_bucket[:, 0:CG * P]
        offc = sb("offc", [P, NCHUNK * NBUK], i32)
        cnt_row = mem["acc"][0:1, 0:2 * CHUNK * NBUK].rearrange("p (r c) -> p r c", r=2)
        offrow = mem["acc"][0:2, 0:CHUNK * NBUK].bitcast(bf16).rearrange("p (r c) -> p r c", r=2)
        row_no = mem["h"][:, 0:CG * P]
        free = CG * P
        bucket_no = mem["h"][:, free:free + NBUK * CHUNK // 2].bitcast(bf16).rearrange("p (b c) -> p b c", c=CHUNK)
        free += NBUK * CHUNK // 2
        off_parts = mem["h"][:, free:free + NCHUNK * NBUK].bitcast(bf16).rearrange("p (h k) -> p h k", h=2)
        hot = q_sb.rearrange("p t f -> p (t f)").bitcast(bf16)[:, 0:2 * NBUK * CHUNK].rearrange(
            "p (r b c) -> p r b c", r=2, c=CHUNK)
        ranked = sb("ranked", [P, 2, NBUK * STEP])
        pos_f = sb("pos_f", [P, CHUNK])
        pos = sb("pos", [P, CHUNK], i32)
        pos_r = sb("pos_r", [P, CHUNK], i32)
        pos_g = sb("pos_g", [P, CHUNK], i32)
        pos_s = sb("pos_s", [P, CHUNK], i32)
        part_f = sb("part_f", [P, CHUNK])
        place_f = sb("place_f", [P, CHUNK])
        to_part = sb("to_part", [P, BRING, BATCH, P])
        to_place = sb("to_place", [P, BRING, BATCH, CG * ROW])
        row_i = sb("row_i", [P, 3, CG], i32)
        addr = sb("addr", [P, 2, CG], i32)
        stage = sb("stage", [P, 2, CG * ROW], i32)
        bk = sb("bk", [P, 4])
        bk_i = sb("bk_i", [P, 2], i32)
        n_i = sb("n_i", [P, 2, NCHUNK], i32)
        rows = sb("rows", [P, NCHUNK])
        before = sb("before", [P, NCHUNK])
        first = sb("first", [P, NCHUNK])
        edge = sb("edge", [P, NCHUNK])
        delta = sb("delta", [P, NCHUNK])
        step_d = sb("step_d", [P, NCHUNK])
        ge = sb("ge", [P, GROUPS], bf16)
        gid = sb("gid", [1, GROUPS])
        w_sb = sb("w_sb", [P, 3 * D])
        stat = sb("stat", [P, 4, NBLK])
        hT = sb("hT", [P, QKV_TILES * P])
        kv = sb("kv", [P, QKV_TILES, 2 * D])

        cnt_ps = [PS[0:1, 1536 * k:1536 * k + 1536].rearrange("p (i c) -> p i c", c=512)[:, :, 0:CROW]
                  for k in range(2)]
        rank_ps = [PS[:, 2048 + 512 * k:2048 + 512 * k + NBUK * STEP] for k in range(2)]
        place_ps = [PS[:, 512 * k:512 * k + CG * ROW] for k in range(2)]
        row_ps = PS[:, 1024:1024 + CG]
        base_ps = PS[0:NBUK, 3072:3073]
        first_ps = PS[0:NBUK, 3074:3074 + NCHUNK]
        step_ps = PS[0:NBUK, 3104:3104 + NCHUNK]
        gid_ps = PS[0:1, 3584:3584 + GROUPS]
        offT_ps = [PS[0:CHUNK, 512 * k:512 * k + 512] for k in range(2)]
        hT_ps = PS[:, 3072:3584]
        qkv_ps = [PS[:, 512 * k:512 * k + 3 * D] for k in range(QKV_TILES)]

        s_const = sem("s_const")
        s_pool = sem("s_pool")
        s_pads = sem("s_pads")
        s_src, s_dst, s_x, s_w, s_gb = (sem(n) for n in ("s_src", "s_dst", "s_x", "s_w", "s_gb"))
        s_filled = sem("s_filled")
        s_v = sem("s_v")
        s_prep = sem("s_prep")
        s_hot = sem("s_hot")
        s_hotread = sem("s_hotread")
        s_cnt = sem("s_cnt")
        s_cntrow = sem("s_cntrow")
        s_cntd = [sem("s_cntd0"), sem("s_cntd1")]
        s_cntb = sem("s_cntb")
        s_packed = sem("s_packed")
        s_edge = sem("s_edge")
        s_sign = sem("s_sign")
        s_equal = sem("s_equal")
        s_gcount = sem("s_gcount")
        s_base = sem("s_base")
        s_delta = sem("s_delta")
        s_step = sem("s_step")
        s_ge = sem("s_ge")
        s_gid = sem("s_gid")
        s_off = sem("s_off")
        s_offT = sem("s_offT")
        s_offc = sem("s_offc")
        s_offd = sem("s_offd")
        s_row = [sem("s_row0"), sem("s_row1")]
        s_rank = sem("s_rank")
        s_ranked = sem("s_ranked")
        s_pos = sem("s_pos")
        s_split = sem("s_split")
        s_rowi = sem("s_rowi")
        s_start = sem("s_start")
        s_rows = sem("s_rows")
        s_rowsread = sem("s_rowsread")
        s_addr = sem("s_addr")
        s_topart = sem("s_topart")
        s_onehot = sem("s_onehot")
        s_used = sem("s_used")
        s_placed = sem("s_placed")
        s_stage = sem("s_stage")
        s_scat = [sem("s_scat0"), sem("s_scat1")]
        s_go = sem("s_go")
        s_sorted = sem("s_sorted")
        s_back = sem("s_back")
        s_xc = sem("s_xc")
        s_sq = sem("s_sq")
        s_var = sem("s_var")
        s_std = sem("s_std")
        s_h = sem("s_h")
        s_hT = sem("s_hT")
        s_hTc = sem("s_hTc")
        s_qkv = sem("s_qkv")
        s_q = sem("s_q")
        s_kv = sem("s_kv")
        s_kvd = sem("s_kvd")

        slots_d = dram["sorted"].rearrange("(p g) j -> p (g j)", p=P)[:, 0:NT]
        block = ctx.enter_context(nc.Block())

        @block.sync
        def _(sp):
            sp.wait_ge(s_pads, 3)
            for tile, edges, done in ((src_i, src, s_src), (dst_i, dst, s_dst)):
                sp.dma_start(tile[0:P - 1, :], edges[0:(P - 1) * COLS].rearrange("(p c) -> p c", c=COLS)).then_inc(done, 16)
                sp.dma_start(tile[P - 1:P, 0:LASTROW],
                             edges[(P - 1) * COLS:E].rearrange("(p c) -> p c", p=1)).then_inc(done, 16)
            sp.wait_ge(s_pads, 4)
            sp.dma_start(slots_d, slots[:, :]).then_inc(s_filled, 16)
            sp.dma_start(x_sb[:, 0:LASTB, :], x[0:LASTB * P, :].rearrange("(t p) f -> p t f", p=P)).then_inc(s_x, 16)
            sp.dma_start(x_sb[0:TAIL, LASTB, :], x[LASTB * P:N, :]).then_inc(s_x, 16)
            for k, w in enumerate((wq, wk, wv)):
                sp.dma_start(w_sb[:, k * D:(k + 1) * D], w).then_inc(s_w, 16)
            for k, w in enumerate((gamma, beta)):
                sp.dma_start(gb_sb[:, k, :], w.rearrange("(o f) -> o f", o=1).broadcast_to((P, D))).then_inc(s_gb, 16)
            sp.dma_start(cb_sb[:, 0:1], cos_beta.rearrange("(o f) -> o f", o=1).broadcast_to((P, 1))).then_inc(s_gb, 16)
            with sp.Fori(0, NCHUNK // 2) as t:
                for r in range(2):
                    sp.wait_ge(s_cntrow, 6 * t + 3 * r + 3)
                    sp.dma_start(dram["counts"][ds(2 * t + r, 1), :], cnt_row[:, r, :]).then_inc(s_cntd[r], 16)
            for r in range(2):
                sp.wait_ge(s_cntd[r], 16 * (NCHUNK // 2))
            sp.dma_start(cnt[0:NBUK, :].rearrange("b (k c) -> b k c", c=CHUNK),
                         dram["counts"].rearrange("k (b c) -> b k c", c=CHUNK)).then_inc(s_cntb, 16)
            sp.wait_ge(s_offc, 1)
            for part in range(2):
                sp.dma_start(dram["offs"][part].rearrange("(k c) b -> c k b", c=CHUNK),
                             off_parts[0:CHUNK, part, :].rearrange("c (k b) -> c k b", b=NBUK)).then_inc(s_offd, 16)
            sp.wait_ge(s_offd, 32)
            offs = dram["offs"].rearrange("h (k c) b -> h k (c b)", c=CHUNK)
            for r in range(2):
                sp.dma_start(offrow[:, r:r + 1, :], offs[:, r:r + 1, :]).then_inc(s_row[r], 16)
            with sp.Fori(1, NCHUNK // 2) as t:
                for r in range(2):
                    sp.wait_ge(s_rank, 2 * SPC * t - SPC * (1 - r))
                    sp.dma_start(offrow[:, r:r + 1, :], offs[:, ds(2 * t + r, 1), :]).then_inc(s_row[r], 16)
            for b in range(0, NBLK, QKV_TILES):
                n = min(QKV_TILES, NBLK - b)
                sp.wait_ge(s_kv, b + n)
                sp.dma_start(dram["kv"][b * P:(b + n) * P, :].rearrange("(t p) f -> p t f", p=P),
                             kv[:, 0:n, :]).then_inc(s_kvd, 16)
            sp.wait_ge(s_sorted, 1)
            sp.dma_start(slots[:, :], slots_d).then_inc(s_back, 16)
            sp.wait_ge(s_kvd, 16 * ((NBLK + QKV_TILES - 1) // QKV_TILES))
            sp.wait_ge(s_gb, 48)
            sp.wait_ge(s_filled, 16)

        @block.gpsimd
        def _(pool):
            nc.gpsimd.iota(iota[:, :], [[1, P]], base=0, channel_multiplier=0,
                           allow_small_or_imprecise_dtypes=True).then_inc(s_const, 1)
            nc.gpsimd.iota(iota_g[:, :], [[1, GROUPS]], base=0, channel_multiplier=0,
                           allow_small_or_imprecise_dtypes=True).then_inc(s_const, 1)
            nc.gpsimd.memset(ident[:, :], 0.0).then_inc(s_pool, 1)
            nc.gpsimd.memset(tri[:, :], 1.0).then_inc(s_pool, 1)
            nc.gpsimd.iota(bucket_no, [[1, NBUK], [0, CHUNK]], base=0, channel_multiplier=0,
                           allow_small_or_imprecise_dtypes=True).then_inc(s_const, 1)
            nc.gpsimd.iota(row_no, [[1, CG * P]], base=0, channel_multiplier=0,
                           allow_small_or_imprecise_dtypes=True).then_inc(s_const, 1)
            nc.gpsimd.memset(bidiag[:, :], 0.0).then_inc(s_pool, 1)
            nc.gpsimd.memset(keep[:, :], 1.0).then_inc(s_pool, 1)
            nc.gpsimd.iota(rho[:, :], [[P, CG]], base=0, channel_multiplier=1,
                           allow_small_or_imprecise_dtypes=True).then_inc(s_const, 1)
            nc.gpsimd.iota(room[:, :], [[CG * P, NCHUNK]], base=GROUPS * P, channel_multiplier=0,
                           allow_small_or_imprecise_dtypes=True).then_inc(s_pool, 1)
            pool.wait_ge(s_pool, 5)
            nc.gpsimd.affine_select(out=ident[:, :], in_=ident[:, :], compare_op=ALU.not_equal, fill=1.0,
                                    base=0, pattern=[[-1, P]], channel_multiplier=1).then_inc(s_const, 1)
            nc.gpsimd.affine_select(out=tri[:, :], in_=tri[:, :], compare_op=ALU.is_gt, fill=0.0,
                                    base=0, pattern=[[1, P]], channel_multiplier=-1).then_inc(s_const, 1)
            nc.gpsimd.affine_select(out=keep[:, :], in_=keep[:, :], compare_op=ALU.not_equal, fill=0.0,
                                    base=-NBLK, pattern=[[0, 1]], channel_multiplier=1).then_inc(s_const, 1)
            nc.gpsimd.affine_select(out=room[:, :], in_=room[:, :], compare_op=ALU.is_equal, fill=0.0,
                                    base=-NBLK, pattern=[[0, NCHUNK]], channel_multiplier=1).then_inc(s_const, 1)
            nc.gpsimd.affine_select(out=bidiag[:, :], in_=bidiag[:, :], compare_op=ALU.not_equal, fill=1.0,
                                    base=0, pattern=[[-1, P]], channel_multiplier=1).then_inc(s_pool, 1)
            pool.wait_ge(s_pool, 6)
            nc.gpsimd.affine_select(out=bidiag[:, :], in_=bidiag[:, :], compare_op=ALU.not_equal, fill=-1.0,
                                    base=1, pattern=[[-1, P]], channel_multiplier=1).then_inc(s_const, 1)
            pool.wait_ge(s_filled, 16)
            with pool.Fori(0, NCHUNK // 2) as t:
                for r in range(2):
                    pool.wait_ge(s_addr, 2 * t + r + 1)
                    pool.wait_ge(s_stage, 2 * t + r + 1)
                    pool.sem_inc(s_go, 1)
                    for g in range(CG):
                        pool.indirect_dma_start(
                            out=dram["sorted"], out_offset=bass.IndirectOffsetOnAxis(ap=addr[:, r, g:g + 1], axis=0),
                            in_=stage[:, r, g * ROW:(g + 1) * ROW], in_offset=None).then_inc(s_scat[r], 16)
            for r in range(2):
                pool.wait_ge(s_scat[r], 16 * CG * (NCHUNK // 2))
            pool.sem_inc(s_sorted, 1)

        @block.tensor
        def _(pe):
            pe.wait_ge(s_const, 10)
            pe.wait_ge(s_prep, 4)
            pe.sem_inc(s_used, BRING)
            def count(t):
                for r in range(2):
                    pe.wait_ge(s_hot, 2 * t + r + 1)
                    for m in range(3):
                        k = (3 * r + m) % 2
                        need(pe, s_cntrow, 6 * t + 3 * r + m - 1)
                        flat = hot[:, r, :, :].rearrange("p b c -> p (b c)")
                        for i in range(3):
                            last = nc.tensor.matmul(cnt_ps[k][:, i, :], ones_b[:, :],
                                                    flat[:, (3 * m + i) * CROW:(3 * m + i + 1) * CROW],
                                                    start=True, stop=True)
                        last.then_inc(s_cnt, 1)
            count(0)
            with pe.Fori(1, NCHUNK // 2) as t:
                count(t)
            pe.wait_ge(s_gcount, 2)
            nc.tensor.matmul(base_ps, tri[0:NBUK, 0:NBUK], bk[0:NBUK, 1:2], start=True, stop=True)
            nc.tensor.matmul(first_ps, tri[0:NBUK, 0:NBUK], rows[0:NBUK, :], start=True, stop=True).then_inc(s_base, 1)
            pe.wait_ge(s_off, 1)
            for k in range(NCHUNK):
                last = nc.tensor.transpose(offT_ps[k // SPC][:, (k % SPC) * NBUK:(k % SPC + 1) * NBUK],
                                           off[0:NBUK, k * CHUNK:(k + 1) * CHUNK], ident[0:NBUK, 0:NBUK])
            last.then_inc(s_offT, 1)
            pe.wait_ge(s_delta, 1)
            nc.tensor.matmul(step_ps, bidiag[0:NBUK, 0:NBUK], delta[0:NBUK, :], start=True, stop=True).then_inc(s_step, 1)
            pe.wait_ge(s_ge, 1)
            nc.tensor.matmul(gid_ps, ones_b[0:NBLK, :], ge[0:NBLK, :], start=True, stop=True).then_inc(s_gid, 1)
            pe.wait_ge(s_offc, 1)

            def sort_chunks(t):
                for r in range(2):
                    ch = 2 * t + r
                    pe.wait_ge(s_hot, NCHUNK + ch + 1)
                    for m in range(SPC):
                        k = (SPC * r + m) % 2
                        need(pe, s_ranked, 2 * SPC * t + SPC * r + m - 1)
                        ranks = nc.tensor.matmul(rank_ps[k], tri_b[:, :], hot[:, r, :, m * STEP:(m + 1) * STEP],
                                                 start=True, stop=False)
                        if m == SPC - 1:
                            ranks.then_inc(s_hotread, 1)
                        if m == 0:
                            pe.wait_ge(s_row[r], 16 * t + 16)
                        o = offrow[:, r, m * STEP * NBUK:(m + 1) * STEP * NBUK]
                        nc.tensor.matmul(rank_ps[k], ones_2[:, :], o.rearrange("p (c b) -> p b c", b=NBUK),
                                         start=False, stop=True).then_inc(s_rank, 1)
                    pe.wait_ge(s_start, ch + 1)
                    need(pe, s_rowsread, ch)
                    for g in range(CG):
                        last = nc.tensor.matmul(row_ps[:, g:g + 1], start[0:NBUK, g * P:(g + 1) * P],
                                                step_d[0:NBUK, ds(ch, 1)], start=True, stop=True)
                    last.then_inc(s_rows, 1)
                    need(pe, s_stage, ch - 1)
                    nc.tensor.matmul(place_ps[r], zeros_b[:, :], zeros_b[:, 0:CG * ROW], start=True, stop=False)
                    with pe.Fori(0, CHUNK // (BATCH * BRING)) as n:
                        for k in range(BRING):
                            q = CHUNK // BATCH * ch + BRING * n + k
                            pe.wait_ge(s_topart, q + 1)
                            pe.wait_ge(s_onehot, q + 1)
                            for c in range(BATCH):
                                last = nc.tensor.matmul(place_ps[r], to_part[:, k, c, :], to_place[:, k, c, :],
                                                        start=False, stop=False)
                            last.then_inc(s_used, 1)
                    nc.tensor.matmul(place_ps[r], zeros_b[:, :], zeros_b[:, 0:CG * ROW],
                                     start=False, stop=True).then_inc(s_placed, 1)
            sort_chunks(0)
            with pe.Fori(1, NCHUNK // 2) as t:
                sort_chunks(t)
            pe.wait_ge(s_stage, NCHUNK)
            pe.wait_ge(s_rowsread, NCHUNK)
            pe.wait_ge(s_w, 48)
            pe.wait_ge(s_h, 1)
            for i, b in enumerate(range(0, NBLK, QKV_TILES)):
                n = min(QKV_TILES, NBLK - b)
                need(pe, s_hTc, i)
                for k in range(n):
                    last = nc.tensor.transpose(hT_ps[:, k * P:(k + 1) * P], h_sb[:, b + k, :], ident[:, :])
                last.then_inc(s_hT, 1)
                pe.wait_ge(s_hTc, i + 1)
                for k in range(n):
                    need(pe, s_q, b + k + 1 - QKV_TILES)
                    need(pe, s_kv, b + k + 1 - QKV_TILES)
                    nc.tensor.matmul(qkv_ps[k], hT[:, k * P:(k + 1) * P], w_sb[:, :],
                                     start=True, stop=True).then_inc(s_qkv, 1)

        @block.scalar
        def _(act):
            def counts(t):
                for r in range(2):
                    need(act, s_cntd[r], 16 * t)
                    for m in range(3):
                        act.wait_ge(s_cnt, 6 * t + 3 * r + m + 1)
                        nc.scalar.activation(
                            cnt_row[:, r, 3 * m * CROW:3 * (m + 1) * CROW].rearrange("p (i c) -> p i c", c=CROW),
                            cnt_ps[(3 * r + m) % 2], ACT.Copy).then_inc(s_cntrow, 1)
            counts(0)
            with act.Fori(1, NCHUNK // 2) as t:
                counts(t)
            act.wait_ge(s_packed, 1)
            act.wait_ge(s_offT, 1)
            act.wait_ge(s_edge, 1)

            def stage_rows(t):
                for r in range(2):
                    ch = 2 * t + r
                    need(act, s_rows, ch)
                    nc.scalar.activation(start[0:NBUK, :], row_no[0:NBUK, :], ACT.Sign,
                                         bias=edge[0:NBUK, ds(ch, 1)]).then_inc(s_sign, 1)
                    act.wait_ge(s_sign, ch + 1)
                    nc.scalar.activation(start[0:NBUK, :], start[0:NBUK, :], ACT.Relu).then_inc(s_start, 1)
                    with act.Fori(0, CHUNK // (BATCH * BRING)) as n:
                        for k in range(BRING):
                            q = CHUNK // BATCH * ch + BRING * n + k
                            act.wait_ge(s_equal, q + 1)
                            for c in range(BATCH):
                                last = nc.scalar.activation(
                                    to_place[:, k, c, :], to_place[:, k, c, :], ACT.Copy,
                                    scale=pk_f[:, ds(CHUNK * ch + BATCH * BRING * n + BATCH * k + c, 1)])
                            last.then_inc(s_onehot, 1)
                    act.wait_ge(s_placed, 2 * t + r + 1)
                    need(act, s_scat[r], 16 * CG * t)
                    nc.scalar.copy(stage[:, r, :], place_ps[r]).then_inc(s_stage, 1)
            stage_rows(0)
            with act.Fori(1, NCHUNK // 2) as t:
                stage_rows(t)
            act.wait_ge(s_xc, 1)
            nc.scalar.activation(q_sb[:, :, :], h_sb[:, :, :], ACT.Square).then_inc(s_sq, 1)
            act.wait_ge(s_var, 1)
            nc.scalar.activation(stat[:, 2, :], stat[:, 1, :], ACT.Sqrt).then_inc(s_std, 1)
            for i, b in enumerate(range(0, NBLK, QKV_TILES)):
                n = min(QKV_TILES, NBLK - b)
                act.wait_ge(s_hT, i + 1)
                need(act, s_qkv, b)
                nc.scalar.activation(hT[:, 0:n * P], hT_ps[:, 0:n * P], ACT.Copy).then_inc(s_hTc, 1)
                need(act, s_kvd, 16 * i)
                for k in range(n):
                    act.wait_ge(s_q, b + k + 1)
                    nc.scalar.activation(kv[:, k, :], qkv_ps[k][:, D:3 * D], ACT.Copy).then_inc(s_kv, 1)

        @block.vector
        def _(dve):
            nc.vector.memset(src_i[96:P, LASTROW:COLS], PAD_SRC).then_inc(s_pads, 1)
            nc.vector.memset(dst_i[96:P, LASTROW:COLS], 0).then_inc(s_pads, 1)
            nc.vector.memset(x_sb[:, LASTB, :], 0.0).then_inc(s_pads, 1)
            nc.vector.memset(slots[:, :], 0).then_inc(s_pads, 1)
            nc.vector.memset(ones_b[:, :], 1.0).then_inc(s_prep, 1)
            nc.vector.memset(zeros_b[:, :], 0.0).then_inc(s_prep, 1)
            nc.vector.memset(ones_2[:, :], 1.0).then_inc(s_prep, 1)
            dve.wait_ge(s_const, 10)
            nc.vector.tensor_copy(tri_b[:, :], tri[:, :]).then_inc(s_prep, 1)
            link = Chain(dve, s_v)
            tt, ts, stt = nc.vector.tensor_tensor, nc.vector.tensor_scalar, nc.vector.scalar_tensor_tensor
            lsr = ALU.logical_shift_right
            scratch = off[:, :].bitcast(i32)
            dve.wait_ge(s_src, 32)
            link(ts(scratch, src_i[:, :], 7, None, lsr))
            link(nc.vector.tensor_copy(blk_b[:, :], scratch))

            def one_hot(r, col):
                return tt(hot[:, r, :, :], under(blk_b[:, ds(col, CHUNK)], NBUK), bucket_no, ALU.is_equal)

            def count(t):
                for r in range(2):
                    need(dve, s_cnt, 6 * t + 3 * r - 3)
                    one_hot(r, 2 * CHUNK * t + CHUNK * r).then_inc(s_hot, 1)
            count(0)
            with dve.Fori(1, NCHUNK // 2) as t:
                count(t)
            link(ts(scratch, src_i[:, :], P - 1, None, ALU.bitwise_and))
            dve.wait_ge(s_dst, 32)
            link(ts(pk_f[:, :], dst_i[:, :], float(PACK), 1.0, ALU.mult, ALU.add))
            tt(pk_f[:, :], pk_f[:, :], scratch, ALU.add).then_inc(s_packed, 1)
            dve.wait_ge(s_packed, 1)

            B = slice(0, NBUK)
            by_chunk = "p (k c) -> p k c"
            dve.wait_ge(s_cntb, 16)
            link(nc.vector.reduce_sum(rows[B, :], cnt[B, :].rearrange(by_chunk, c=CHUNK), AX_X))
            link(ts(n_i[B, 0, :], rows[B, :], float(ROW - 1), None, ALU.add))
            link(ts(n_i[B, 1, :], n_i[B, 0, :], ROW.bit_length() - 1, None, lsr))
            nc.vector.tensor_copy(rows[B, :], n_i[B, 1, :]).then_inc(s_gcount, 1)
            dve.wait_ge(s_gcount, 1)
            link(nc.vector.reduce_sum(bk[B, 0:1], rows[B, :], AX_X))
            link(ts(bk_i[B, 0:1], bk[B, 0:1], float(P - 1), None, ALU.add))
            link(ts(bk_i[B, 1:2], bk_i[B, 0:1], 7, None, lsr))
            nc.vector.tensor_copy(bk[B, 1:2], bk_i[B, 1:2]).then_inc(s_gcount, 1)
            link(nc.vector.memset(off[B, :], 0.0))
            link(nc.vector.tensor_tensor_scan(off[B, :], cnt[B, :], off[B, :], 0.0, ALU.add, ALU.add))
            link(tt(off[B, :], off[B, :], cnt[B, :], ALU.subtract))
            link(nc.vector.memset(delta[B, :], 0.0))
            link(nc.vector.tensor_tensor_scan(before[B, :], rows[B, :], delta[B, :], 0.0, ALU.add, ALU.add))
            link(tt(before[B, :], before[B, :], rows[B, :], ALU.subtract))
            dve.wait_ge(s_base, 1)
            link(nc.vector.tensor_copy(bk[B, 2:3], base_ps))
            link(nc.vector.tensor_copy(first[B, :], first_ps))
            ts(edge[B, :], first[B, :], -1.0, 0.5, ALU.mult, ALU.add).then_inc(s_edge, 1)
            off_k = off[B, :].rearrange(by_chunk, c=CHUNK)
            link(stt(step_d[B, :].unsqueeze(2), first[B, :].unsqueeze(2), float(ROW), off_k[:, :, 0:1],
                     ALU.mult, ALU.subtract))
            tt(off_k, off_k, over(step_d[B, :], CHUNK), ALU.add).then_inc(s_off, 1)
            link(ts(bk[B, 3:4], bk[B, 2:3], float(P), None, ALU.mult))
            link(stt(delta[B, :], before[B, :], bk[B, 3:4], first[B, :], ALU.add, ALU.subtract))
            stt(delta[B, :], delta[B, :], keep[B, :], room[B, :], ALU.mult, ALU.add).then_inc(s_delta, 1)
            ts(ge[0:NBLK, :], iota_g[0:NBLK, :], bk[0:NBLK, 2:3], None, ALU.is_ge).then_inc(s_ge, 1)
            dve.wait_ge(s_offT, 1)
            for k in range(2):
                link(nc.vector.tensor_copy(offc[0:CHUNK, k * SPC * NBUK:(k + 1) * SPC * NBUK],
                                           offT_ps[k][:, 0:SPC * NBUK]))
            part = ranked[:, :, :].rearrange("p k c -> p (k c)")[0:CHUNK, 0:NCHUNK * NBUK].bitcast(i32)
            link(ts(part, offc[0:CHUNK, :], 8, 8, lsr, ALU.logical_shift_left))
            link(nc.vector.tensor_copy(off_parts[0:CHUNK, 0, :], part))
            link(ts(part, offc[0:CHUNK, :], 255, None, ALU.bitwise_and))
            nc.vector.tensor_copy(off_parts[0:CHUNK, 1, :], part).then_inc(s_offc, 1)
            dve.wait_ge(s_off, 1)
            dve.wait_ge(s_step, 1)
            link(nc.vector.tensor_copy(step_d[B, :], step_ps))
            dve.wait_ge(s_gid, 1)
            link(ts(gid[:, :], gid_ps, -1.0, None, ALU.add))
            link(nc.vector.tensor_copy(blkid[:, :], gid[:, :]))

            def sort_chunks(t):
                for r in range(2):
                    ch = 2 * t + r
                    need(dve, s_hotread, ch - 1)
                    need(dve, s_pos, SPC * (ch - 1))
                    one_hot(r, CHUNK * ch).then_inc(s_hot, 1)

                    def pick(m):
                        k, q = (SPC * r + m) % 2, 2 * SPC * t + SPC * r + m
                        dve.wait_ge(s_rank, q + 1)
                        need(dve, s_pos, q - 1)
                        if m == 0:
                            dve.wait_ge(s_hot, NCHUNK + ch + 1)
                        tt(ranked[:, k, :].rearrange("p (b c) -> p b c", c=STEP),
                           rank_ps[k].rearrange("p (b c) -> p b c", c=STEP),
                           hot[:, r, :, m * STEP:(m + 1) * STEP], ALU.mult).then_inc(s_ranked, 1)

                    def total(m):
                        k, q = (SPC * r + m) % 2, 2 * SPC * t + SPC * r + m
                        dve.wait_ge(s_ranked, q + 1)
                        nc.vector.reduce_sum(pos_f[:, m * STEP:(m + 1) * STEP],
                                             ranked[:, k, :].rearrange("p (b c) -> p c b", c=STEP),
                                             AX_X).then_inc(s_pos, 1)

                    pick(0)
                    for m in range(SPC):
                        if m + 1 < SPC:
                            pick(m + 1)
                        total(m)
                    dve.wait_ge(s_pos, 2 * SPC * t + SPC * (r + 1))
                    c4 = 5 * ch
                    nc.vector.tensor_copy(pos[:, :], pos_f[:, :]).then_inc(s_split, 1)
                    dve.wait_ge(s_split, c4 + 1)
                    ts(pos_r[:, :], pos[:, :], ROW.bit_length() - 1, P - 1, lsr, ALU.bitwise_and).then_inc(s_split, 1)
                    ts(pos_g[:, :], pos[:, :], (ROW * P).bit_length() - 1, ROW.bit_length() - 1,
                       lsr, ALU.logical_shift_left).then_inc(s_split, 1)
                    ts(pos_s[:, :], pos[:, :], ROW - 1, None, ALU.bitwise_and).then_inc(s_split, 1)
                    dve.wait_ge(s_split, c4 + 4)
                    nc.vector.tensor_copy(part_f[:, :], pos_r[:, :])
                    tt(place_f[:, :], pos_g[:, :], pos_s[:, :], ALU.add).then_inc(s_split, 1)
                    dve.wait_ge(s_rows, ch + 1)
                    c3 = 3 * ch
                    tt(row_i[:, 0, :], row_ps, rho[:, :], ALU.add).then_inc(s_rowsread, 1)
                    dve.wait_ge(s_rowsread, ch + 1)
                    ts(row_i[:, 1, :], row_i[:, 0, :], P - 1, None, ALU.bitwise_and).then_inc(s_rowi, 1)
                    ts(row_i[:, 2, :], row_i[:, 0, :], 7, None, lsr).then_inc(s_rowi, 1)
                    dve.wait_ge(s_rowi, 2 * ch + 2)
                    dve.wait_ge(s_split, c4 + 5)
                    need(dve, s_scat[r], 16 * CG * t)
                    stt(addr[:, r, :], row_i[:, 1, :], float(ROOM), row_i[:, 2, :],
                        ALU.mult, ALU.add).then_inc(s_addr, 1)
                    with dve.Fori(0, CHUNK // (BATCH * BRING)) as n:
                        for k in range(BRING):
                            q = CHUNK // BATCH * ch + BRING * n + k
                            dve.wait_ge(s_used, q + 1)
                            col = BATCH * BRING * n + BATCH * k
                            tt(to_place[:, k, :, :], over(place_f[:, ds(col, BATCH)], CG * ROW),
                               under(iota[:, 0:CG * ROW], BATCH), ALU.is_equal).then_inc(s_equal, 1)
                            tt(to_part[:, k, :, :], over(part_f[:, ds(col, BATCH)], P),
                               under(iota[:, :], BATCH), ALU.is_equal).then_inc(s_topart, 1)
            sort_chunks(0)
            with dve.Fori(1, NCHUNK // 2) as t:
                sort_chunks(t)

            dve.wait_ge(s_x, 32)
            link(nc.vector.reduce_sum(stat[:, 0, :], x_sb[:, :, :], AX_X))
            link(nc.vector.tensor_scalar(stat[:, 0, :], stat[:, 0, :], 1.0 / D, None, ALU.mult))
            nc.vector.tensor_tensor(h_sb[:, :, :], x_sb[:, :, :], over(stat[:, 0, :], D), ALU.subtract).then_inc(s_xc, 1)
            dve.wait_ge(s_sq, 1)
            link(nc.vector.reduce_sum(stat[:, 1, :], q_sb[:, :, :], AX_X))
            nc.vector.tensor_scalar(stat[:, 1, :], stat[:, 1, :], 1.0 / D, 1e-5, ALU.mult, ALU.add).then_inc(s_var, 1)
            dve.wait_ge(s_std, 1)
            link(nc.vector.reciprocal(stat[:, 3, :], stat[:, 2, :]))
            link(nc.vector.tensor_tensor(h_sb[:, :, :], h_sb[:, :, :], over(stat[:, 3, :], D), ALU.mult))
            nc.vector.tensor_scalar(h_sb[:, :, :], h_sb[:, :, :], 0.0, None, ALU.max).then_inc(s_h, 1)
            for b in range(NBLK):
                dve.wait_ge(s_qkv, b + 1)
                nc.vector.tensor_copy(q_sb[:, b, :], qkv_ps[b % QKV_TILES][:, 0:D]).then_inc(s_q, 1)

            dve.wait_ge(s_back, 16)
            link(nc.vector.tensor_scalar(loc_f[:, :].bitcast(i32), slots[:, :], PACK - 1, None, ALU.bitwise_and))
            link(nc.vector.tensor_scalar(loc_f[:, :], loc_f[:, :].bitcast(i32), -1.0, None, ALU.add))
            link(nc.vector.tensor_scalar(slots[:, :], slots[:, :], PACK.bit_length() - 1, None,
                                         ALU.logical_shift_right))
            dve.wait_ge(s_q, NBLK)


def walk(eng, step, ring, first=-2, drain=4, peel=1):
    whole = (GROUPS - ring) // ring
    for i in range(first, peel * ring):
        step(i, i % ring, i // ring)
    with eng.Fori(peel, whole) as t:
        for u in range(ring):
            step(ring * t + u, u, t)
    for i in range(ring * whole, GROUPS + drain):
        step(i, i % ring, i // ring)


def inside(g):
    return not isinstance(g, int) or 0 <= g < GROUPS


def block_of(eng, blkid, g):
    return eng.value_load(blkid[0:1, ds(g, 1)], min_val=0, max_val=LASTB)


def gather_groups(pool, ring, table, G, idx, s_idx, s_read, s_gat, s_go):
    def step(i, u, t):
        if not inside(i):
            return
        pool.wait_ge(s_idx, i + 1)
        need(pool, s_read, i - ring + 1)
        pool.sem_inc(s_go, 1)
        for j in range(GT):
            pool.indirect_dma_start(out=G[:, u, j, :], out_offset=None, in_=table,
                                    in_offset=bass.IndirectOffsetOnAxis(ap=idx[:, u, j:j + 1], axis=0)
                                    ).then_inc(s_gat[u], 16)
    walk(pool, step, ring, first=0, drain=0)


def layer0_edges(nc, mem, dram):
    with ExitStack() as ctx:
        def sb(name, shape, dt=f32):
            return ctx.enter_context(nc.sbuf_tensor(name, shape, dt))

        def sem(name):
            return ctx.enter_context(nc.semaphore(name))

        iota, ident, q_sb = mem["iota"], mem["ident"], mem["q"]
        slots, loc_f, blkid, acc = mem["slots"], mem["loc"], mem["blkid"], mem["acc"]
        acc = acc[:, 0:NBLK * AW0]
        PS = mem["psum"]
        G = sb("kv_rows", [P, RING0, GT, 2 * D])
        idx = sb("idx_ring", [P, RING0, GT], i32)
        hot = sb("hot0", [P, RING0, GE])
        hotT = sb("hotT0", [P, 2, GE])
        prod = sb("prod0", [P, GE])
        att = sb("att0", [P, 2, GT * HEADS])
        clip = sb("clip0", [P, 2, GT * HEADS])
        vx = sb("vx0", [P, 2, GT, AW0])
        T_ps = [PS[:, 512 * k:512 * k + GE] for k in (0, 1)]
        Q_ps = [PS[:, 512 * k:512 * k + GE] for k in (2, 3)]
        S_ps = [PS[:, 512 * k:512 * k + AW0] for k in (4, 5)]

        s_zero = sem("s_zero0")
        s_idx = sem("s_idx0")
        s_gat = [sem(f"s_gat0_{k}") for k in range(RING0)]
        s_go = sem("s_go0")
        s_hot = sem("s_hot0")
        s_T = sem("s_T0")
        s_hotT = sem("s_hotT0")
        s_q = sem("s_q0")
        s_prod = sem("s_prod0")
        s_red = sem("s_red0")
        s_clip = sem("s_clip0")
        s_ex = sem("s_ex0")
        s_vx = sem("s_vx0")
        s_sum = sem("s_sum0")
        s_acc = sem("s_acc0")
        block = ctx.enter_context(nc.Block())

        @block.gpsimd
        def _(pool):
            gather_groups(pool, RING0, dram["kv"], G, idx, s_idx, s_vx, s_gat, s_go)

        @block.scalar
        def _(act):
            def indices(g, u):
                if inside(g):
                    nc.scalar.copy(idx[:, u, :], slots[:, ds(GT * g, GT)]).then_inc(s_idx, 1)

            for g in range(RING0):
                indices(g, g)

            def step(i, u, t):
                if inside(i + 2):
                    act.wait_ge(s_T, i + 3)
                    need(act, s_q, i + 1)
                    nc.scalar.activation(hotT[:, u % 2, :], T_ps[u % 2], ACT.Copy).then_inc(s_hotT, 1)
                if inside(i):
                    act.wait_ge(s_clip, i + 1)
                    need(act, s_sum, i - 1)
                    nc.scalar.activation(vx[:, u % 2, :, D:AW0],
                                         clip[:, u % 2, :].rearrange("p (j h) -> p j h", h=HEADS),
                                         ACT.Exp).then_inc(s_ex, 1)
                    indices(i + RING0, u)
            walk(act, step, RING0, drain=0)

        @block.tensor
        def _(pe):
            def step(i, u, t):
                if inside(i + 1):
                    blk = block_of(pe, blkid, i + 1)
                    pe.wait_ge(s_hotT, i + 2)
                    need(pe, s_prod, i)
                    for j in range(GT):
                        last = nc.tensor.matmul(Q_ps[(u + 1) % 2][:, j * P:(j + 1) * P],
                                                hotT[:, (u + 1) % 2, j * P:(j + 1) * P],
                                                q_sb[:, ds(blk, 1), :].rearrange("p o f -> p (o f)"),
                                                start=True, stop=True)
                    last.then_inc(s_q, 1)
                if inside(i + 2):
                    pe.wait_ge(s_hot, i + 3)
                    need(pe, s_hotT, i + 1)
                    for j in range(GT):
                        last = nc.tensor.transpose(T_ps[u % 2][:, j * P:(j + 1) * P],
                                                   hot[:, (u + 2) % RING0, j * P:(j + 1) * P], ident[:, :])
                    last.then_inc(s_T, 1)
                if inside(i - 1):
                    pe.wait_ge(s_vx, i)
                    need(pe, s_acc, i - 2)
                    for j in range(GT):
                        last = nc.tensor.matmul(S_ps[(u + 1) % 2], hot[:, (u - 1) % RING0, j * P:(j + 1) * P],
                                                vx[:, (u + 1) % 2, j, :], start=(j == 0), stop=(j == GT - 1))
                    last.then_inc(s_sum, 1)
            walk(pe, step, RING0, drain=1)

        @block.vector
        def _(dve):
            nc.vector.memset(acc[:, :], 0.0).then_inc(s_zero, 1)
            dve.wait_ge(s_zero, 1)

            def step(i, u, t):
                if inside(i + 2):
                    need(dve, s_sum, i + 3 - RING0)
                    nc.vector.tensor_tensor(hot[:, (u + 2) % RING0, :].rearrange("p (j n) -> p j n", n=P),
                                            over(loc_f[:, ds(GT * (i + 2), GT)], P), under(iota[:, :], GT),
                                            ALU.is_equal).then_inc(s_hot, 1)
                if inside(i):
                    dve.wait_ge(s_gat[u], 16 * GT * (t + 1))
                    dve.wait_ge(s_q, i + 1)
                    need(dve, s_red, i)
                    nc.vector.tensor_tensor(prod[:, :].rearrange("p (j f) -> p j f", f=D),
                                            Q_ps[u % 2].rearrange("p (j f) -> p j f", f=D),
                                            G[:, u, :, 0:D], ALU.mult).then_inc(s_prod, 1)
                if inside(i - 2):
                    blk = block_of(dve, blkid, i - 2)
                    dve.wait_ge(s_sum, i - 1)
                    need(dve, s_acc, i - 2)
                    rows = acc[:, ds(blk * AW0, AW0)]
                    nc.vector.tensor_tensor(rows, rows, S_ps[u % 2], ALU.add).then_inc(s_acc, 1)
                if inside(i):
                    dve.wait_ge(s_prod, i + 1)
                    nc.vector.reduce_sum(att[:, u % 2, :],
                                         prod[:, :].rearrange("p (a d) -> p a d", d=HD), AX_X).then_inc(s_red, 1)
                if inside(i - 1):
                    dve.wait_ge(s_ex, i)
                    need(dve, s_sum, i - 2)
                    v = vx[:, (u + 1) % 2, :, :]
                    nc.vector.tensor_tensor(v[:, :, 0:D].rearrange("p j (h d) -> p j h d", d=HD),
                                            G[:, (u - 1) % RING0, :, D:2 * D].rearrange("p j (h d) -> p j h d", d=HD),
                                            v[:, :, D:AW0].unsqueeze(3).broadcast_to((P, GT, HEADS, HD)),
                                            ALU.mult).then_inc(s_vx, 1)
                if inside(i):
                    dve.wait_ge(s_red, i + 1)
                    need(dve, s_ex, i - 1)
                    nc.vector.tensor_scalar(clip[:, u % 2, :], att[:, u % 2, :], -10.0, 10.0,
                                            ALU.max, ALU.min).then_inc(s_clip, 1)
            walk(dve, step, RING0, drain=2)


def between_layers(nc, mem, dram):
    with ExitStack() as ctx:
        def sb(name, shape, dt=f32):
            return ctx.enter_context(nc.sbuf_tensor(name, shape, dt))

        def sem(name):
            return ctx.enter_context(nc.semaphore(name))

        x_sb, q_sb, gb, cb = mem["x"], mem["q"], mem["gb"], mem["cb"]
        h_sb = mem["h"][:, 0:NBLK * D].rearrange("p (t f) -> p t f", f=D)
        acc = mem["acc"][:, 0:NBLK * AW0].rearrange("p (t f) -> p t f", f=AW0)
        table = mem["acc"][:, 0:NBLK * TW].rearrange("p (t f) -> p t f", f=TW)
        sums = mem["h"][:, :].rearrange("p (t f) -> p t f", f=AW1)
        rden = sb("rden", [P, NBLK, HEADS])
        mean = sb("mean", [P, NBLK])
        var = sb("var", [P, NBLK])
        std = sb("std", [P, NBLK])
        rstd = sb("rstd", [P, NBLK])

        s_v = sem("s_v1")
        s_centred = sem("s_centred")
        s_sq = sem("s_sq1")
        s_var = sem("s_var1")
        s_std = sem("s_std1")
        s_tab = sem("s_tab")
        s_h1 = sem("s_h1")
        block = ctx.enter_context(nc.Block())

        @block.sync
        def _(sp):
            sp.wait_ge(s_tab, 1)
            sp.dma_start(dram["h1"].rearrange("(t p) f -> p t f", p=P), table[:, :, :]).then_inc(s_h1, 16)
            sp.wait_ge(s_h1, 16)

        @block.scalar
        def _(act):
            for n, (centred, square) in enumerate(((q_sb, h_sb), (h_sb, q_sb), (table[:, :, 0:D], q_sb))):
                act.wait_ge(s_centred, n + 1)
                nc.scalar.activation(square[:, :, :], centred[:, :, :], ACT.Square).then_inc(s_sq, 1)
                act.wait_ge(s_var, n + 1)
                nc.scalar.activation(std[:, :], var[:, :], ACT.Sqrt).then_inc(s_std, 1)

        @block.vector
        def _(dve):
            link = Chain(dve, s_v)
            tt, ts = nc.vector.tensor_tensor, nc.vector.tensor_scalar

            def normalise(src, centred, squares, n, eps):
                link(nc.vector.reduce_sum(mean[:, :], src, AX_X))
                link(ts(mean[:, :], mean[:, :], 1.0 / D, None, ALU.mult))
                tt(centred[:, :, :], src, over(mean[:, :], D), ALU.subtract).then_inc(s_centred, 1)
                dve.wait_ge(s_sq, n)
                link(nc.vector.reduce_sum(var[:, :], squares[:, :, :], AX_X))
                ts(var[:, :], var[:, :], 1.0 / D, eps, ALU.mult, ALU.add).then_inc(s_var, 1)
                dve.wait_ge(s_std, n)
                link(nc.vector.reciprocal(rstd[:, :], std[:, :]))

            link(ts(rden[:, :, :], acc[:, :, D:AW0], 1e-8, None, ALU.add))
            link(nc.vector.reciprocal(rden[:, :, :], rden[:, :, :]))
            heads = "p t (h d) -> p t h d"
            link(tt(q_sb[:, :, :].rearrange(heads, d=HD), acc[:, :, 0:D].rearrange(heads, d=HD),
                    rden[:, :, :].unsqueeze(3).broadcast_to((P, NBLK, HEADS, HD)), ALU.mult))
            link(tt(q_sb[:, :, :], q_sb[:, :, :], h_sb[:, :, :], ALU.add))
            normalise(q_sb[:, :, :], q_sb, h_sb, 1, 1e-6)
            link(tt(q_sb[:, :, :], q_sb[:, :, :], over(rstd[:, :], D), ALU.mult))
            link(tt(q_sb[:, :, :], q_sb[:, :, :], under(gb[:, 0, :], NBLK), ALU.mult))
            link(tt(q_sb[:, :, :], q_sb[:, :, :], under(gb[:, 1, :], NBLK), ALU.add))
            link(tt(x_sb[:, :, :], x_sb[:, :, :], q_sb[:, :, :], ALU.add))
            normalise(x_sb[:, :, :], h_sb, q_sb, 2, 1e-5)
            link(tt(h_sb[:, :, :], h_sb[:, :, :], over(rstd[:, :], D), ALU.mult))
            nc.vector.memset(table[:, :, D:D + 1], 1.0)
            ts(table[:, :, 0:D], h_sb[:, :, :], 0.0, None, ALU.max).then_inc(s_centred, 1)
            dve.wait_ge(s_sq, 3)
            nc.vector.reduce_sum(var[:, :], q_sb[:, :, :], AX_X).then_inc(s_var, 1)
            dve.wait_ge(s_std, 3)
            link(ts(std[:, :], std[:, :], 1e-30, None, ALU.max))
            link(nc.vector.reciprocal(rstd[:, :], std[:, :]))
            nc.vector.tensor_copy(table[:, :, D + 1:TW], rstd[:, :].unsqueeze(2)).then_inc(s_tab, 1)
            link(ts(mean[:, :], rstd[:, :], cb[:, 0:1], None, ALU.mult))
            link(tt(q_sb[:, :, :], table[:, :, 0:D], over(mean[:, :], D), ALU.mult))
            link(ts(cb[:, 1:2], cb[:, 0:1], -1.0, None, ALU.mult))
            link(tt(cb[:, 2:3], cb[:, 0:1], cb[:, 1:2], ALU.max))
            link(ts(cb[:, 1:2], cb[:, 2:3], 1.01, 1e-3, ALU.mult, ALU.add))
            link(nc.vector.tensor_copy(sums[:, :, :], table[:, :, 0:AW1]))
            link(tt(var[:, :], var[:, :], rstd[:, :], ALU.mult))
            link(tt(var[:, :], var[:, :], mean[:, :], ALU.mult))
            link(ts(mem["top"][:, :], var[:, :], cb[:, 1:2], None, ALU.add))


def layer1_edges(nc, mem, dram):
    with ExitStack() as ctx:
        def sb(name, shape, dt=f32):
            return ctx.enter_context(nc.sbuf_tensor(name, shape, dt))

        def sem(name):
            return ctx.enter_context(nc.semaphore(name))

        iota, ident, q_sb = mem["iota"], mem["ident"], mem["q"]
        slots, loc_f, blkid, cb = mem["slots"], mem["loc"], mem["blkid"], mem["cb"]
        acc = mem["h"]
        PS = mem["psum"]
        G = sb("h_rows", [P, RING1, GT, TW])
        idx = sb("idx_ring1", [P, RING1, GT], i32)
        hot = sb("hot1", [P, RING1, GE])
        hotT = sb("hotT1", [P, RING1, GE])
        prod = sb("prod1", [P, GE])
        dots = sb("dots", [P, GT])
        cosb = sb("cosb", [P, GT])
        logit = sb("logit", [P, RING1, GT])
        hotl = sb("hotl", [P, 2, GE])
        hotw = sb("hotw", [P, 2, GE])
        gmax = sb("gmax", [P, 1])
        top = mem["top"]
        newtop = sb("newtop", [P, RING1])
        fall = sb("fall", [P, 2])
        corr = sb("corr", [P, RING1])
        below = sb("below", [P, 2, GT])
        wgt = sb("wgt", [P, 2, GT])
        T_ps = [PS[:, 512 * k:512 * k + GE] for k in (0, 1)]
        Q_ps = [PS[:, 512 * k:512 * k + GE] for k in (2, 3)]
        S_ps = [PS[:, 512 * k:512 * k + AW1] for k in (4, 5)]
        L_ps = PS[:, 512 * 6:512 * 6 + GE]
        E_ps = PS[:, 512 * 7:512 * 7 + GT]

        s_idx = sem("s_idx1")
        s_gat = [sem(f"s_gat1_{k}") for k in range(RING1)]
        s_go = sem("s_go1")
        s_hot = sem("s_hot1")
        s_T = sem("s_T1")
        s_hotT = sem("s_hotT1")
        s_q = sem("s_q1")
        s_prod = sem("s_prod1")
        s_dots = sem("s_dots")
        s_cosb = sem("s_cosb")
        s_logit = sem("s_logit")
        s_hotl = sem("s_hotl")
        s_L = sem("s_L")
        s_gmax = sem("s_gmax")
        s_newtop = sem("s_newtop")
        s_fall = sem("s_fall")
        s_top = sem("s_top")
        s_corr = sem("s_corr")
        s_E = sem("s_E")
        s_below = sem("s_below")
        s_wgt = sem("s_wgt")
        s_hotw = sem("s_hotw")
        s_sum = sem("s_sum1")
        s_acc = sem("s_acc1")
        block = ctx.enter_context(nc.Block())

        @block.gpsimd
        def _(pool):
            gather_groups(pool, RING1, dram["h1"], G, idx, s_idx, s_sum, s_gat, s_go)

        @block.scalar
        def _(act):
            def indices(g, u):
                if inside(g):
                    nc.scalar.copy(idx[:, u, :], slots[:, ds(GT * g, GT)]).then_inc(s_idx, 1)

            for g in range(RING1):
                indices(g, g)

            def scaled(out, u, scale):
                for j in range(GT):
                    last = nc.scalar.activation(out[:, j * P:(j + 1) * P], hot[:, u, j * P:(j + 1) * P],
                                                ACT.Copy, scale=scale[:, j:j + 1])
                return last

            def step(i, u, t):
                if inside(i - 1):
                    act.wait_ge(s_logit, i)
                    need(act, s_L, i - 2)
                    scaled(hotl[:, (u + 1) % 2, :], (u - 1) % RING1, logit[:, (u - 1) % RING1, :]).then_inc(s_hotl, 1)
                if inside(i + 2):
                    act.wait_ge(s_T, i + 3)
                    need(act, s_E, i + 3 - RING1)
                    nc.scalar.activation(hotT[:, (u + 2) % RING1, :], T_ps[u % 2], ACT.Copy).then_inc(s_hotT, 1)
                if inside(i - 2):
                    act.wait_ge(s_fall, i - 1)
                    need(act, s_acc, i - 1 - RING1)
                    w = (u - 2) % RING1
                    nc.scalar.activation(corr[:, w:w + 1], fall[:, u % 2:u % 2 + 1], ACT.Exp).then_inc(s_corr, 1)
                if inside(i - 3):
                    p = (u + 1) % 2
                    act.wait_ge(s_below, i - 2)
                    nc.scalar.activation(wgt[:, p, :], below[:, p, :], ACT.Exp).then_inc(s_wgt, 1)
                if inside(i):
                    act.wait_ge(s_prod, i + 1)
                    indices(i + RING1, u)
                if inside(i - 3):
                    act.wait_ge(s_wgt, i - 2)
                    need(act, s_sum, i - 4)
                    scaled(hotw[:, p, :], (u - 3) % RING1, wgt[:, p, :]).then_inc(s_hotw, 1)
            walk(act, step, RING1, drain=3, peel=2)

        @block.tensor
        def _(pe):
            def step(i, u, t):
                if inside(i + 1):
                    blk = block_of(pe, blkid, i + 1)
                    pe.wait_ge(s_hotT, i + 2)
                    need(pe, s_prod, i)
                    for j in range(GT):
                        last = nc.tensor.matmul(Q_ps[(u + 1) % 2][:, j * P:(j + 1) * P],
                                                hotT[:, (u + 1) % RING1, j * P:(j + 1) * P],
                                                q_sb[:, ds(blk, 1), :].rearrange("p o f -> p (o f)"),
                                                start=True, stop=True)
                    last.then_inc(s_q, 1)
                if inside(i - 1):
                    pe.wait_ge(s_hotl, i)
                    need(pe, s_gmax, i - 1)
                    for j in range(GT):
                        last = nc.tensor.transpose(L_ps[:, j * P:(j + 1) * P],
                                                   hotl[:, (u + 1) % 2, j * P:(j + 1) * P], ident[:, :])
                    last.then_inc(s_L, 1)
                if inside(i + 2):
                    pe.wait_ge(s_hot, i + 3)
                    need(pe, s_hotT, i + 1)
                    for j in range(GT):
                        last = nc.tensor.transpose(T_ps[u % 2][:, j * P:(j + 1) * P],
                                                   hot[:, (u + 2) % RING1, j * P:(j + 1) * P], ident[:, :])
                    last.then_inc(s_T, 1)
                if inside(i - 2):
                    pe.wait_ge(s_newtop, i - 1)
                    need(pe, s_below, i - 2)
                    for j in range(GT):
                        last = nc.tensor.matmul(E_ps[:, j:j + 1], hotT[:, (u - 2) % RING1, j * P:(j + 1) * P],
                                                newtop[:, (u - 2) % RING1:(u - 2) % RING1 + 1],
                                                start=True, stop=True)
                    last.then_inc(s_E, 1)
                if inside(i - 4):
                    pe.wait_ge(s_hotw, i - 3)
                    need(pe, s_acc, i - 5)
                    for j in range(GT):
                        last = nc.tensor.matmul(S_ps[u % 2], hotw[:, u % 2, j * P:(j + 1) * P],
                                                G[:, (u - 4) % RING1, j, 0:AW1],
                                                start=(j == 0), stop=(j == GT - 1))
                    last.then_inc(s_sum, 1)
            walk(pe, step, RING1, drain=4)

        @block.vector
        def _(dve):
            def step(i, u, t):
                if inside(i - 2):
                    blk = block_of(dve, blkid, i - 2)
                    w = (u - 2) % RING1
                    v = u % 2
                    old, new = top[:, ds(blk, 1)], newtop[:, w:w + 1]
                if inside(i + 2):
                    need(dve, s_hotw, i + 3 - RING1)
                    need(dve, s_T, i + 3 - RING1)
                    nc.vector.tensor_tensor(hot[:, (u + 2) % RING1, :].rearrange("p (j n) -> p j n", n=P),
                                            over(loc_f[:, ds(GT * (i + 2), GT)], P), under(iota[:, :], GT),
                                            ALU.is_equal).then_inc(s_hot, 1)
                if inside(i - 2):
                    dve.wait_ge(s_L, i - 1)
                    nc.vector.reduce_max(gmax[:, :], L_ps, AX_X).then_inc(s_gmax, 1)
                if inside(i):
                    dve.wait_ge(s_gat[u], 16 * GT * (t + 1))
                    dve.wait_ge(s_q, i + 1)
                    need(dve, s_dots, i)
                    nc.vector.tensor_tensor(prod[:, :].rearrange("p (j f) -> p j f", f=D),
                                            Q_ps[u % 2].rearrange("p (j f) -> p j f", f=D),
                                            G[:, u, :, 0:D], ALU.mult).then_inc(s_prod, 1)
                if inside(i - 2):
                    dve.wait_ge(s_gmax, i - 1)
                    need(dve, s_top, i - 2)
                    need(dve, s_E, i - 1 - RING1)
                    nc.vector.tensor_tensor(new, old, gmax[:, :], ALU.max).then_inc(s_newtop, 1)
                if inside(i):
                    dve.wait_ge(s_prod, i + 1)
                    need(dve, s_cosb, i)
                    nc.vector.reduce_sum(dots[:, :], prod[:, :].rearrange("p (j f) -> p j f", f=D),
                                         AX_X).then_inc(s_dots, 1)
                if inside(i - 2):
                    dve.wait_ge(s_newtop, i - 1)
                    need(dve, s_corr, i - 3)
                    nc.vector.tensor_tensor(fall[:, v:v + 1], old, new, ALU.subtract).then_inc(s_fall, 1)
                if inside(i - 3):
                    dve.wait_ge(s_E, i - 2)
                    need(dve, s_wgt, i - 4)
                    nc.vector.tensor_tensor(below[:, (u + 1) % 2, :], logit[:, (u - 3) % RING1, :], E_ps,
                                            ALU.subtract).then_inc(s_below, 1)
                if inside(i - 2):
                    dve.wait_ge(s_fall, i - 1)
                    nc.vector.tensor_tensor(old, old, new, ALU.max).then_inc(s_top, 1)
                if inside(i):
                    dve.wait_ge(s_dots, i + 1)
                    need(dve, s_logit, i)
                    nc.vector.tensor_tensor(cosb[:, :].unsqueeze(2), dots[:, :].unsqueeze(2), G[:, u, :, D + 1:TW],
                                            ALU.mult).then_inc(s_cosb, 1)
                if inside(i - 5):
                    blk5 = block_of(dve, blkid, i - 5)
                    dve.wait_ge(s_sum, i - 4)
                    dve.wait_ge(s_corr, i - 4)
                    need(dve, s_acc, i - 5)
                    rows = acc[:, ds(blk5 * AW1, AW1)]
                    w5 = (u - 5) % RING1
                    nc.vector.scalar_tensor_tensor(rows, rows, corr[:, w5:w5 + 1], S_ps[(u + 1) % 2],
                                                   ALU.mult, ALU.add).then_inc(s_acc, 1)
                if inside(i):
                    dve.wait_ge(s_cosb, i + 1)
                    need(dve, s_hotl, i + 1 - RING1)
                    nc.vector.tensor_scalar(logit[:, u, :], cosb[:, :], cb[:, 1:2], None,
                                            ALU.add).then_inc(s_logit, 1)
            walk(dve, step, RING1, drain=5, peel=2)


def finish(nc, mem, out):
    with ExitStack() as ctx:
        den = ctx.enter_context(nc.sbuf_tensor("den", [P, NBLK], f32))
        s_v = ctx.enter_context(nc.semaphore("s_v2"))
        s_res = ctx.enter_context(nc.semaphore("s_res"))
        s_out = ctx.enter_context(nc.semaphore("s_out"))
        x_sb, q_sb = mem["x"], mem["q"]
        acc = mem["h"][:, :].rearrange("p (t f) -> p t f", f=AW1)
        half = LASTB // 2
        block = ctx.enter_context(nc.Block())

        @block.vector
        def _(dve):
            link = Chain(dve, s_v)
            sums = acc[:, :, D:AW1].rearrange("p t o -> p (t o)")
            link(nc.vector.reciprocal(den[:, :], sums))
            for a, b in ((0, half), (half, NBLK)):
                link(nc.vector.tensor_tensor(q_sb[:, a:b, :], acc[:, a:b, 0:D], over(den[:, a:b], D), ALU.mult))
                nc.vector.tensor_tensor(q_sb[:, a:b, :], q_sb[:, a:b, :], x_sb[:, a:b, :], ALU.add).then_inc(s_res, 1)

        @block.sync
        def _(sp):
            sp.wait_ge(s_res, 1)
            sp.dma_start(out[0:half * P, :].rearrange("(t p) f -> p t f", p=P), q_sb[:, 0:half, :]).then_inc(s_out, 16)
            sp.wait_ge(s_res, 2)
            sp.dma_start(out[half * P:LASTB * P, :].rearrange("(t p) f -> p t f", p=P),
                         q_sb[:, half:LASTB, :]).then_inc(s_out, 16)
            sp.dma_start(out[LASTB * P:N, :], q_sb[0:TAIL, LASTB, :]).then_inc(s_out, 16)
            sp.wait_ge(s_out, 48)


_INS = ["x", "src", "dst", "L0_gnn_Wq", "L0_gnn_Wk", "L0_gnn_Wv", "L0_gnn_gamma", "L0_gnn_beta", "L1_gnn_beta"]


def program(nc, x, src, dst, wq, wk, wv, gamma, beta, cos_beta, out):
    dram = {
        "sorted": nc.dram_tensor("sorted_edges", (P * ROOM, ROW), i32).ap(),
        "counts": nc.dram_tensor("column_counts", (NCHUNK, NBUK * CHUNK), f32).ap(),
        "offs": nc.dram_tensor("column_offsets", (2, COLS, NBUK), bf16).ap(),
        "kv": nc.dram_tensor("kv_table", (NPAD, 2 * D), f32).ap(),
        "h1": nc.dram_tensor("h1_table", (NPAD, TW), f32).ap(),
    }
    with ExitStack() as ctx:
        def sb(name, shape, dt=f32):
            return ctx.enter_context(nc.sbuf_tensor(name, shape, dt))
        mem = {
            "iota": sb("iota", [P, P]),
            "ident": sb("ident", [P, P]),
            "x": sb("x_sb", [P, NBLK, D]),
            "h": sb("h_sb", [P, NBLK * AW1]),
            "q": sb("q_sb", [P, NBLK, D]),
            "slots": sb("slots", [P, NT], i32),
            "loc": sb("loc_f", [P, NT]),
            "blkid": sb("blkid", [1, GROUPS], i32),
            "acc": sb("acc", [P, max(NBLK * AW0, 2 * CHUNK * NBUK)]),
            "gb": sb("gb_sb", [P, 2, D]),
            "cb": sb("cb_sb", [P, 3]),
            "top": sb("top", [P, NBLK]),
            "psum": ctx.enter_context(nc.psum_tensor("psum", [P, 4096], f32)),
        }
        sort_and_project(nc, mem, dram, (src, dst, x, wq, wk, wv, gamma, beta, cos_beta))
        layer0_edges(nc, mem, dram)
        between_layers(nc, mem, dram)
        layer1_edges(nc, mem, dram)
        finish(nc, mem, out)


def kernel(**inputs):
    import numpy as np
    import concourse.bacc as bacc
    from concourse.bass_utils import run_bass_kernel_spmd

    nc = bacc.Bacc("TRN2", target_bir_lowering=False, num_devices=1)
    arrays, args = {}, []
    for name in _INS:
        a = np.ascontiguousarray(inputs[name])
        arrays[f"in_{name}"] = a
        args.append(nc.dram_tensor(f"in_{name}", a.shape, mybir.dt.from_np(a.dtype), kind="ExternalInput").ap())
    args.append(nc.dram_tensor("out_0", (N, D), f32, kind="ExternalOutput").ap())
    program(nc, *args)
    return run_bass_kernel_spmd(nc, [arrays], core_ids=[0]).results[0]["out_0"]
```

```python
import concourse.bass as bass
from concourse import mybir
from contextlib import ExitStack

P = 128
N = 6250
D = 128
HEADS = 8
HD = D // HEADS
E = 206250
NBLK = (N + P - 1) // P
NPAD = NBLK * P
NBUK = NBLK + 1
TAIL = N - (NBLK - 1) * P
LASTB = NBLK - 1

STEP = 10
CHUNK = 90
SPC = CHUNK // STEP
PLACED_AT, FLIP_AT, SIGN_AT, START_AT, STAGE_AT, ROWS_AT, ADDR_AT, HOT_AT, ROWI_AT = 3, 6, 1, 4, 8, 8, 8, 1, 13
CROW = CHUNK * NBUK // 9
NCHUNK = 18
COLS = NCHUNK * CHUNK
LASTROW = E - (P - 1) * COLS
PAD_SRC = P * NBLK
BATCH = 5
BATCHES = CHUNK // BATCH
BRING = 6

GT = 4
GE = GT * P
ROW = GT
CG = (P * CHUNK + NBUK * (ROW - 1) + ROW * P - 1) // (ROW * P)
ALL_ROWS = (E + NCHUNK * NBLK * (ROW - 1)) // ROW
GROUPS = (ALL_ROWS + NBLK * (P - 1)) // P
ROOM = GROUPS + NCHUNK * CG
NT = GT * GROUPS
PACK = 256

RING0 = 6
RING1 = 8
AW0 = D + HEADS
AW1 = D + 1
TW = D + 2
QKV_TILES = 4

f32 = mybir.dt.float32
bf16 = mybir.dt.bfloat16
i32 = mybir.dt.int32
ALU = mybir.AluOpType
ACT = mybir.ActivationFunctionType
AX_X = mybir.AxisListType.X
ds = bass.ds


def need(eng, semaphore, value):
    if isinstance(value, int) and value <= 0:
        return
    eng.wait_ge(semaphore, value)


class Chain:

    def __init__(self, eng, semaphore):
        self.eng, self.semaphore, self.count = eng, semaphore, 0

    def __call__(self, instruction):
        self.count += 1
        instruction.then_inc(self.semaphore, 1)
        self.eng.wait_ge(self.semaphore, self.count)


def over(ap, n):
    return ap.unsqueeze(2).broadcast_to((ap.shape[0], ap.shape[1], n))


def under(ap, n):
    return ap.unsqueeze(1).broadcast_to((ap.shape[0], n, ap.shape[1]))


def sort_and_project(nc, mem, dram, ins):
    src, dst, x, wq, wk, wv, gamma, beta, cos_beta = ins
    with ExitStack() as ctx:
        def sb(name, shape, dt=f32):
            return ctx.enter_context(nc.sbuf_tensor(name, shape, dt))

        def sem(name):
            return ctx.enter_context(nc.semaphore(name))

        iota, ident, x_sb, q_sb = mem["iota"], mem["ident"], mem["x"], mem["q"]
        h_sb = mem["h"][:, 0:NBLK * D].rearrange("p (t f) -> p t f", f=D)
        slots, loc_f, blkid, gb_sb, cb_sb = mem["slots"], mem["loc"], mem["blkid"], mem["gb"], mem["cb"]
        PS = mem["psum"]

        ends = sb("ends", [P, 2 * COLS], i32)
        src_i, dst_i = ends[:, 0:COLS], ends[:, COLS:2 * COLS]
        blk_b = sb("blk_b", [P, COLS], bf16)
        pk_f = sb("pk_f", [P, COLS])
        tri = sb("tri", [P, P])
        tri_b = sb("tri_b", [P, P], bf16)
        bidiag = sb("bidiag", [P, P])
        ones_b = sb("ones_b", [P, 1], bf16)
        ones_2 = sb("ones_2", [2, P], bf16)
        zeros_b = sb("zeros_b", [1, P], bf16)
        iota_g = sb("iota_g", [P, GROUPS])
        rho = sb("rho", [P, CG])
        keep = sb("keep", [P, 1])
        room = sb("room", [P, NCHUNK])
        by_bucket = sb("by_bucket", [P, 2 * COLS])
        cnt = by_bucket[:, 0:COLS]
        off = by_bucket[:, COLS:2 * COLS]
        start = by_bucket[:, 0:CG * P // 2].bitcast(bf16)
        offc = sb("offc", [P, NCHUNK * NBUK], i32)
        cnt_row = mem["acc"][0:1, 0:2 * CHUNK * NBUK].rearrange("p (r c) -> p r c", r=2)
        offrow = mem["acc"][0:2, 0:CHUNK * NBUK].bitcast(bf16).rearrange("p (r c) -> p r c", r=2)
        row_no = mem["h"][:, 0:CG * P]
        free = CG * P
        bucket_no = mem["h"][:, free:free + NBUK * CHUNK // 2].bitcast(bf16).rearrange("p (b c) -> p b c", c=CHUNK)
        free += NBUK * CHUNK // 2
        off_parts = mem["h"][:, free:free + NCHUNK * NBUK].bitcast(bf16).rearrange("p (h k) -> p h k", h=2)
        hot = q_sb.rearrange("p t f -> p (t f)").bitcast(bf16)[:, 0:2 * NBUK * CHUNK].rearrange(
            "p (r b c) -> p r b c", r=2, c=CHUNK)
        ranked = sb("ranked", [P, 2, NBUK * STEP])
        pos_f = sb("pos_f", [P, CHUNK])
        pos = sb("pos", [P, CHUNK], i32)
        pos_r = sb("pos_r", [P, CHUNK], i32)
        pos_g = sb("pos_g", [P, CHUNK], i32)
        pos_s = sb("pos_s", [P, CHUNK], i32)
        part_f = sb("part_f", [P, 2, CHUNK])
        place_b = sb("place_b", [P, 2, CHUNK], bf16)
        place_no = sb("place_no", [P, CG * ROW, BATCH], bf16)
        is_place = sb("is_place", [P, BRING, CG * ROW, BATCH], bf16)
        pk_now = sb("pk_now", [P, 2, CHUNK])
        to_part = sb("to_part", [P, BRING, BATCH, P])
        to_place = ends.bitcast(f32)[:, 0:BRING * BATCH * CG * ROW].rearrange("p (k c n) -> p k c n", k=BRING, c=BATCH)
        row_i = sb("row_i", [P, 3, CG], i32)
        addr = sb("addr", [P, 2, CG], i32)
        placed = sb("placed", [CG * ROW, P])
        stage = sb("stage", [P, 2, CG * ROW], i32)
        bk = sb("bk", [P, 4])
        bk_i = sb("bk_i", [P, 2], i32)
        n_i = sb("n_i", [P, 2, NCHUNK], i32)
        rows = sb("rows", [P, NCHUNK])
        before = sb("before", [P, NCHUNK])
        first = sb("first", [P, NCHUNK])
        edge = sb("edge", [P, NCHUNK])
        delta = sb("delta", [P, NCHUNK])
        step_d = sb("step_d", [P, NCHUNK])
        step_i = sb("step_i", [P, 2, NCHUNK], i32)
        step_b = sb("step_b", [P, NCHUNK, 3], bf16)
        row_f = sb("row_f", [P, CG])
        ge = sb("ge", [P, GROUPS], bf16)
        gid = sb("gid", [1, GROUPS])
        w_sb = sb("w_sb", [P, 3 * D])
        stat = sb("stat", [P, 4, NBLK])
        hT = by_bucket[:, 0:QKV_TILES * P]
        kv = by_bucket[:, QKV_TILES * P:3 * QKV_TILES * P].rearrange("p (k f) -> p k f", f=2 * D)

        cnt_ps = [PS[0:1, 1536 * k:1536 * k + 1536].rearrange("p (i c) -> p i c", c=512)[:, :, 0:CROW]
                  for k in range(2)]
        rank_ps = [PS[:, 2048 + 512 * k:2048 + 512 * k + NBUK * STEP] for k in range(2)]
        place_ps = [PS[0:CG * ROW, 512 * k:512 * k + P] for k in range(2)]
        flip_ps = PS[:, 1536:1536 + CG * ROW]
        row_ps = PS[:, 1024:1024 + 3 * CG]
        base_ps = PS[0:NBUK, 3072:3073]
        first_ps = PS[0:NBUK, 3074:3074 + NCHUNK]
        step_ps = PS[0:NBUK, 3104:3104 + NCHUNK]
        gid_ps = PS[0:1, 3584:3584 + GROUPS]
        offT_ps = [PS[0:CHUNK, 512 * k:512 * k + 512] for k in range(2)]
        hT_ps = PS[:, 3072:3584]
        qkv_ps = [PS[:, 512 * k:512 * k + 3 * D] for k in range(QKV_TILES)]

        s_const = sem("s_const")
        s_pool = sem("s_pool")
        s_pads = sem("s_pads")
        s_src, s_dst, s_x, s_w, s_gb = (sem(n) for n in ("s_src", "s_dst", "s_x", "s_w", "s_gb"))
        s_filled = sem("s_filled")
        s_v = sem("s_v")
        s_prep = sem("s_prep")
        s_hot = sem("s_hot")
        s_hotread = sem("s_hotread")
        s_cnt = sem("s_cnt")
        s_cntrow = sem("s_cntrow")
        s_cntd = [sem("s_cntd0"), sem("s_cntd1")]
        s_cntb = sem("s_cntb")
        s_packed = sem("s_packed")
        s_edge = sem("s_edge")
        s_sign = sem("s_sign")
        s_pknow = sem("s_pknow")
        s_equal = sem("s_equal")
        s_gcount = sem("s_gcount")
        s_base = sem("s_base")
        s_delta = sem("s_delta")
        s_step = sem("s_step")
        s_stepb = sem("s_stepb")
        s_ge = sem("s_ge")
        s_gid = sem("s_gid")
        s_off = sem("s_off")
        s_offT = sem("s_offT")
        s_offc = sem("s_offc")
        s_offd = sem("s_offd")
        s_row = [sem("s_row0"), sem("s_row1")]
        s_rank = sem("s_rank")
        s_ranked = sem("s_ranked")
        s_pos = sem("s_pos")
        s_split = sem("s_split")
        s_rowi = sem("s_rowi")
        s_start = sem("s_start")
        s_rows = sem("s_rows")
        s_rowsread = sem("s_rowsread")
        s_addr = sem("s_addr")
        s_topart = sem("s_topart")
        s_onehot = sem("s_onehot")
        s_used = sem("s_used")
        s_placed = sem("s_placed")
        s_out = sem("s_out")
        s_flip = sem("s_flip")
        s_stage = sem("s_stage")
        s_scat = [sem("s_scat0"), sem("s_scat1")]
        s_go = sem("s_go")
        s_sorted = sem("s_sorted")
        s_back = sem("s_back")
        s_xc = sem("s_xc")
        s_sq = sem("s_sq")
        s_var = sem("s_var")
        s_std = sem("s_std")
        s_h = sem("s_h")
        s_hT = sem("s_hT")
        s_hTc = sem("s_hTc")
        s_qkv = sem("s_qkv")
        s_q = sem("s_q")
        s_kv = sem("s_kv")
        s_kvd = sem("s_kvd")

        slots_d = dram["sorted"].rearrange("(p g) j -> p (g j)", p=P)[:, 0:NT]
        block = ctx.enter_context(nc.Block())

        def every_chunk(eng, chunk):
            turns = NCHUNK // 2
            for r in range(2):
                chunk(0, r)
            with eng.Fori(1, turns - 1) as t:
                for r in range(2):
                    chunk(t, r)
            for r in range(2):
                chunk(turns - 1, r)

        def after(t, r, n):
            t, r = (t + (r + n) // 2 if r + n >= 2 else t), (r + n) % 2
            return None if isinstance(t, int) and t >= NCHUNK // 2 else (t, r)

        @block.sync
        def _(sp):
            sp.wait_ge(s_pads, 3)
            for tile, edges, done in ((src_i, src, s_src), (dst_i, dst, s_dst)):
                sp.dma_start(tile[0:P - 1, :], edges[0:(P - 1) * COLS].rearrange("(p c) -> p c", c=COLS)).then_inc(done, 16)
                sp.dma_start(tile[P - 1:P, 0:LASTROW],
                             edges[(P - 1) * COLS:E].rearrange("(p c) -> p c", p=1)).then_inc(done, 16)
            sp.wait_ge(s_pads, 4)
            sp.dma_start(slots_d, slots[:, :]).then_inc(s_filled, 16)
            sp.dma_start(x_sb[:, 0:LASTB, :], x[0:LASTB * P, :].rearrange("(t p) f -> p t f", p=P)).then_inc(s_x, 16)
            sp.dma_start(x_sb[0:TAIL, LASTB, :], x[LASTB * P:N, :]).then_inc(s_x, 16)
            for k, w in enumerate((wq, wk, wv)):
                sp.dma_start(w_sb[:, k * D:(k + 1) * D], w).then_inc(s_w, 16)
            for k, w in enumerate((gamma, beta)):
                sp.dma_start(gb_sb[:, k, :], w.rearrange("(o f) -> o f", o=1).broadcast_to((P, D))).then_inc(s_gb, 16)
            sp.dma_start(cb_sb[:, 0:1], cos_beta.rearrange("(o f) -> o f", o=1).broadcast_to((P, 1))).then_inc(s_gb, 16)
            with sp.Fori(0, NCHUNK // 2) as t:
                for r in range(2):
                    sp.wait_ge(s_cntrow, 6 * t + 3 * r + 3)
                    sp.dma_start(dram["counts"][ds(2 * t + r, 1), :], cnt_row[:, r, :]).then_inc(s_cntd[r], 16)
            for r in range(2):
                sp.wait_ge(s_cntd[r], 16 * (NCHUNK // 2))
            sp.dma_start(cnt[0:NBUK, :].rearrange("b (k c) -> b k c", c=CHUNK),
                         dram["counts"].rearrange("k (b c) -> b k c", c=CHUNK)).then_inc(s_cntb, 16)
            sp.wait_ge(s_offc, 1)
            for part in range(2):
                sp.dma_start(dram["offs"][part].rearrange("(k c) b -> c k b", c=CHUNK),
                             off_parts[0:CHUNK, part, :].rearrange("c (k b) -> c k b", b=NBUK)).then_inc(s_offd, 16)
            sp.wait_ge(s_offd, 32)
            offs = dram["offs"].rearrange("h (k c) b -> h k (c b)", c=CHUNK)
            for r in range(2):
                sp.dma_start(offrow[:, r:r + 1, :], offs[:, r:r + 1, :]).then_inc(s_row[r], 16)
            with sp.Fori(1, NCHUNK // 2) as t:
                for r in range(2):
                    sp.wait_ge(s_rank, 2 * SPC * t - SPC * (1 - r))
                    sp.dma_start(offrow[:, r:r + 1, :], offs[:, ds(2 * t + r, 1), :]).then_inc(s_row[r], 16)
            for b in range(0, NBLK, QKV_TILES):
                n = min(QKV_TILES, NBLK - b)
                sp.wait_ge(s_kv, b + n)
                sp.dma_start(dram["kv"][b * P:(b + n) * P, :].rearrange("(t p) f -> p t f", p=P),
                             kv[:, 0:n, :]).then_inc(s_kvd, 16)
            sp.wait_ge(s_sorted, 1)
            sp.dma_start(slots[:, :], slots_d).then_inc(s_back, 16)
            sp.wait_ge(s_kvd, 16 * ((NBLK + QKV_TILES - 1) // QKV_TILES))
            sp.wait_ge(s_gb, 48)
            sp.wait_ge(s_filled, 16)

        @block.gpsimd
        def _(pool):
            nc.gpsimd.iota(iota[:, :], [[1, P]], base=0, channel_multiplier=0,
                           allow_small_or_imprecise_dtypes=True).then_inc(s_const, 1)
            nc.gpsimd.iota(iota_g[:, :], [[1, GROUPS]], base=0, channel_multiplier=0,
                           allow_small_or_imprecise_dtypes=True).then_inc(s_const, 1)
            nc.gpsimd.memset(ident[:, :], 0.0).then_inc(s_pool, 1)
            nc.gpsimd.memset(tri[:, :], 1.0).then_inc(s_pool, 1)
            nc.gpsimd.iota(bucket_no, [[1, NBUK], [0, CHUNK]], base=0, channel_multiplier=0,
                           allow_small_or_imprecise_dtypes=True).then_inc(s_const, 1)
            nc.gpsimd.iota(row_no, [[1, CG * P]], base=0, channel_multiplier=0,
                           allow_small_or_imprecise_dtypes=True).then_inc(s_const, 1)
            nc.gpsimd.memset(bidiag[:, :], 0.0).then_inc(s_pool, 1)
            nc.gpsimd.memset(keep[:, :], 1.0).then_inc(s_pool, 1)
            nc.gpsimd.iota(rho[:, :], [[P, CG]], base=0, channel_multiplier=1,
                           allow_small_or_imprecise_dtypes=True).then_inc(s_const, 1)
            nc.gpsimd.iota(room[:, :], [[CG * P, NCHUNK]], base=GROUPS * P, channel_multiplier=0,
                           allow_small_or_imprecise_dtypes=True).then_inc(s_pool, 1)
            pool.wait_ge(s_pool, 5)
            nc.gpsimd.affine_select(out=ident[:, :], in_=ident[:, :], compare_op=ALU.not_equal, fill=1.0,
                                    base=0, pattern=[[-1, P]], channel_multiplier=1).then_inc(s_const, 1)
            nc.gpsimd.affine_select(out=tri[:, :], in_=tri[:, :], compare_op=ALU.is_gt, fill=0.0,
                                    base=0, pattern=[[1, P]], channel_multiplier=-1).then_inc(s_const, 1)
            nc.gpsimd.affine_select(out=keep[:, :], in_=keep[:, :], compare_op=ALU.not_equal, fill=0.0,
                                    base=-NBLK, pattern=[[0, 1]], channel_multiplier=1).then_inc(s_const, 1)
            nc.gpsimd.affine_select(out=room[:, :], in_=room[:, :], compare_op=ALU.is_equal, fill=0.0,
                                    base=-NBLK, pattern=[[0, NCHUNK]], channel_multiplier=1).then_inc(s_const, 1)
            nc.gpsimd.affine_select(out=bidiag[:, :], in_=bidiag[:, :], compare_op=ALU.not_equal, fill=1.0,
                                    base=0, pattern=[[-1, P]], channel_multiplier=1).then_inc(s_pool, 1)
            pool.wait_ge(s_pool, 6)
            nc.gpsimd.affine_select(out=bidiag[:, :], in_=bidiag[:, :], compare_op=ALU.not_equal, fill=-1.0,
                                    base=1, pattern=[[-1, P]], channel_multiplier=1).then_inc(s_const, 1)
            pool.wait_ge(s_filled, 16)
            with pool.Fori(0, NCHUNK // 2) as t:
                for r in range(2):
                    pool.wait_ge(s_addr, 2 * t + r + 1)
                    pool.wait_ge(s_stage, 2 * t + r + 1)
                    pool.sem_inc(s_go, 1)
                    for g in range(CG):
                        pool.indirect_dma_start(
                            out=dram["sorted"], out_offset=bass.IndirectOffsetOnAxis(ap=addr[:, r, g:g + 1], axis=0),
                            in_=stage[:, r, g * ROW:(g + 1) * ROW], in_offset=None).then_inc(s_scat[r], 16)
            for r in range(2):
                pool.wait_ge(s_scat[r], 16 * CG * (NCHUNK // 2))
            pool.sem_inc(s_sorted, 1)

        @block.tensor
        def _(pe):
            pe.wait_ge(s_const, 10)
            pe.wait_ge(s_prep, 4)
            pe.sem_inc(s_used, BRING)
            def count(t):
                for r in range(2):
                    pe.wait_ge(s_hot, 2 * t + r + 1)
                    for m in range(3):
                        k = (3 * r + m) % 2
                        need(pe, s_cntrow, 6 * t + 3 * r + m - 1)
                        flat = hot[:, r, :, :].rearrange("p b c -> p (b c)")
                        for i in range(3):
                            last = nc.tensor.matmul(cnt_ps[k][:, i, :], ones_b[:, :],
                                                    flat[:, (3 * m + i) * CROW:(3 * m + i + 1) * CROW],
                                                    start=True, stop=True)
                        last.then_inc(s_cnt, 1)
            count(0)
            with pe.Fori(1, NCHUNK // 2) as t:
                count(t)
            pe.wait_ge(s_gcount, 2)
            nc.tensor.matmul(base_ps, tri[0:NBUK, 0:NBUK], bk[0:NBUK, 1:2], start=True, stop=True)
            nc.tensor.matmul(first_ps, tri[0:NBUK, 0:NBUK], rows[0:NBUK, :], start=True, stop=True).then_inc(s_base, 1)
            pe.wait_ge(s_off, 1)
            for k in range(NCHUNK):
                last = nc.tensor.transpose(offT_ps[k // SPC][:, (k % SPC) * NBUK:(k % SPC + 1) * NBUK],
                                           off[0:NBUK, k * CHUNK:(k + 1) * CHUNK], ident[0:NBUK, 0:NBUK])
            last.then_inc(s_offT, 1)
            pe.wait_ge(s_delta, 1)
            nc.tensor.matmul(step_ps, bidiag[0:NBUK, 0:NBUK], delta[0:NBUK, :], start=True, stop=True).then_inc(s_step, 1)
            pe.wait_ge(s_ge, 1)
            nc.tensor.matmul(gid_ps, ones_b[0:NBLK, :], ge[0:NBLK, :], start=True, stop=True).then_inc(s_gid, 1)
            pe.wait_ge(s_offc, 1)

            def rank(t, r, m):
                ch, k = 2 * t + r, (SPC * r + m) % 2
                if m == 0:
                    pe.wait_ge(s_hot, NCHUNK + ch + 1)
                need(pe, s_ranked, SPC * ch + m - 1)
                ranks = nc.tensor.matmul(rank_ps[k], tri_b[:, :], hot[:, r, :, m * STEP:(m + 1) * STEP],
                                         start=True, stop=False)
                if m == SPC - 1:
                    ranks.then_inc(s_hotread, 1)
                if m == 0:
                    pe.wait_ge(s_row[r], 16 * t + 16)
                o = offrow[:, r, m * STEP * NBUK:(m + 1) * STEP * NBUK]
                nc.tensor.matmul(rank_ps[k], ones_2[:, :], o.rearrange("p (c b) -> p b c", b=NBUK),
                                 start=False, stop=True).then_inc(s_rank, 1)

            def rows_of(t, r):
                ch = 2 * t + r
                pe.wait_ge(s_start, ch + 1)
                pe.wait_ge(s_stepb, 1)
                need(pe, s_rowsread, ch)
                for g in range(CG):
                    last = nc.tensor.matmul(row_ps[:, 3 * g:3 * g + 3], start[0:NBUK, g * P:(g + 1) * P],
                                            step_b[0:NBUK, ds(ch, 1), :].rearrange("p o k -> p (o k)"),
                                            start=True, stop=True)
                last.then_inc(s_rows, 1)

            def flip(ch):
                pe.wait_ge(s_out, ch + 1)
                need(pe, s_stage, ch)
                nc.tensor.transpose(flip_ps, placed[:, :], ident[0:CG * ROW, 0:CG * ROW]).then_inc(s_flip, 1)

            def chunk(t, r):
                ch, following = 2 * t + r, after(t, r, 1)
                need(pe, s_out, ch - 1)
                nc.tensor.matmul(place_ps[r], zeros_b[:, 0:CG * ROW], zeros_b[:, :], start=True, stop=False)
                for b in range(BATCHES):
                    k, q = b % BRING, BATCHES * ch + b
                    if following and b % 2 == 0:
                        rank(*following, b // 2)
                    pe.wait_ge(s_topart, q + 1)
                    pe.wait_ge(s_onehot, q + 1)
                    for c in range(BATCH):
                        last = nc.tensor.matmul(place_ps[r], to_place[:, k, c, :], to_part[:, k, c, :],
                                                start=False, stop=False)
                    last.then_inc(s_used, 1)
                    if b == FLIP_AT and not (isinstance(ch, int) and ch == 0):
                        flip(ch - 1)
                    if following and b == ROWS_AT:
                        rows_of(*following)
                nc.tensor.matmul(place_ps[r], zeros_b[:, 0:CG * ROW], zeros_b[:, :],
                                 start=False, stop=True).then_inc(s_placed, 1)
            for m in range(SPC):
                rank(0, 0, m)
            rows_of(0, 0)
            every_chunk(pe, chunk)
            flip(NCHUNK - 1)
            pe.wait_ge(s_stage, NCHUNK)
            pe.wait_ge(s_rowsread, NCHUNK)
            pe.wait_ge(s_w, 48)
            pe.wait_ge(s_h, 1)
            for i, b in enumerate(range(0, NBLK, QKV_TILES)):
                n = min(QKV_TILES, NBLK - b)
                need(pe, s_hTc, i)
                for k in range(n):
                    last = nc.tensor.transpose(hT_ps[:, k * P:(k + 1) * P], h_sb[:, b + k, :], ident[:, :])
                last.then_inc(s_hT, 1)
                pe.wait_ge(s_hTc, i + 1)
                for k in range(n):
                    need(pe, s_q, b + k + 1 - QKV_TILES)
                    need(pe, s_kv, b + k + 1 - QKV_TILES)
                    nc.tensor.matmul(qkv_ps[k], hT[:, k * P:(k + 1) * P], w_sb[:, :],
                                     start=True, stop=True).then_inc(s_qkv, 1)

        @block.scalar
        def _(act):
            def counts(t):
                for r in range(2):
                    need(act, s_cntd[r], 16 * t)
                    for m in range(3):
                        act.wait_ge(s_cnt, 6 * t + 3 * r + m + 1)
                        nc.scalar.activation(
                            cnt_row[:, r, 3 * m * CROW:3 * (m + 1) * CROW].rearrange("p (i c) -> p i c", c=CROW),
                            cnt_ps[(3 * r + m) % 2], ACT.Copy).then_inc(s_cntrow, 1)
            counts(0)
            with act.Fori(1, NCHUNK // 2) as t:
                counts(t)
            act.wait_ge(s_packed, 1)
            act.wait_ge(s_offT, 1)
            act.wait_ge(s_edge, 1)

            def sign_of(t, r):
                nc.scalar.activation(pk_now[:, r, :], pk_f[:, ds(CHUNK * (2 * t + r), CHUNK)],
                                     ACT.Copy).then_inc(s_pknow, 1)
                nc.scalar.activation(start[0:NBUK, :], row_no[0:NBUK, :], ACT.Sign,
                                     bias=edge[0:NBUK, ds(2 * t + r, 1)]).then_inc(s_sign, 1)

            def start_of(t, r):
                act.wait_ge(s_sign, 2 * t + r + 1)
                nc.scalar.activation(start[0:NBUK, :], start[0:NBUK, :], ACT.Relu).then_inc(s_start, 1)

            def placed_out(ch, r):
                act.wait_ge(s_placed, ch + 1)
                need(act, s_flip, ch)
                nc.scalar.activation(placed[:, :], place_ps[r], ACT.Copy).then_inc(s_out, 1)

            def stage_rows(t, r):
                act.wait_ge(s_flip, 2 * t + r + 1)
                need(act, s_scat[r], 16 * CG * t)
                nc.scalar.copy(stage[:, r, :], flip_ps).then_inc(s_stage, 1)

            def chunk(t, r):
                ch, following = 2 * t + r, after(t, r, 1)
                act.wait_ge(s_pknow, ch + 1)
                for b in range(BATCHES):
                    k, q = b % BRING, BATCHES * ch + b
                    act.wait_ge(s_equal, q + 1)
                    for c in range(BATCH):
                        last = nc.scalar.activation(to_place[:, k, c, :], is_place[:, k, :, c], ACT.Copy,
                                                    scale=pk_now[:, r, BATCH * b + c:BATCH * b + c + 1])
                    last.then_inc(s_onehot, 1)
                    if b == PLACED_AT and not (isinstance(ch, int) and ch == 0):
                        placed_out(ch - 1, 1 - r)
                    if b == STAGE_AT and r == 1:
                        stage_rows(t, 0)
                    elif b == STAGE_AT and not (isinstance(t, int) and t == 0):
                        stage_rows(t - 1, 1)
                    if following and b == SIGN_AT:
                        act.wait_ge(s_rows, ch + 1)
                        need(act, s_onehot, BATCHES * ch)
                        sign_of(*following)
                    if following and b == START_AT:
                        start_of(*following)
            sign_of(0, 0)
            start_of(0, 0)
            every_chunk(act, chunk)
            placed_out(NCHUNK - 1, 1)
            stage_rows(NCHUNK // 2 - 1, 1)
            act.wait_ge(s_xc, 1)
            nc.scalar.activation(q_sb[:, :, :], h_sb[:, :, :], ACT.Square).then_inc(s_sq, 1)
            act.wait_ge(s_var, 1)
            nc.scalar.activation(stat[:, 2, :], stat[:, 1, :], ACT.Sqrt).then_inc(s_std, 1)
            for i, b in enumerate(range(0, NBLK, QKV_TILES)):
                n = min(QKV_TILES, NBLK - b)
                act.wait_ge(s_hT, i + 1)
                need(act, s_qkv, b)
                nc.scalar.activation(hT[:, 0:n * P], hT_ps[:, 0:n * P], ACT.Copy).then_inc(s_hTc, 1)
                need(act, s_kvd, 16 * i)
                for k in range(n):
                    act.wait_ge(s_q, b + k + 1)
                    nc.scalar.activation(kv[:, k, :], qkv_ps[k][:, D:3 * D], ACT.Copy).then_inc(s_kv, 1)

        @block.vector
        def _(dve):
            nc.vector.memset(src_i[96:P, LASTROW:COLS], PAD_SRC).then_inc(s_pads, 1)
            nc.vector.memset(dst_i[96:P, LASTROW:COLS], 0).then_inc(s_pads, 1)
            nc.vector.memset(x_sb[:, LASTB, :], 0.0).then_inc(s_pads, 1)
            nc.vector.memset(slots[:, :], 0).then_inc(s_pads, 1)
            nc.vector.memset(ones_b[:, :], 1.0).then_inc(s_prep, 1)
            nc.vector.memset(zeros_b[:, :], 0.0).then_inc(s_prep, 1)
            nc.vector.memset(ones_2[:, :], 1.0).then_inc(s_prep, 1)
            dve.wait_ge(s_const, 10)
            nc.vector.tensor_copy(tri_b[:, :], tri[:, :]).then_inc(s_prep, 1)
            link = Chain(dve, s_v)
            link(nc.vector.tensor_copy(place_no[:, :, :], over(iota[:, 0:CG * ROW], BATCH)))
            tt, ts, stt = nc.vector.tensor_tensor, nc.vector.tensor_scalar, nc.vector.scalar_tensor_tensor
            lsr = ALU.logical_shift_right
            scratch = off[:, :].bitcast(i32)
            dve.wait_ge(s_src, 32)
            link(ts(scratch, src_i[:, :], 7, None, lsr))
            link(nc.vector.tensor_copy(blk_b[:, :], scratch))

            def one_hot(r, col):
                return tt(hot[:, r, :, :], under(blk_b[:, ds(col, CHUNK)], NBUK), bucket_no, ALU.is_equal)

            def count(t):
                for r in range(2):
                    need(dve, s_cnt, 6 * t + 3 * r - 3)
                    one_hot(r, 2 * CHUNK * t + CHUNK * r).then_inc(s_hot, 1)
            count(0)
            with dve.Fori(1, NCHUNK // 2) as t:
                count(t)
            link(ts(scratch, src_i[:, :], P - 1, None, ALU.bitwise_and))
            dve.wait_ge(s_dst, 32)
            link(ts(pk_f[:, :], dst_i[:, :], float(PACK), 1.0, ALU.mult, ALU.add))
            tt(pk_f[:, :], pk_f[:, :], scratch, ALU.add).then_inc(s_packed, 1)
            dve.wait_ge(s_packed, 1)

            B = slice(0, NBUK)
            by_chunk = "p (k c) -> p k c"
            dve.wait_ge(s_cntb, 16)
            link(nc.vector.reduce_sum(rows[B, :], cnt[B, :].rearrange(by_chunk, c=CHUNK), AX_X))
            link(ts(n_i[B, 0, :], rows[B, :], float(ROW - 1), None, ALU.add))
            link(ts(n_i[B, 1, :], n_i[B, 0, :], ROW.bit_length() - 1, None, lsr))
            nc.vector.tensor_copy(rows[B, :], n_i[B, 1, :]).then_inc(s_gcount, 1)
            dve.wait_ge(s_gcount, 1)
            link(nc.vector.reduce_sum(bk[B, 0:1], rows[B, :], AX_X))
            link(ts(bk_i[B, 0:1], bk[B, 0:1], float(P - 1), None, ALU.add))
            link(ts(bk_i[B, 1:2], bk_i[B, 0:1], 7, None, lsr))
            nc.vector.tensor_copy(bk[B, 1:2], bk_i[B, 1:2]).then_inc(s_gcount, 1)
            link(nc.vector.memset(off[B, :], 0.0))
            link(nc.vector.tensor_tensor_scan(off[B, :], cnt[B, :], off[B, :], 0.0, ALU.add, ALU.add))
            link(tt(off[B, :], off[B, :], cnt[B, :], ALU.subtract))
            link(nc.vector.memset(delta[B, :], 0.0))
            link(nc.vector.tensor_tensor_scan(before[B, :], rows[B, :], delta[B, :], 0.0, ALU.add, ALU.add))
            link(tt(before[B, :], before[B, :], rows[B, :], ALU.subtract))
            dve.wait_ge(s_base, 1)
            link(nc.vector.tensor_copy(bk[B, 2:3], base_ps))
            link(nc.vector.tensor_copy(first[B, :], first_ps))
            ts(edge[B, :], first[B, :], -1.0, 0.5, ALU.mult, ALU.add).then_inc(s_edge, 1)
            off_k = off[B, :].rearrange(by_chunk, c=CHUNK)
            link(stt(step_d[B, :].unsqueeze(2), first[B, :].unsqueeze(2), float(ROW), off_k[:, :, 0:1],
                     ALU.mult, ALU.subtract))
            tt(off_k, off_k, over(step_d[B, :], CHUNK), ALU.add).then_inc(s_off, 1)
            link(ts(bk[B, 3:4], bk[B, 2:3], float(P), None, ALU.mult))
            link(stt(delta[B, :], before[B, :], bk[B, 3:4], first[B, :], ALU.add, ALU.subtract))
            stt(delta[B, :], delta[B, :], keep[B, :], room[B, :], ALU.mult, ALU.add).then_inc(s_delta, 1)
            ts(ge[0:NBLK, :], iota_g[0:NBLK, :], bk[0:NBLK, 2:3], None, ALU.is_ge).then_inc(s_ge, 1)
            dve.wait_ge(s_offT, 1)
            for k in range(2):
                link(nc.vector.tensor_copy(offc[0:CHUNK, k * SPC * NBUK:(k + 1) * SPC * NBUK],
                                           offT_ps[k][:, 0:SPC * NBUK]))
            part = ranked[:, :, :].rearrange("p k c -> p (k c)")[0:CHUNK, 0:NCHUNK * NBUK].bitcast(i32)
            link(ts(part, offc[0:CHUNK, :], 8, 8, lsr, ALU.logical_shift_left))
            link(nc.vector.tensor_copy(off_parts[0:CHUNK, 0, :], part))
            link(ts(part, offc[0:CHUNK, :], 255, None, ALU.bitwise_and))
            nc.vector.tensor_copy(off_parts[0:CHUNK, 1, :], part).then_inc(s_offc, 1)
            dve.wait_ge(s_off, 1)
            dve.wait_ge(s_step, 1)
            link(nc.vector.tensor_copy(step_i[B, 0, :], step_ps))
            for k, shifts in enumerate((16, 8, 0)):
                if k < 2:
                    asr = ALU.arith_shift_right
                    link(ts(step_i[B, 1, :], step_i[B, 0, :], shifts, None, asr))
                    link(ts(step_i[B, 1, :], step_i[B, 1, :], shifts, None, ALU.logical_shift_left))
                    link(nc.vector.tensor_copy(step_b[B, :, k:k + 1], step_i[B, 1, :].unsqueeze(2)))
                    link(tt(step_i[B, 0, :], step_i[B, 0, :], step_i[B, 1, :], ALU.subtract))
                else:
                    nc.vector.tensor_copy(step_b[B, :, k:k + 1], step_i[B, 0, :].unsqueeze(2)).then_inc(s_stepb, 1)
            dve.wait_ge(s_stepb, 1)
            dve.wait_ge(s_gid, 1)
            link(ts(gid[:, :], gid_ps, -1.0, None, ALU.add))
            link(nc.vector.tensor_copy(blkid[:, :], gid[:, :]))

            def hot_of(t, r):
                need(dve, s_hotread, 2 * t + r - 1)
                need(dve, s_ranked, SPC * (2 * t + r - 1))
                one_hot(r, CHUNK * (2 * t + r)).then_inc(s_hot, 1)

            def pick(t, r, m):
                k, q = (SPC * r + m) % 2, SPC * (2 * t + r) + m
                dve.wait_ge(s_rank, q + 1)
                need(dve, s_pos, q - 1)
                if m == 0:
                    dve.wait_ge(s_hot, NCHUNK + 2 * t + r + 1)
                tt(ranked[:, k, :].rearrange("p (b c) -> p b c", c=STEP),
                   rank_ps[k].rearrange("p (b c) -> p b c", c=STEP),
                   hot[:, r, :, m * STEP:(m + 1) * STEP], ALU.mult).then_inc(s_ranked, 1)

            def total(t, r, m):
                k, q = (SPC * r + m) % 2, SPC * (2 * t + r) + m
                dve.wait_ge(s_ranked, q + 1)
                nc.vector.reduce_sum(pos_f[:, m * STEP:(m + 1) * STEP],
                                     ranked[:, k, :].rearrange("p (b c) -> p c b", c=STEP),
                                     AX_X).then_inc(s_pos, 1)

            def row_numbers(t, r):
                dve.wait_ge(s_rows, 2 * t + r + 1)
                nc.vector.reduce_sum(row_f[:, :], row_ps.rearrange("p (g k) -> p g k", k=3), AX_X).then_inc(s_rowsread, 1)

            def split(t, r):
                ch = 2 * t + r
                n = 6 * ch
                dve.wait_ge(s_pos, SPC * (ch + 1))
                nc.vector.tensor_copy(pos[:, :], pos_f[:, :]).then_inc(s_split, 1)
                dve.wait_ge(s_split, n + 1)
                ts(pos_r[:, :], pos[:, :], ROW.bit_length() - 1, P - 1, lsr, ALU.bitwise_and).then_inc(s_split, 1)
                ts(pos_g[:, :], pos[:, :], (ROW * P).bit_length() - 1, ROW.bit_length() - 1,
                   lsr, ALU.logical_shift_left).then_inc(s_split, 1)
                ts(pos_s[:, :], pos[:, :], ROW - 1, None, ALU.bitwise_and).then_inc(s_split, 1)
                dve.wait_ge(s_split, n + 4)
                nc.vector.tensor_copy(part_f[:, r, :], pos_r[:, :]).then_inc(s_split, 1)
                tt(place_b[:, r, :], pos_g[:, :], pos_s[:, :], ALU.add).then_inc(s_split, 1)

            def addresses(t, r):
                ch = 2 * t + r
                dve.wait_ge(s_rowsread, ch + 1)
                tt(row_i[:, 0, :], row_f[:, :], rho[:, :], ALU.add).then_inc(s_rowi, 1)
                dve.wait_ge(s_rowi, 3 * ch + 1)
                ts(row_i[:, 1, :], row_i[:, 0, :], P - 1, None, ALU.bitwise_and).then_inc(s_rowi, 1)
                ts(row_i[:, 2, :], row_i[:, 0, :], 7, None, lsr).then_inc(s_rowi, 1)
                dve.wait_ge(s_rowi, 3 * ch + 3)
                need(dve, s_scat[r], 16 * CG * t)
                stt(addr[:, r, :], row_i[:, 1, :], float(ROOM), row_i[:, 2, :],
                    ALU.mult, ALU.add).then_inc(s_addr, 1)

            def chunk(t, r):
                ch, following, next_but_one = 2 * t + r, after(t, r, 1), after(t, r, 2)
                dve.wait_ge(s_split, 6 * ch + 6)
                for b in range(BATCHES):
                    k, q, col = b % BRING, BATCHES * ch + b, BATCH * b
                    dve.wait_ge(s_used, q + 1)
                    tt(is_place[:, k, :, :], under(place_b[:, r, col:col + BATCH], CG * ROW),
                       place_no[:, :, :], ALU.is_equal).then_inc(s_equal, 1)
                    tt(to_part[:, k, :, :], over(part_f[:, r, col:col + BATCH], P),
                       under(iota[:, :], BATCH), ALU.is_equal).then_inc(s_topart, 1)
                    if following and b % 2 == 1:
                        pick(*following, b // 2)
                    if following and b % 2 == 0 and b > 0:
                        total(*following, b // 2 - 1)
                    if next_but_one and b == HOT_AT:
                        hot_of(*next_but_one)
                    if b == ADDR_AT:
                        addresses(t, r)
                    if following and b == ROWI_AT:
                        row_numbers(*following)
                if following:
                    total(*following, SPC - 1)
                    split(*following)
            hot_of(0, 0)
            pick(0, 0, 0)
            for m in range(SPC):
                if m + 1 < SPC:
                    pick(0, 0, m + 1)
                total(0, 0, m)
            row_numbers(0, 0)
            split(0, 0)
            hot_of(0, 1)
            every_chunk(dve, chunk)

            dve.wait_ge(s_x, 32)
            link(nc.vector.reduce_sum(stat[:, 0, :], x_sb[:, :, :], AX_X))
            link(nc.vector.tensor_scalar(stat[:, 0, :], stat[:, 0, :], 1.0 / D, None, ALU.mult))
            nc.vector.tensor_tensor(h_sb[:, :, :], x_sb[:, :, :], over(stat[:, 0, :], D), ALU.subtract).then_inc(s_xc, 1)
            dve.wait_ge(s_sq, 1)
            link(nc.vector.reduce_sum(stat[:, 1, :], q_sb[:, :, :], AX_X))
            nc.vector.tensor_scalar(stat[:, 1, :], stat[:, 1, :], 1.0 / D, 1e-5, ALU.mult, ALU.add).then_inc(s_var, 1)
            dve.wait_ge(s_std, 1)
            link(nc.vector.reciprocal(stat[:, 3, :], stat[:, 2, :]))
            link(nc.vector.tensor_tensor(h_sb[:, :, :], h_sb[:, :, :], over(stat[:, 3, :], D), ALU.mult))
            nc.vector.tensor_scalar(h_sb[:, :, :], h_sb[:, :, :], 0.0, None, ALU.max).then_inc(s_h, 1)
            for b in range(NBLK):
                dve.wait_ge(s_qkv, b + 1)
                nc.vector.tensor_copy(q_sb[:, b, :], qkv_ps[b % QKV_TILES][:, 0:D]).then_inc(s_q, 1)

            dve.wait_ge(s_back, 16)
            link(nc.vector.tensor_scalar(loc_f[:, :].bitcast(i32), slots[:, :], PACK - 1, None, ALU.bitwise_and))
            link(nc.vector.tensor_scalar(loc_f[:, :], loc_f[:, :].bitcast(i32), -1.0, None, ALU.add))
            link(nc.vector.tensor_scalar(slots[:, :], slots[:, :], PACK.bit_length() - 1, None,
                                         ALU.logical_shift_right))
            dve.wait_ge(s_q, NBLK)


def walk(eng, step, ring, first=-2, drain=4, peel=1):
    whole = (GROUPS - ring) // ring
    for i in range(first, peel * ring):
        step(i, i % ring, i // ring)
    with eng.Fori(peel, whole) as t:
        for u in range(ring):
            step(ring * t + u, u, t)
    for i in range(ring * whole, GROUPS + drain):
        step(i, i % ring, i // ring)


def inside(g):
    return not isinstance(g, int) or 0 <= g < GROUPS


def block_of(eng, blkid, g):
    return eng.value_load(blkid[0:1, ds(g, 1)], min_val=0, max_val=LASTB)


def gather_groups(pool, ring, table, G, idx, s_idx, s_read, s_gat, s_go):
    def step(i, u, t):
        if not inside(i):
            return
        pool.wait_ge(s_idx, i + 1)
        need(pool, s_read, i - ring + 1)
        pool.sem_inc(s_go, 1)
        for j in range(GT):
            pool.indirect_dma_start(out=G[:, u, j, :], out_offset=None, in_=table,
                                    in_offset=bass.IndirectOffsetOnAxis(ap=idx[:, u, j:j + 1], axis=0)
                                    ).then_inc(s_gat[u], 16)
    walk(pool, step, ring, first=0, drain=0)


def layer0_edges(nc, mem, dram):
    with ExitStack() as ctx:
        def sb(name, shape, dt=f32):
            return ctx.enter_context(nc.sbuf_tensor(name, shape, dt))

        def sem(name):
            return ctx.enter_context(nc.semaphore(name))

        iota, ident, q_sb = mem["iota"], mem["ident"], mem["q"]
        slots, loc_f, blkid, acc = mem["slots"], mem["loc"], mem["blkid"], mem["acc"]
        acc = acc[:, 0:NBLK * AW0]
        PS = mem["psum"]
        G = sb("kv_rows", [P, RING0, GT, 2 * D])
        idx = sb("idx_ring", [P, RING0, GT], i32)
        hot = sb("hot0", [P, RING0, GE])
        hotT = sb("hotT0", [P, 2, GE])
        prod = sb("prod0", [P, GE])
        att = sb("att0", [P, 2, GT * HEADS])
        clip = sb("clip0", [P, 2, GT * HEADS])
        vx = sb("vx0", [P, 2, GT, AW0])
        T_ps = [PS[:, 512 * k:512 * k + GE] for k in (0, 1)]
        Q_ps = [PS[:, 512 * k:512 * k + GE] for k in (2, 3)]
        S_ps = [PS[:, 512 * k:512 * k + AW0] for k in (4, 5)]

        s_zero = sem("s_zero0")
        s_idx = sem("s_idx0")
        s_gat = [sem(f"s_gat0_{k}") for k in range(RING0)]
        s_go = sem("s_go0")
        s_hot = sem("s_hot0")
        s_T = sem("s_T0")
        s_hotT = sem("s_hotT0")
        s_q = sem("s_q0")
        s_prod = sem("s_prod0")
        s_red = sem("s_red0")
        s_clip = sem("s_clip0")
        s_ex = sem("s_ex0")
        s_vx = sem("s_vx0")
        s_sum = sem("s_sum0")
        s_acc = sem("s_acc0")
        block = ctx.enter_context(nc.Block())

        @block.gpsimd
        def _(pool):
            gather_groups(pool, RING0, dram["kv"], G, idx, s_idx, s_vx, s_gat, s_go)

        @block.scalar
        def _(act):
            def indices(g, u):
                if inside(g):
                    nc.scalar.copy(idx[:, u, :], slots[:, ds(GT * g, GT)]).then_inc(s_idx, 1)

            for g in range(RING0):
                indices(g, g)

            def step(i, u, t):
                if inside(i + 2):
                    act.wait_ge(s_T, i + 3)
                    need(act, s_q, i + 1)
                    nc.scalar.activation(hotT[:, u % 2, :], T_ps[u % 2], ACT.Copy).then_inc(s_hotT, 1)
                if inside(i):
                    act.wait_ge(s_clip, i + 1)
                    need(act, s_sum, i - 1)
                    nc.scalar.activation(vx[:, u % 2, :, D:AW0],
                                         clip[:, u % 2, :].rearrange("p (j h) -> p j h", h=HEADS),
                                         ACT.Exp).then_inc(s_ex, 1)
                    indices(i + RING0, u)
            walk(act, step, RING0, drain=0)

        @block.tensor
        def _(pe):
            def step(i, u, t):
                if inside(i + 1):
                    blk = block_of(pe, blkid, i + 1)
                    pe.wait_ge(s_hotT, i + 2)
                    need(pe, s_prod, i)
                    for j in range(GT):
                        last = nc.tensor.matmul(Q_ps[(u + 1) % 2][:, j * P:(j + 1) * P],
                                                hotT[:, (u + 1) % 2, j * P:(j + 1) * P],
                                                q_sb[:, ds(blk, 1), :].rearrange("p o f -> p (o f)"),
                                                start=True, stop=True)
                    last.then_inc(s_q, 1)
                if inside(i + 2):
                    pe.wait_ge(s_hot, i + 3)
                    need(pe, s_hotT, i + 1)
                    for j in range(GT):
                        last = nc.tensor.transpose(T_ps[u % 2][:, j * P:(j + 1) * P],
                                                   hot[:, (u + 2) % RING0, j * P:(j + 1) * P], ident[:, :])
                    last.then_inc(s_T, 1)
                if inside(i - 1):
                    pe.wait_ge(s_vx, i)
                    need(pe, s_acc, i - 2)
                    for j in range(GT):
                        last = nc.tensor.matmul(S_ps[(u + 1) % 2], hot[:, (u - 1) % RING0, j * P:(j + 1) * P],
                                                vx[:, (u + 1) % 2, j, :], start=(j == 0), stop=(j == GT - 1))
                    last.then_inc(s_sum, 1)
            walk(pe, step, RING0, drain=1)

        @block.vector
        def _(dve):
            nc.vector.memset(acc[:, :], 0.0).then_inc(s_zero, 1)
            dve.wait_ge(s_zero, 1)

            def step(i, u, t):
                if inside(i + 2):
                    need(dve, s_sum, i + 3 - RING0)
                    nc.vector.tensor_tensor(hot[:, (u + 2) % RING0, :].rearrange("p (j n) -> p j n", n=P),
                                            over(loc_f[:, ds(GT * (i + 2), GT)], P), under(iota[:, :], GT),
                                            ALU.is_equal).then_inc(s_hot, 1)
                if inside(i):
                    dve.wait_ge(s_gat[u], 16 * GT * (t + 1))
                    dve.wait_ge(s_q, i + 1)
                    need(dve, s_red, i)
                    nc.vector.tensor_tensor(prod[:, :].rearrange("p (j f) -> p j f", f=D),
                                            Q_ps[u % 2].rearrange("p (j f) -> p j f", f=D),
                                            G[:, u, :, 0:D], ALU.mult).then_inc(s_prod, 1)
                if inside(i - 2):
                    blk = block_of(dve, blkid, i - 2)
                    dve.wait_ge(s_sum, i - 1)
                    need(dve, s_acc, i - 2)
                    rows = acc[:, ds(blk * AW0, AW0)]
                    nc.vector.tensor_tensor(rows, rows, S_ps[u % 2], ALU.add).then_inc(s_acc, 1)
                if inside(i):
                    dve.wait_ge(s_prod, i + 1)
                    nc.vector.reduce_sum(att[:, u % 2, :],
                                         prod[:, :].rearrange("p (a d) -> p a d", d=HD), AX_X).then_inc(s_red, 1)
                if inside(i - 1):
                    dve.wait_ge(s_ex, i)
                    need(dve, s_sum, i - 2)
                    v = vx[:, (u + 1) % 2, :, :]
                    nc.vector.tensor_tensor(v[:, :, 0:D].rearrange("p j (h d) -> p j h d", d=HD),
                                            G[:, (u - 1) % RING0, :, D:2 * D].rearrange("p j (h d) -> p j h d", d=HD),
                                            v[:, :, D:AW0].unsqueeze(3).broadcast_to((P, GT, HEADS, HD)),
                                            ALU.mult).then_inc(s_vx, 1)
                if inside(i):
                    dve.wait_ge(s_red, i + 1)
                    need(dve, s_ex, i - 1)
                    nc.vector.tensor_scalar(clip[:, u % 2, :], att[:, u % 2, :], -10.0, 10.0,
                                            ALU.max, ALU.min).then_inc(s_clip, 1)
            walk(dve, step, RING0, drain=2)


def between_layers(nc, mem, dram):
    with ExitStack() as ctx:
        def sb(name, shape, dt=f32):
            return ctx.enter_context(nc.sbuf_tensor(name, shape, dt))

        def sem(name):
            return ctx.enter_context(nc.semaphore(name))

        x_sb, q_sb, gb, cb = mem["x"], mem["q"], mem["gb"], mem["cb"]
        h_sb = mem["h"][:, 0:NBLK * D].rearrange("p (t f) -> p t f", f=D)
        acc = mem["acc"][:, 0:NBLK * AW0].rearrange("p (t f) -> p t f", f=AW0)
        table = mem["acc"][:, 0:NBLK * TW].rearrange("p (t f) -> p t f", f=TW)
        sums = mem["h"][:, :].rearrange("p (t f) -> p t f", f=AW1)
        rden = sb("rden", [P, NBLK, HEADS])
        mean = sb("mean", [P, NBLK])
        var = sb("var", [P, NBLK])
        std = sb("std", [P, NBLK])
        rstd = sb("rstd", [P, NBLK])

        s_v = sem("s_v1")
        s_centred = sem("s_centred")
        s_sq = sem("s_sq1")
        s_var = sem("s_var1")
        s_std = sem("s_std1")
        s_tab = sem("s_tab")
        s_h1 = sem("s_h1")
        block = ctx.enter_context(nc.Block())

        @block.sync
        def _(sp):
            sp.wait_ge(s_tab, 1)
            sp.dma_start(dram["h1"].rearrange("(t p) f -> p t f", p=P), table[:, :, :]).then_inc(s_h1, 16)
            sp.wait_ge(s_h1, 16)

        @block.scalar
        def _(act):
            for n, (centred, square) in enumerate(((q_sb, h_sb), (h_sb, q_sb), (table[:, :, 0:D], q_sb))):
                act.wait_ge(s_centred, n + 1)
                nc.scalar.activation(square[:, :, :], centred[:, :, :], ACT.Square).then_inc(s_sq, 1)
                act.wait_ge(s_var, n + 1)
                nc.scalar.activation(std[:, :], var[:, :], ACT.Sqrt).then_inc(s_std, 1)

        @block.vector
        def _(dve):
            link = Chain(dve, s_v)
            tt, ts = nc.vector.tensor_tensor, nc.vector.tensor_scalar

            def normalise(src, centred, squares, n, eps):
                link(nc.vector.reduce_sum(mean[:, :], src, AX_X))
                link(ts(mean[:, :], mean[:, :], 1.0 / D, None, ALU.mult))
                tt(centred[:, :, :], src, over(mean[:, :], D), ALU.subtract).then_inc(s_centred, 1)
                dve.wait_ge(s_sq, n)
                link(nc.vector.reduce_sum(var[:, :], squares[:, :, :], AX_X))
                ts(var[:, :], var[:, :], 1.0 / D, eps, ALU.mult, ALU.add).then_inc(s_var, 1)
                dve.wait_ge(s_std, n)
                link(nc.vector.reciprocal(rstd[:, :], std[:, :]))

            link(ts(rden[:, :, :], acc[:, :, D:AW0], 1e-8, None, ALU.add))
            link(nc.vector.reciprocal(rden[:, :, :], rden[:, :, :]))
            heads = "p t (h d) -> p t h d"
            link(tt(q_sb[:, :, :].rearrange(heads, d=HD), acc[:, :, 0:D].rearrange(heads, d=HD),
                    rden[:, :, :].unsqueeze(3).broadcast_to((P, NBLK, HEADS, HD)), ALU.mult))
            link(tt(q_sb[:, :, :], q_sb[:, :, :], h_sb[:, :, :], ALU.add))
            normalise(q_sb[:, :, :], q_sb, h_sb, 1, 1e-6)
            link(tt(q_sb[:, :, :], q_sb[:, :, :], over(rstd[:, :], D), ALU.mult))
            link(tt(q_sb[:, :, :], q_sb[:, :, :], under(gb[:, 0, :], NBLK), ALU.mult))
            link(tt(q_sb[:, :, :], q_sb[:, :, :], under(gb[:, 1, :], NBLK), ALU.add))
            link(tt(x_sb[:, :, :], x_sb[:, :, :], q_sb[:, :, :], ALU.add))
            normalise(x_sb[:, :, :], h_sb, q_sb, 2, 1e-5)
            link(tt(h_sb[:, :, :], h_sb[:, :, :], over(rstd[:, :], D), ALU.mult))
            nc.vector.memset(table[:, :, D:D + 1], 1.0)
            ts(table[:, :, 0:D], h_sb[:, :, :], 0.0, None, ALU.max).then_inc(s_centred, 1)
            dve.wait_ge(s_sq, 3)
            nc.vector.reduce_sum(var[:, :], q_sb[:, :, :], AX_X).then_inc(s_var, 1)
            dve.wait_ge(s_std, 3)
            link(ts(std[:, :], std[:, :], 1e-30, None, ALU.max))
            link(nc.vector.reciprocal(rstd[:, :], std[:, :]))
            nc.vector.tensor_copy(table[:, :, D + 1:TW], rstd[:, :].unsqueeze(2)).then_inc(s_tab, 1)
            link(ts(mean[:, :], rstd[:, :], cb[:, 0:1], None, ALU.mult))
            link(tt(q_sb[:, :, :], table[:, :, 0:D], over(mean[:, :], D), ALU.mult))
            link(ts(cb[:, 1:2], cb[:, 0:1], -1.0, None, ALU.mult))
            link(tt(cb[:, 2:3], cb[:, 0:1], cb[:, 1:2], ALU.max))
            link(ts(cb[:, 1:2], cb[:, 2:3], 1.01, 1e-3, ALU.mult, ALU.add))
            link(nc.vector.tensor_copy(sums[:, :, :], table[:, :, 0:AW1]))
            link(tt(var[:, :], var[:, :], rstd[:, :], ALU.mult))
            link(tt(var[:, :], var[:, :], mean[:, :], ALU.mult))
            link(ts(mem["top"][:, :], var[:, :], cb[:, 1:2], None, ALU.add))


def layer1_edges(nc, mem, dram):
    with ExitStack() as ctx:
        def sb(name, shape, dt=f32):
            return ctx.enter_context(nc.sbuf_tensor(name, shape, dt))

        def sem(name):
            return ctx.enter_context(nc.semaphore(name))

        iota, ident, q_sb = mem["iota"], mem["ident"], mem["q"]
        slots, loc_f, blkid, cb = mem["slots"], mem["loc"], mem["blkid"], mem["cb"]
        acc = mem["h"]
        PS = mem["psum"]
        G = sb("h_rows", [P, RING1, GT, TW])
        idx = sb("idx_ring1", [P, RING1, GT], i32)
        loc_b = sb("loc_b", [P, NT], bf16)
        iota_j = sb("iota_j", [P, P, GT], bf16)
        hot = sb("hot1", [P, RING1, P, GT], bf16)
        ident_b = sb("ident_b", [P, P], bf16)
        hotT = sb("hotT1", [P, RING1, GE])
        prod = sb("prod1", [P, GE])
        cosb = sb("cosb", [P, 2, GT])
        logit = sb("logit", [P, RING1, GT])
        hotl = sb("hotl", [P, 2, GE])
        hotw = sb("hotw", [P, 2, GE])
        gmax = sb("gmax", [P, 1])
        top = mem["top"]
        newtop = sb("newtop", [P, RING1])
        fall = sb("fall", [P, 2])
        corr = sb("corr", [P, RING1])
        below = sb("below", [P, 2, GT])
        wgt = sb("wgt", [P, 2, GT])
        T_ps = [PS[:, 512 * k:512 * k + GE // 2].bitcast(bf16) for k in (0, 1)]
        Q_ps = [PS[:, 512 * k:512 * k + GE] for k in (2, 3)]
        S_ps = [PS[:, 512 * k:512 * k + AW1] for k in (4, 5)]
        L_ps = PS[:, 512 * 6:512 * 6 + GE]
        E_ps = PS[:, 512 * 7:512 * 7 + GT]

        s_idx = sem("s_idx1")
        s_gat = [sem(f"s_gat1_{k}") for k in range(RING1)]
        s_go = sem("s_go1")
        s_identb = sem("s_identb")
        s_locb = sem("s_locb")
        s_hot = sem("s_hot1")
        s_T = sem("s_T1")
        s_hotT = sem("s_hotT1")
        s_q = sem("s_q1")
        s_prod = sem("s_prod1")
        s_logit = sem("s_logit")
        s_hotl = sem("s_hotl")
        s_L = sem("s_L")
        s_gmax = sem("s_gmax")
        s_newtop = sem("s_newtop")
        s_fall = sem("s_fall")
        s_top = sem("s_top")
        s_corr = sem("s_corr")
        s_E = sem("s_E")
        s_below = sem("s_below")
        s_wgt = sem("s_wgt")
        s_hotw = sem("s_hotw")
        s_sum = sem("s_sum1")
        s_acc = sem("s_acc1")
        block = ctx.enter_context(nc.Block())

        @block.gpsimd
        def _(pool):
            gather_groups(pool, RING1, dram["h1"], G, idx, s_idx, s_sum, s_gat, s_go)

        @block.scalar
        def _(act):
            def indices(g, u):
                if inside(g):
                    nc.scalar.copy(idx[:, u, :], slots[:, ds(GT * g, GT)]).then_inc(s_idx, 1)

            for g in range(RING1):
                indices(g, g)

            def scaled(out, u, scale):
                for j in range(GT):
                    last = nc.scalar.activation(out[:, j * P:(j + 1) * P], hot[:, u, :, j],
                                                ACT.Copy, scale=scale[:, j:j + 1])
                return last

            def step(i, u, t):
                if inside(i - 1):
                    act.wait_ge(s_logit, i)
                    need(act, s_L, i - 2)
                    scaled(hotl[:, (u + 1) % 2, :], (u - 1) % RING1, logit[:, (u - 1) % RING1, :]).then_inc(s_hotl, 1)
                if inside(i + 2):
                    act.wait_ge(s_T, i + 3)
                    need(act, s_E, i + 3 - RING1)
                    nc.scalar.activation(hotT[:, (u + 2) % RING1, :], T_ps[u % 2], ACT.Copy).then_inc(s_hotT, 1)
                if inside(i - 2):
                    act.wait_ge(s_fall, i - 1)
                    need(act, s_acc, i - 1 - RING1)
                    w = (u - 2) % RING1
                    nc.scalar.activation(corr[:, w:w + 1], fall[:, u % 2:u % 2 + 1], ACT.Exp).then_inc(s_corr, 1)
                if inside(i - 3):
                    p = (u + 1) % 2
                    act.wait_ge(s_below, i - 2)
                    nc.scalar.activation(wgt[:, p, :], below[:, p, :], ACT.Exp).then_inc(s_wgt, 1)
                if inside(i):
                    act.wait_ge(s_prod, i + 1)
                    need(act, s_below, i + 1 - RING1)
                    need(act, s_hotl, i + 1 - RING1)
                    nc.scalar.activation(logit[:, u, :], cosb[:, u % 2, :], ACT.Identity,
                                         bias=cb[:, 1:2]).then_inc(s_logit, 1)
                    indices(i + RING1, u)
                if inside(i - 3):
                    act.wait_ge(s_wgt, i - 2)
                    need(act, s_sum, i - 4)
                    scaled(hotw[:, p, :], (u - 3) % RING1, wgt[:, p, :]).then_inc(s_hotw, 1)
            walk(act, step, RING1, drain=3, peel=2)

        @block.tensor
        def _(pe):
            pe.wait_ge(s_identb, 1)

            def step(i, u, t):
                if inside(i + 1):
                    blk = block_of(pe, blkid, i + 1)
                    pe.wait_ge(s_hotT, i + 2)
                    need(pe, s_prod, i)
                    for j in range(GT):
                        last = nc.tensor.matmul(Q_ps[(u + 1) % 2][:, j * P:(j + 1) * P],
                                                hotT[:, (u + 1) % RING1, j * P:(j + 1) * P],
                                                q_sb[:, ds(blk, 1), :].rearrange("p o f -> p (o f)"),
                                                start=True, stop=True)
                    last.then_inc(s_q, 1)
                if inside(i - 1):
                    pe.wait_ge(s_hotl, i)
                    need(pe, s_gmax, i - 1)
                    for j in range(GT):
                        last = nc.tensor.transpose(L_ps[:, j * P:(j + 1) * P],
                                                   hotl[:, (u + 1) % 2, j * P:(j + 1) * P], ident[:, :])
                    last.then_inc(s_L, 1)
                if inside(i + 2):
                    pe.wait_ge(s_hot, i + 3)
                    need(pe, s_hotT, i + 1)
                    for j in range(GT):
                        last = nc.tensor.transpose(T_ps[u % 2][:, j * P:(j + 1) * P],
                                                   hot[:, (u + 2) % RING1, :, j], ident_b[:, :])
                    last.then_inc(s_T, 1)
                if inside(i - 2):
                    pe.wait_ge(s_newtop, i - 1)
                    need(pe, s_below, i - 2)
                    for j in range(GT):
                        last = nc.tensor.matmul(E_ps[:, j:j + 1], hotT[:, (u - 2) % RING1, j * P:(j + 1) * P],
                                                newtop[:, (u - 2) % RING1:(u - 2) % RING1 + 1],
                                                start=True, stop=True)
                    last.then_inc(s_E, 1)
                if inside(i - 4):
                    pe.wait_ge(s_hotw, i - 3)
                    need(pe, s_acc, i - 5)
                    for j in range(GT):
                        last = nc.tensor.matmul(S_ps[u % 2], hotw[:, u % 2, j * P:(j + 1) * P],
                                                G[:, (u - 4) % RING1, j, 0:AW1],
                                                start=(j == 0), stop=(j == GT - 1))
                    last.then_inc(s_sum, 1)
            walk(pe, step, RING1, drain=4)

        @block.vector
        def _(dve):
            nc.vector.tensor_copy(ident_b[:, :], ident[:, :]).then_inc(s_identb, 1)
            nc.vector.tensor_copy(loc_b[:, :], loc_f[:, :]).then_inc(s_locb, 1)
            nc.vector.tensor_copy(iota_j[:, :, :], over(iota[:, :], GT)).then_inc(s_locb, 1)
            dve.wait_ge(s_locb, 2)

            def step(i, u, t):
                if inside(i - 2):
                    blk = block_of(dve, blkid, i - 2)
                    w = (u - 2) % RING1
                    v = u % 2
                    old, new = top[:, ds(blk, 1)], newtop[:, w:w + 1]
                if inside(i + 2):
                    need(dve, s_hotw, i + 3 - RING1)
                    need(dve, s_T, i + 3 - RING1)
                    nc.vector.tensor_tensor(hot[:, (u + 2) % RING1, :, :], under(loc_b[:, ds(GT * (i + 2), GT)], P),
                                            iota_j[:, :, :], ALU.is_equal).then_inc(s_hot, 1)
                if inside(i - 2):
                    dve.wait_ge(s_L, i - 1)
                    nc.vector.reduce_max(gmax[:, :], L_ps, AX_X).then_inc(s_gmax, 1)
                if inside(i):
                    dve.wait_ge(s_gat[u], 16 * GT * (t + 1))
                    dve.wait_ge(s_q, i + 1)
                    need(dve, s_logit, i - 1)
                    need(dve, s_prod, i)
                    for j in range(GT):
                        last = nc.vector.scalar_tensor_tensor(prod[:, j * P:(j + 1) * P], Q_ps[u % 2][:, j * P:(j + 1) * P],
                                                              G[:, u, j, D + 1:TW], G[:, u, j, 0:D], ALU.mult,
                                                              ALU.mult, accum_out=cosb[:, u % 2, j:j + 1])
                    last.then_inc(s_prod, 1)
                if inside(i - 2):
                    dve.wait_ge(s_gmax, i - 1)
                    need(dve, s_top, i - 2)
                    need(dve, s_E, i - 1 - RING1)
                    nc.vector.tensor_tensor(new, old, gmax[:, :], ALU.max).then_inc(s_newtop, 1)
                if inside(i - 2):
                    dve.wait_ge(s_newtop, i - 1)
                    need(dve, s_corr, i - 3)
                    nc.vector.tensor_tensor(fall[:, v:v + 1], old, new, ALU.subtract).then_inc(s_fall, 1)
                if inside(i - 3):
                    dve.wait_ge(s_E, i - 2)
                    need(dve, s_wgt, i - 4)
                    nc.vector.tensor_tensor(below[:, (u + 1) % 2, :], logit[:, (u - 3) % RING1, :], E_ps,
                                            ALU.subtract).then_inc(s_below, 1)
                if inside(i - 2):
                    dve.wait_ge(s_fall, i - 1)
                    nc.vector.tensor_tensor(old, old, new, ALU.max).then_inc(s_top, 1)
                if inside(i - 5):
                    blk5 = block_of(dve, blkid, i - 5)
                    dve.wait_ge(s_sum, i - 4)
                    dve.wait_ge(s_corr, i - 4)
                    need(dve, s_acc, i - 5)
                    rows = acc[:, ds(blk5 * AW1, AW1)]
                    w5 = (u - 5) % RING1
                    nc.vector.scalar_tensor_tensor(rows, rows, corr[:, w5:w5 + 1], S_ps[(u + 1) % 2],
                                                   ALU.mult, ALU.add).then_inc(s_acc, 1)
            walk(dve, step, RING1, drain=5, peel=2)


def finish(nc, mem, out):
    with ExitStack() as ctx:
        den = ctx.enter_context(nc.sbuf_tensor("den", [P, NBLK], f32))
        s_v = ctx.enter_context(nc.semaphore("s_v2"))
        s_res = ctx.enter_context(nc.semaphore("s_res"))
        s_out = ctx.enter_context(nc.semaphore("s_out"))
        x_sb, q_sb = mem["x"], mem["q"]
        acc = mem["h"][:, :].rearrange("p (t f) -> p t f", f=AW1)
        half = LASTB // 2
        block = ctx.enter_context(nc.Block())

        @block.vector
        def _(dve):
            link = Chain(dve, s_v)
            sums = acc[:, :, D:AW1].rearrange("p t o -> p (t o)")
            link(nc.vector.reciprocal(den[:, :], sums))
            for a, b in ((0, half), (half, NBLK)):
                link(nc.vector.tensor_tensor(q_sb[:, a:b, :], acc[:, a:b, 0:D], over(den[:, a:b], D), ALU.mult))
                nc.vector.tensor_tensor(q_sb[:, a:b, :], q_sb[:, a:b, :], x_sb[:, a:b, :], ALU.add).then_inc(s_res, 1)

        @block.sync
        def _(sp):
            sp.wait_ge(s_res, 1)
            sp.dma_start(out[0:half * P, :].rearrange("(t p) f -> p t f", p=P), q_sb[:, 0:half, :]).then_inc(s_out, 16)
            sp.wait_ge(s_res, 2)
            sp.dma_start(out[half * P:LASTB * P, :].rearrange("(t p) f -> p t f", p=P),
                         q_sb[:, half:LASTB, :]).then_inc(s_out, 16)
            sp.dma_start(out[LASTB * P:N, :], q_sb[0:TAIL, LASTB, :]).then_inc(s_out, 16)
            sp.wait_ge(s_out, 48)


_INS = ["x", "src", "dst", "L0_gnn_Wq", "L0_gnn_Wk", "L0_gnn_Wv", "L0_gnn_gamma", "L0_gnn_beta", "L1_gnn_beta"]


def program(nc, x, src, dst, wq, wk, wv, gamma, beta, cos_beta, out):
    dram = {
        "sorted": nc.dram_tensor("sorted_edges", (P * ROOM, ROW), i32).ap(),
        "counts": nc.dram_tensor("column_counts", (NCHUNK, NBUK * CHUNK), f32).ap(),
        "offs": nc.dram_tensor("column_offsets", (2, COLS, NBUK), bf16).ap(),
        "kv": nc.dram_tensor("kv_table", (NPAD, 2 * D), f32).ap(),
        "h1": nc.dram_tensor("h1_table", (NPAD, TW), f32).ap(),
    }
    with ExitStack() as ctx:
        def sb(name, shape, dt=f32):
            return ctx.enter_context(nc.sbuf_tensor(name, shape, dt))
        mem = {
            "iota": sb("iota", [P, P]),
            "ident": sb("ident", [P, P]),
            "x": sb("x_sb", [P, NBLK, D]),
            "h": sb("h_sb", [P, NBLK * AW1]),
            "q": sb("q_sb", [P, NBLK, D]),
            "slots": sb("slots", [P, NT], i32),
            "loc": sb("loc_f", [P, NT]),
            "blkid": sb("blkid", [1, GROUPS], i32),
            "acc": sb("acc", [P, max(NBLK * AW0, 2 * CHUNK * NBUK)]),
            "gb": sb("gb_sb", [P, 2, D]),
            "cb": sb("cb_sb", [P, 3]),
            "top": sb("top", [P, NBLK]),
            "psum": ctx.enter_context(nc.psum_tensor("psum", [P, 4096], f32)),
        }
        sort_and_project(nc, mem, dram, (src, dst, x, wq, wk, wv, gamma, beta, cos_beta))
        layer0_edges(nc, mem, dram)
        between_layers(nc, mem, dram)
        layer1_edges(nc, mem, dram)
        finish(nc, mem, out)


def kernel(**inputs):
    import numpy as np
    import concourse.bacc as bacc
    from concourse.bass_utils import run_bass_kernel_spmd

    nc = bacc.Bacc("TRN2", target_bir_lowering=False, num_devices=1)
    arrays, args = {}, []
    for name in _INS:
        a = np.ascontiguousarray(inputs[name])
        arrays[f"in_{name}"] = a
        args.append(nc.dram_tensor(f"in_{name}", a.shape, mybir.dt.from_np(a.dtype), kind="ExternalInput").ap())
    args.append(nc.dram_tensor("out_0", (N, D), f32, kind="ExternalOutput").ap())
    program(nc, *args)
    return run_bass_kernel_spmd(nc, [arrays], core_ids=[0]).results[0]["out_0"]
```
